# Optimizing a Trainium2 kernel written in Bass

```python
import numpy as np
import jax
import jax.numpy as jnp

def _softmax(x, axis=-1):
    return jax.nn.softmax(x, axis=axis)

def _gelu(x):
    return jax.nn.gelu(x, approximate=True)

def _silu(x):
    return jax.nn.silu(x)

def _sigmoid(x):
    return jax.nn.sigmoid(x)

def _layernorm(x, axis=-1, eps=1e-05):
    m = jnp.mean(x, axis=axis, keepdims=True)
    v = jnp.var(x, axis=axis, keepdims=True)
    return (x - m) / jnp.sqrt(v + eps)

def _scatter_add(tgt, idx, src, axis=0):
    return tgt.at[idx].add(src)

def _segment_sum(src, seg, n):
    return jax.ops.segment_sum(src, seg, n)
kernel_name = 'mk_adaln_d1_jaxref_r8_2aa181'

def setup_inputs(seed: int=0):
    np.random.seed(seed)
    _w = jnp.asarray

    def _L0_attn_setup():
        import jax, jax.numpy as jnp
        import numpy as np
        NF4 = jnp.array([-1.0, -0.6961928009986877, -0.5250730514526367, -0.39491748809814453, -0.28444138169288635, -0.18477343022823334, -0.09105003625154495, 0.0, 0.07958029955625534, 0.16093020141124725, 0.24611230194568634, 0.33791524171829224, 0.44070982933044434, 0.5626170039176941, 0.7229568362236023, 1.0], dtype=jnp.float32)
        BLOCK = 64

        def _dequant(codes, scales):
            w = NF4[codes]
            O, I = w.shape
            w = w.reshape(O, I // BLOCK, BLOCK) * scales[:, :, None]
            return w.reshape(O, I)

        def _lin_lora(x, W, A, B):
            base = jnp.einsum('bsh,oh->bso', x, W)
            lora = jnp.einsum('bsr,or->bso', jnp.einsum('bsh,rh->bsr', x, A), B)
            return base + lora
        H, I, R, BT, S = (512, 1792, 16, 2, 256)
        key = jax.random.key(seed)
        ks = jax.random.split(key, 12)
        x = jax.random.normal(ks[0], (BT, S, H), jnp.float32)
        codes_attn = jax.random.randint(ks[1], (4, H, H), 0, 16, jnp.int32)
        scales_attn = jax.random.uniform(ks[2], (4, H, H // BLOCK), jnp.float32) * 0.02
        codes_gu = jax.random.randint(ks[3], (2, I, H), 0, 16, jnp.int32)
        scales_gu = jax.random.uniform(ks[4], (2, I, H // BLOCK), jnp.float32) * 0.02
        codes_down = jax.random.randint(ks[5], (H, I), 0, 16, jnp.int32)
        scales_down = jax.random.uniform(ks[6], (H, I // BLOCK), jnp.float32) * 0.02
        lora_A_h = jax.random.normal(ks[7], (6, R, H), jnp.float32) * 0.02
        lora_A_down = jax.random.normal(ks[8], (R, I), jnp.float32) * 0.02
        lora_B_attn = jax.random.normal(ks[9], (4, H, R), jnp.float32) * 0.02
        lora_B_gu = jax.random.normal(ks[10], (2, I, R), jnp.float32) * 0.02
        lora_B_down = jax.random.normal(ks[11], (H, R), jnp.float32) * 0.02
        return dict(x=x, codes_attn=codes_attn, scales_attn=scales_attn, codes_gu=codes_gu, scales_gu=scales_gu, codes_down=codes_down, scales_down=scales_down, lora_A_h=lora_A_h, lora_A_down=lora_A_down, lora_B_attn=lora_B_attn, lora_B_gu=lora_B_gu, lora_B_down=lora_B_down)
    _L0_attn_in = _L0_attn_setup()

    def _L0_ffn_setup():
        import jax, jax.numpy as jnp
        import numpy as np
        HD, M = (512, 1792)
        key = jax.random.key(seed)
        k_x, k_g, k_u, k_d = jax.random.split(key, 4)
        scale = 1.0 / np.sqrt(HD)
        x = jax.random.normal(k_x, (4, 256, HD), dtype=jnp.float16)
        W_gate = jax.random.normal(k_g, (M, HD), dtype=jnp.float16) * jnp.float16(scale)
        W_up = jax.random.normal(k_u, (M, HD), dtype=jnp.float16) * jnp.float16(scale)
        W_down = jax.random.normal(k_d, (HD, M), dtype=jnp.float16) * jnp.float16(1.0 / np.sqrt(M))
        return {'x': x, 'W_gate': W_gate, 'W_up': W_up, 'W_down': W_down}
    _L0_ffn_in = _L0_ffn_setup()
    _L0_c = _w((lambda *s: np.random.randn(*s).astype(np.float32) * 0.05)(8, 512))
    _L0_wmod = _w((lambda *s: np.random.randn(*s).astype(np.float32) * 0.05)(512, 6 * 512) * 512 ** (-0.5))
    _d = {'L0_attn_x': _L0_attn_in['x'], 'L0_attn_codes_attn': _L0_attn_in['codes_attn'], 'L0_attn_scales_attn': _L0_attn_in['scales_attn'], 'L0_attn_codes_gu': _L0_attn_in['codes_gu'], 'L0_attn_scales_gu': _L0_attn_in['scales_gu'], 'L0_attn_codes_down': _L0_attn_in['codes_down'], 'L0_attn_scales_down': _L0_attn_in['scales_down'], 'L0_attn_lora_A_h': _L0_attn_in['lora_A_h'], 'L0_attn_lora_A_down': _L0_attn_in['lora_A_down'], 'L0_attn_lora_B_attn': _L0_attn_in['lora_B_attn'], 'L0_attn_lora_B_gu': _L0_attn_in['lora_B_gu'], 'L0_attn_lora_B_down': _L0_attn_in['lora_B_down'], 'L0_ffn_W_gate': _L0_ffn_in['W_gate'], 'L0_ffn_W_up': _L0_ffn_in['W_up'], 'L0_ffn_W_down': _L0_ffn_in['W_down'], 'L0_c': _L0_c, 'L0_wmod': _L0_wmod}
    _x0 = _d['L0_attn_x']
    _d['L0_attn_x'] = jax.random.normal(jax.random.fold_in(jax.random.key(seed), 1), (8, 256, 512), dtype=_x0.dtype)
    del _x0
    return _d

def reference(L0_attn_x, L0_attn_codes_attn, L0_attn_scales_attn, L0_attn_codes_gu, L0_attn_scales_gu, L0_attn_codes_down, L0_attn_scales_down, L0_attn_lora_A_h, L0_attn_lora_A_down, L0_attn_lora_B_attn, L0_attn_lora_B_gu, L0_attn_lora_B_down, L0_ffn_W_gate, L0_ffn_W_up, L0_ffn_W_down, L0_c, L0_wmod):

    def _L0_attn_ref(x, codes_attn, scales_attn, codes_gu, scales_gu, codes_down, scales_down, lora_A_h, lora_A_down, lora_B_attn, lora_B_gu, lora_B_down):
        import jax, jax.numpy as jnp
        import numpy as np
        NF4 = jnp.array([-1.0, -0.6961928009986877, -0.5250730514526367, -0.39491748809814453, -0.28444138169288635, -0.18477343022823334, -0.09105003625154495, 0.0, 0.07958029955625534, 0.16093020141124725, 0.24611230194568634, 0.33791524171829224, 0.44070982933044434, 0.5626170039176941, 0.7229568362236023, 1.0], dtype=jnp.float32)
        BLOCK = 64

        def _dequant(codes, scales):
            w = NF4[codes]
            O, I = w.shape
            w = w.reshape(O, I // BLOCK, BLOCK) * scales[:, :, None]
            return w.reshape(O, I)

        def _lin_lora(x, W, A, B):
            base = jnp.einsum('bsh,oh->bso', x, W)
            lora = jnp.einsum('bsr,or->bso', jnp.einsum('bsh,rh->bsr', x, A), B)
            return base + lora
        q = _lin_lora(x, _dequant(codes_attn[0], scales_attn[0]), lora_A_h[0], lora_B_attn[0])
        k = _lin_lora(x, _dequant(codes_attn[1], scales_attn[1]), lora_A_h[1], lora_B_attn[1])
        v = _lin_lora(x, _dequant(codes_attn[2], scales_attn[2]), lora_A_h[2], lora_B_attn[2])
        attn = (q + k + v) / 3.0
        o = _lin_lora(attn, _dequant(codes_attn[3], scales_attn[3]), lora_A_h[3], lora_B_attn[3])
        x1 = x + o
        g = _lin_lora(x1, _dequant(codes_gu[0], scales_gu[0]), lora_A_h[4], lora_B_gu[0])
        u = _lin_lora(x1, _dequant(codes_gu[1], scales_gu[1]), lora_A_h[5], lora_B_gu[1])
        h = jax.nn.silu(g) * u
        d = _lin_lora(h, _dequant(codes_down, scales_down), lora_A_down, lora_B_down)
        return x1 + d

    def _L0_ffn_ref(x, W_gate, W_up, W_down):
        import jax, jax.numpy as jnp
        import numpy as np
        HD, M = (512, 1792)
        gate = jnp.einsum('bsh,mh->bsm', x, W_gate)
        up = jnp.einsum('bsh,mh->bsm', x, W_up)
        h = jax.nn.silu(gate) * up
        out = jnp.einsum('bsm,hm->bsh', h, W_down)
        return out
    x = L0_attn_x
    mod = (_silu(L0_c) @ L0_wmod).reshape(L0_c.shape[0], 6, 1, -1)
    sa, ca, ga, sb, cb, gb = (mod[:, 0], mod[:, 1], mod[:, 2], mod[:, 3], mod[:, 4], mod[:, 5])
    ga = (2 * (ga >= 0) - 1) * jnp.maximum(jnp.abs(ga), 0.25)
    gb = (2 * (gb >= 0) - 1) * jnp.maximum(jnp.abs(gb), 0.25)
    h = _layernorm(x, axis=-1) * (1 + ca) + sa
    x = x + ga * _L0_attn_ref(h, L0_attn_codes_attn, L0_attn_scales_attn, L0_attn_codes_gu, L0_attn_scales_gu, L0_attn_codes_down, L0_attn_scales_down, L0_attn_lora_A_h, L0_attn_lora_A_down, L0_attn_lora_B_attn, L0_attn_lora_B_gu, L0_attn_lora_B_down)
    h = _layernorm(x, axis=-1) * (1 + cb) + sb
    x = x + gb * _L0_ffn_ref(h, L0_ffn_W_gate, L0_ffn_W_up, L0_ffn_W_down)
    return x

_drawn_inputs = setup_inputs


def setup_inputs(seed=0):
    import zlib

    import numpy as np

    out = dict(_drawn_inputs(seed))
    spreads = {}
    factors = {'L0_attn_scales_attn': 8.0,
     'L0_attn_scales_gu': 8.0,
     'L0_attn_scales_down': 8.0,
     'L0_attn_lora_A_h': 8.0,
     'L0_attn_lora_A_down': 8.0,
     'L0_attn_lora_B_attn': 8.0,
     'L0_attn_lora_B_gu': 8.0,
     'L0_attn_lora_B_down': 8.0,
     'L0_ffn_W_gate': 8.0,
     'L0_ffn_W_up': 8.0,
     'L0_ffn_W_down': 8.0}
    for name, (base, spread) in spreads.items():
        noise = np.random.default_rng([zlib.crc32(name.encode()), seed]).standard_normal(out[name].shape)
        drawn = base * np.exp(spread * noise) if base else spread * noise
        out[name] = jnp.asarray(drawn.astype(out[name].dtype))
    for name, factor in factors.items():
        out[name] = (out[name] * factor).astype(out[name].dtype)
    return out
```

```python
import concourse.bass as bass
from concourse import mybir
from contextlib import ExitStack

P = 128
NB, SEQ, H, I, R = 8, 256, 512, 1792, 16
T = NB * SEQ
KT = H // P
MT = I // P
TG, GT = 4, 512
TT = T // P
BLOCK = 64
UNIT = 12 * P
HALF = MT // 2
EPS = 1e-5

SHIFT = [-0.035814154893159866, -3.722414255142212, -0.4697154462337494, -3.2984719276428223,
         -1.0957497358322144, -2.6926143169403076, -1.9447404146194458]
OFFSET = [0.011445658281445503, 0.013174708932638168, 0.15736202895641327, 0.17014329135417938,
          0.338535875082016, 0.3751530349254608, 0.3761288821697235]
LEAD = 0.0039697647687094795
NF = len(SHIFT)

WS = 256.0
MS = 64.0
HS = 1.0 / 16.0


def adaln_kernel(nc, x, codes_attn, scales_attn, codes_gu, scales_gu, codes_down, scales_down,
                 lora_A_h, lora_A_down, lora_B_attn, lora_B_gu, lora_B_down,
                 W_gate, W_up, W_down, cond, wmod, gates_dram, out):
    f32, f16, i32 = mybir.dt.float32, mybir.dt.float16, mybir.dt.int32
    ALU = mybir.AluOpType
    ACT = mybir.ActivationFunctionType
    x_rows = x.rearrange("b s h -> (b s) h")
    out_rows = out.rearrange("b s h -> (b s) h")

    ctx = ExitStack()
    with ctx:
        def sb(name, nbytes):
            return ctx.enter_context(nc.sbuf_tensor(name, [P, nbytes // 4], f32))

        def view(region, at, dt, n):
            size = 2 if dt == f16 else 4
            v = region[:, at // 4:(at + n * size) // 4]
            return v if dt == f32 else v.bitcast(dt)

        def sem(name):
            return ctx.enter_context(nc.semaphore(name))

        HID = sb("hidden_region", HALF * 2 * T * 2)
        X1 = sb("x1_region", TT * 2 * KT * P * 2)
        Z = sb("z_region", TT * H * 4)
        WD = sb("down_weights_region", MT * 2 * H * 2)
        DQ = sb("dequant_region", 5 * UNIT * 4)
        NAT = sb("natural_region", 2 * UNIT * 2)
        WTR = sb("weights_region", 2 * 2 * 2 * H * 2)
        SR = sb("scratch_region", 8192)
        LSH = sb("lora_shared_region", (2 * H + H) * 2)
        CST = sb("constants_region", 512 + 256 + 256 + 512 + 1344 + 128)

        identF = view(CST, 0, f32, P)
        ident = view(CST, 512, f16, P)
        identS = view(CST, 768, f16, P)
        modT = view(CST, 1024, f32, NB * 16).rearrange("p (b c) -> p b c", b=NB)
        sc_gu = view(CST, 1536, f32, MT * 24).rearrange("p (m s) -> p m s", m=MT)
        small = view(CST, 2880, f32, 32)
        stats = small[:, 0:12].rearrange("p (j s) -> p j s", j=2)
        moments = small[:, 12:16].rearrange("p (j s) -> p j s", j=2)
        varpe = small[:, 16:18]
        rstd = small[:, 18:20]
        minus_half = small[:, 20:22]

        def acts(region):
            return view(region, 0, f16, TT * 2 * KT * P).rearrange("p (t a k n) -> p t a k n", t=TT, a=2, k=KT)
        hT, x1T, h2T = acts(HID), acts(X1), acts(X1)
        z = view(Z, 0, f32, TT * H).rearrange("p (t n) -> p t n", t=TT)
        hid = view(HID, 0, f16, HALF * 2 * T).rearrange("p (m a n) -> p m a n", m=HALF, a=2)
        hid2 = view(HID, 0, f16, MT * 2 * GT).rearrange("p (m a n) -> p m a n", m=MT, a=2)
        WdT = view(WD, 0, f16, MT * 2 * H).rearrange("p (m a n) -> p m a n", m=MT, a=2)
        loraM = view(WD, 0, f16, MT * 1024).rearrange("p (m n) -> p m n", m=MT)
        WT = view(WTR, 0, f16, 2 * 2 * 2 * H).rearrange("p (s g a n) -> p s g a n", s=2, g=2, a=2)
        sq = view(DQ, 0, f32, 3 * UNIT).rearrange("p (s n) -> p s n", s=3)
        acc = view(DQ, 3 * UNIT * 4, f32, 2 * UNIT).rearrange("p (s n) -> p s n", s=2)
        nat = view(NAT, 0, f16, 2 * UNIT).rearrange("p (a n) -> p a n", a=2)
        srow = view(SR, 0, f32, 2 * GT).rearrange("p (s n) -> p s n", s=2)
        A_gu = view(LSH, 0, f16, 2 * H)
        B_dn = view(LSH, 2 * H * 2, f16, H)
        codesZ = view(Z, 0, i32, 2 * UNIT).rearrange("p (s n) -> p s n", s=2)
        codesW = view(WD, 0, i32, 2 * UNIT).rearrange("p (s n) -> p s n", s=2)

        xin = view(Z, 2 * UNIT * 4, f32, 4 * 2 * H).rearrange("p (s j n) -> p s j n", s=4, j=2)
        hmod1 = view(Z, 2 * UNIT * 4 + 4 * 4096, f32, 2 * H).rearrange("p (k n) -> p k n", k=KT)
        WoT = view(HID, 32768, f16, 2 * 4 * H).rearrange("p (a o n) -> p a o n", a=2, o=4)
        M1T = view(HID, 40960, f16, 4 * 2 * H).rearrange("p (k a n) -> p k a n", k=4, a=2)
        qkvS = view(HID, 49152, f16, 2 * 2 * H).rearrange("p (s a n) -> p s a n", s=2, a=2)
        raw_sa = view(HID, 53248, f32, 128).rearrange("p (m t s) -> p m t s", m=4, t=4)
        raw_sg = view(HID, 53760, f32, 224).rearrange("p (g m s) -> p g m s", g=2, m=MT)
        raw_sd = view(HID, 54656, f32, 112).rearrange("p (t m s) -> p t m s", t=4, m=MT)
        sc_o = view(HID, 55104, f32, 32)
        sc_q = view(HID, 55232, f32, 96).rearrange("p (t m s) -> p t m s", t=4, m=3)
        rawA = view(HID, 0, f32, 6 * H + I)
        rawB = view(HID, 19456, f32, 48 * R).rearrange("p (t r) -> p t r", t=48)
        Bst = view(HID, 22528, f16, 48 * 96).rearrange("p (t c) -> p t c", t=48)
        A_at = view(WTR, 0, f16, 4 * H)
        B_at = view(WTR, 4096, f16, 4 * H)
        wm = view(X1, 0, f32, 2 * 4 * H).rearrange("p (s k n) -> p s k n", s=2, k=4)
        rows = view(X1, 16384, f32, 6 * H).rearrange("p (j n) -> p j n", j=6)
        clamp = view(X1, 28672, f32, 2 * H).rearrange("p (s n) -> p s n", s=2)
        crow = view(SR, 4096, f32, H)
        csT = view(SR, 6144, f32, 4 * NB).rearrange("p (k b) -> p k b", k=4)
        mrow = srow

        xr = view(WTR, 0, f32, 2 * H).rearrange("p (j n) -> p j n", j=2)
        gateA = view(WTR, 4096, f32, H)
        xn2 = view(SR, 0, f32, 2 * H).rearrange("p (j n) -> p j n", j=2)
        hmod2 = view(SR, 4096, f32, 2 * H).rearrange("p (k n) -> p k n", k=KT)
        ffn_nat = view(NAT, 0, f16, 2 * UNIT).rearrange("p (s n) -> p s n", s=2)
        F_gu = view(DQ, 0, f16, MT * 2 * H).rearrange("p (m g n) -> p m g n", m=MT, g=2)
        F_d = view(WD, 0, f16, MT * H).rearrange("p (m n) -> p m n", m=MT)
        orow = view(WTR, 0, f32, 2 * H).rearrange("p (s n) -> p s n", s=2)
        gateB = view(WTR, 4096, f32, 2 * H).rearrange("p (s n) -> p s n", s=2)

        bank = [ctx.enter_context(nc.psum_tensor(f"bank{i}", [P, 512], f32)) for i in range(8)]
        gate_bank, up_bank, prep_bank, out_bank = bank[0:2], bank[2:4], bank[4:6], bank[4:6]
        d_bank, ln_bank, fold_bank = bank[0:2], bank[6:8], bank[0:4]
        ffn_gu_bank = bank[2][:, :].bitcast(f16)
        ffn_d_bank = bank[3][:, 0:256].bitcast(f16)

        raw_clear, ident_ready, lora_b_in, lora_a_in, scales_in, cond_in = map(
            sem, ["raw_clear", "ident_ready", "lora_b_in", "lora_a_in", "scales_in", "cond_in"])
        bst_hi, bst_ready, lora_T, lora_out, a_hi, a_ready, scales_ready = map(
            sem, ["bst_hi", "bst_ready", "lora_T", "lora_out", "a_hi", "a_ready", "scales_ready"])
        silu_c, cs_T, cs_ready, mod_done, row_done, modT_T, modT_ready, clamp_step, gates_out = map(
            sem, ["silu_c", "cs_T", "cs_ready", "mod_done", "row_done", "modT_T", "modT_ready",
                  "clamp_step", "gates_out"])
        wmod_in = [sem("wmod_in0"), sem("wmod_in1")]
        codes_in = [sem("codes_in0"), sem("codes_in1")]
        x_in = [sem(f"x_in{s}") for s in range(4)]
        sq_ready, lin_done, sq_used, chain, nat_hi, nat_lo = map(
            sem, ["sq_ready", "lin_done", "sq_used", "chain", "nat_hi", "nat_lo"])
        prep_done, prep_hi, prep_evac = map(sem, ["prep_done", "prep_hi", "prep_evac"])
        fold_done, m_step, m_hi, m_lo = map(sem, ["fold_done", "m_step", "m_hi", "m_lo"])
        ln_stat, ln_var, ln_rstd, ln_xn, ln_T, ln_mod, ln_hi, ln_lo = map(
            sem, ["ln_stat", "ln_var", "ln_rstd", "ln_xn", "ln_T", "ln_mod", "ln_hi", "ln_lo"])
        x1_done, x1_hi, x1_lo = map(sem, ["x1_done", "x1_hi", "x1_lo"])
        g_done, u_done, silu_done, hid_mul, hid_hi, hid_lo = map(
            sem, ["g_done", "u_done", "silu_done", "hid_mul", "hid_hi", "hid_lo"])
        d_done, z_evac, y_step, x2_done, xg_in = map(
            sem, ["d_done", "z_evac", "y_step", "x2_done", "xg_in"])
        ffn_in = [sem("ffn_in0"), sem("ffn_in1")]
        ffn_T, ffn_gu_out, ffn_d_out = map(sem, ["ffn_T", "ffn_gu_out", "ffn_d_out"])
        gateb_in, o_done, o_mul, out_ready = map(sem, ["gateb_in", "o_done", "o_mul", "out_ready"])
        out_dma = [sem("out_dma0"), sem("out_dma1")]

        def wait(eng, s, value):
            if isinstance(value, int) and value <= 0:
                return
            eng.wait_ge(s, value)

        Q0, J0 = 6, 8

        block = ctx.enter_context(nc.Block())

        @block.sync
        def _(sp):
            def load_x(b):
                if b >= 4:
                    sp.wait_ge(ln_T, b - 3)
                sp.dma_start(xin[:, b % 4], x_rows[b * SEQ:(b + 1) * SEQ].rearrange("(j p) n -> p j n", p=P))\
                    .then_inc(x_in[b % 4], 16)

            def slot_free(q):
                wait(sp, sq_ready, 7 * (q - 1))
                wait(sp, lin_done, q - 1)

            def load_attn(q):
                slot_free(q)
                if q == 0:
                    src = codes_attn[3, 0:3 * P].rearrange("(t p) n -> p t n", p=P)
                elif q == 1:
                    src = codes_attn[3, 3 * P:4 * P].rearrange("(t p) n -> p t n", p=P)
                else:
                    src = codes_attn[0:3, (q - 2) * P:(q - 1) * P].rearrange("m p n -> p m n")
                n = 1 if q == 1 else 3
                sp.dma_start(codesZ[:, q % 2, 0:n * H].rearrange("p (t n) -> p t n", t=n), src)\
                    .then_inc(codes_in[q % 2], 16)

            def load_mlp(m, p, codes, first):
                if first:
                    sp.wait_ge(d_done, TT)
                else:
                    slot_free(Q0 + m)
                sp.dma_start(codes[:, p, 0:2 * H].rearrange("p (g n) -> p g n", g=2),
                             codes_gu[:, bass.ds(m * P, P)].rearrange("g p n -> p g n"))\
                    .then_inc(codes_in[p], 16)
                sp.dma_start(codes[:, p, 2 * H:3 * H].rearrange("p (t n) -> p t n", t=4),
                             codes_down[:, bass.ds(m * P, P)].rearrange("(t p) n -> p t n", p=P))\
                    .then_inc(codes_in[p], 16)

            def load_wmod(n, j):
                if n >= 2:
                    sp.wait_ge(mod_done, n - 1)
                sp.dma_start(wm[:, n % 2], wmod[:, j * H:(j + 1) * H].rearrange("(k p) n -> p k n", p=P))\
                    .then_inc(wmod_in[n % 2], 16)

            load_attn(0)
            load_x(0)
            load_x(1)
            load_attn(1)
            for n, j in enumerate([0, 1, 3, 4]):
                load_wmod(n, j)
            load_attn(2)
            load_wmod(4, 2)
            load_wmod(5, 5)
            load_x(2)
            load_x(3)
            load_attn(3)
            load_x(4)
            load_x(5)
            sp.wait_ge(clamp_step, 8)
            sp.dma_start(gates_dram[0], rows[0:NB, 2]).then_inc(gates_out, 16)
            sp.dma_start(gates_dram[1], rows[0:NB, 5]).then_inc(gates_out, 16)
            load_attn(4)
            load_x(6)
            load_x(7)
            load_attn(5)
            with sp.Fori(0, 4) as i:
                load_mlp(2 * i, 0, codesZ, False)
                load_mlp(2 * i + 1, 1, codesZ, False)
            load_mlp(8, 0, codesZ, False)
            load_mlp(9, 1, codesW, True)
            load_mlp(10, 0, codesW, True)
            load_mlp(11, 1, codesW, False)
            load_mlp(12, 0, codesW, False)
            load_mlp(13, 1, codesW, False)

            def load_ffn(e, s):
                wait(sp, ffn_T, e - 1)
                row = bass.ds(e * P, P)
                sp.dma_start(ffn_nat[:, s, 0:H], W_gate[row]).then_inc(ffn_in[s], 16)
                sp.dma_start(ffn_nat[:, s, H:2 * H], W_up[row]).then_inc(ffn_in[s], 16)
                sp.dma_start(ffn_nat[:, s, 2 * H:3 * H].rearrange("p (t n) -> p t n", t=4),
                             W_down[:, row].rearrange("(t p) n -> p t n", p=P)).then_inc(ffn_in[s], 16)

            def load_residual(b):
                wait(sp, x2_done, 2 * b)
                sp.dma_start(xr[:, :, :], x_rows[bass.ds(b * SEQ, SEQ)].rearrange("(j p) n -> p j n", p=P))\
                    .then_inc(xg_in, 16)
                sp.dma_start(gateA[:, :], gates_dram[0, bass.ds(b, 1)].partition_broadcast(P)
                             .rearrange("p a n -> p (a n)")).then_inc(xg_in, 16)

            sp.wait_ge(prep_done, J0 + 3 * MT)
            load_ffn(0, 0)
            load_ffn(1, 1)
            sp.wait_ge(gates_out, 32)
            sp.wait_ge(u_done, 4 * MT)
            load_residual(0)
            with sp.Fori(1, 7) as b:
                load_residual(b)
                load_ffn(2 * b, 0)
                load_ffn(2 * b + 1, 1)
            load_residual(7)

            def load_gate(tg):
                for s in range(2):
                    sp.dma_start(gateB[:, s], gates_dram[1, bass.ds(2 * tg + s, 1)].partition_broadcast(P)
                                 .rearrange("p a n -> p (a n)")).then_inc(gateb_in, 16)

            def store(tg):
                for j in range(4):
                    sp.wait_ge(out_ready, 4 * tg + j + 1)
                    sp.dma_start(out_rows[bass.ds(tg * GT + j * P, P)], orow[:, j % 2]).then_inc(out_dma[j % 2], 16)

            sp.wait_ge(x2_done, TT)
            load_gate(0)
            with sp.Fori(0, 3) as tg:
                store(tg)
                load_gate(tg + 1)
            store(3)
            sp.wait_ge(out_dma[0], 16 * TT // 2)
            sp.wait_ge(out_dma[1], 16 * TT // 2)

        @block.gpsimd
        def _(pool):
            pool.memset(minus_half, -0.5)
            pool.memset(identF, 0.0).then_inc(ident_ready, 1)
            pool.wait_ge(ident_ready, 1)
            pool.affine_select(out=identF, in_=identF, compare_op=ALU.not_equal, fill=1.0, base=0,
                               pattern=[[-1, P]], channel_multiplier=1).then_inc(ident_ready, 1)

            def low_a():
                grp = slice(32, 48)
                pool.wait_ge(ln_rstd, 2)
                pool.wait_ge(a_hi, 3)
                for dst, at, n in ((A_at, 0, 4 * H), (A_gu, 4 * H, 2 * H)):
                    pool.tensor_tensor(dst[grp], rawA[grp, at:at + n], dst[grp], ALU.subtract)
                pool.tensor_tensor(loraM[grp, :, 256:384], rawA[grp, 6 * H:].rearrange("p (m n) -> p m n", m=MT),
                                   loraM[grp, :, 256:384], ALU.subtract).then_inc(a_ready, 1)
                pool.wait_ge(a_ready, 1)

            def ln_power(L):
                pool.wait_ge(ln_var, L + 1)
                pool.tensor_tensor(rstd, varpe, minus_half, ALU.pow).then_inc(ln_rstd, 1)

            def ln_low(L, b, dst, hmod):
                pool.wait_ge(ln_hi, L + 1)
                view4 = dst[:, bass.ds(2 * b, 2)].rearrange("p j a k n -> p a k j n")
                pool.tensor_tensor(view4[:, 1], hmod.rearrange("p k (j n) -> p k j n", j=2), view4[:, 0],
                                   ALU.subtract).then_inc(ln_lo, 1)

            def natural_low(q, p, n):
                pool.wait_ge(nat_hi, q + 1)
                pool.tensor_tensor(nat[:, 1, 0:n], acc[:, p, 0:n], nat[:, 0, 0:n], ALU.subtract).then_inc(nat_lo, 1)

            def hidden_low(n, s, dst):
                pool.wait_ge(hid_hi, n + 1)
                pool.tensor_tensor(dst[:, 1], srow[:, s], dst[:, 0], ALU.subtract).then_inc(hid_lo, 1)

            def mlp_tile(m, p, slot, unit):
                for tg in range(TG):
                    hidden_low(4 * m + tg, tg % 2, hid[:, slot, :, tg * GT:(tg + 1) * GT])
                if unit:
                    natural_low(Q0 + m + 2, p, UNIT)

            ln_power(0)
            ln_power(1)
            low_a()
            natural_low(0, 0, UNIT)
            natural_low(1, 1, H)
            for ot in range(4):
                if ot > 0:
                    ln_power(2 * ot)
                    ln_power(2 * ot + 1)
                ln_low(2 * ot, 2 * ot, hT, hmod1)
                ln_low(2 * ot + 1, 2 * ot + 1, hT, hmod1)
                natural_low(2 + ot, ot % 2, UNIT)
            natural_low(Q0, 0, UNIT)
            natural_low(Q0 + 1, 1, UNIT)
            with pool.Fori(0, 3) as i:
                mlp_tile(2 * i, 0, 2 * i, True)
                mlp_tile(2 * i + 1, 1, 2 * i + 1, True)
            mlp_tile(6, 0, 6, True)
            mlp_tile(7, 1, 0, True)
            with pool.Fori(4, 6) as i:
                mlp_tile(2 * i, 0, 2 * i - HALF, True)
                mlp_tile(2 * i + 1, 1, 2 * i + 1 - HALF, True)
            mlp_tile(12, 0, 5, False)
            mlp_tile(13, 1, 6, False)

            ln_power(NB)
            with pool.Fori(1, NB) as b:
                ln_power(NB + b)
                ln_low(NB + b - 1, b - 1, h2T, hmod2)
            ln_low(2 * NB - 1, NB - 1, h2T, hmod2)
            with pool.Fori(0, TG) as tg:
                with pool.Fori(0, MT // 2) as i:
                    for s in range(2):
                        hidden_low(4 * MT + tg * MT + 2 * i + s, s, hid2[:, 2 * i + s])

        @block.scalar
        def _(act):
            act.dma_start(rawB[:, 0:16].rearrange("p (m t) r -> p m t r", m=4),
                          lora_B_attn.rearrange("m (t p) r -> p m t r", p=P)).then_inc(lora_b_in, 16)
            act.dma_start(rawB[:, 16:44].rearrange("p (g t) r -> p g t r", g=2),
                          lora_B_gu.rearrange("g (t p) r -> p g t r", p=P)).then_inc(lora_b_in, 16)
            act.dma_start(rawB[:, 44:48], lora_B_down.rearrange("(t p) r -> p t r", p=P)).then_inc(lora_b_in, 16)
            act.dma_start(crow[0:NB], cond).then_inc(cond_in, 16)
            act.dma_start(raw_sa, scales_attn.rearrange("m (t p) s -> p m t s", p=P)).then_inc(scales_in, 16)
            act.dma_start(raw_sg, scales_gu.rearrange("g (m p) s -> p g m s", p=P)).then_inc(scales_in, 16)
            act.dma_start(raw_sd.rearrange("p t m s -> p t (m s)"),
                          scales_down.rearrange("(t p) s -> p t s", p=P)).then_inc(scales_in, 16)
            act.wait_ge(raw_clear, 1)
            for g in range(3):
                rowsA = slice(32 * g, 32 * g + R)
                act.dma_start(rawA[rowsA, 0:6 * H].rearrange("r (m n) -> r m n", m=6),
                              lora_A_h.rearrange("m r n -> r m n")).then_inc(lora_a_in, 16)
                act.dma_start(rawA[rowsA, 6 * H:6 * H + I], lora_A_down).then_inc(lora_a_in, 16)

            act.wait_ge(ident_ready, 2)
            act.activation(ident, identF, ACT.Copy).then_inc(ident_ready, 1)
            act.activation(identS, identF, ACT.Copy, scale=WS * HS).then_inc(ident_ready, 1)
            act.wait_ge(cond_in, 16)
            act.activation(crow[0:NB], crow[0:NB], ACT.Silu).then_inc(silu_c, 1)
            act.wait_ge(lora_b_in, 48)
            act.wait_ge(raw_clear, 2)
            act.activation(Bst[:, :, 0:R], rawB[:, :, :], ACT.Copy, scale=WS).then_inc(bst_hi, 1)
            act.activation(Bst[:, :, 32:32 + R], rawB[:, :, :], ACT.Copy, scale=WS).then_inc(bst_hi, 1)

            def square(q, p, i, codes, n):
                if i == 0:
                    wait(act, sq_used, NF * q)
                elif i >= 3:
                    act.wait_ge(sq_used, NF * q + i - 2)
                act.activation(sq[:, i % 3, 0:n], codes[:, p, 0:n], ACT.Square, bias=SHIFT[i], scale=0.25)\
                    .then_inc(sq_ready, 1)

            def natural_high(q, p, n):
                act.wait_ge(sq_used, NF * (q + 1))
                wait(act, prep_done, (J0 + 3 * (q - Q0)) if not isinstance(q, int) or q >= Q0
                     else [0, 3, 4, 5, 6, 7][q])
                act.activation(nat[:, 0, 0:n], acc[:, p, 0:n], ACT.Copy).then_inc(nat_hi, 1)

            def prep_high(j, bk, dst, src=None):
                act.wait_ge(prep_done, j + 1)
                act.activation(dst, bk[:, :] if src is None else src(bk), ACT.Copy).then_inc(prep_hi, 1)

            def ln_modulate(L, b, kind, dst, hmod):
                act.wait_ge(ln_T, L + 1)
                wait(act, ln_lo, L)
                for k in range(KT):
                    last = act.activation(hmod[:, k], ln_bank[k // 2][:, (k % 2) * SEQ:(k % 2 + 1) * SEQ],
                                          ACT.Identity,
                                          scale=modT[:, bass.ds(b, 1), kind + 4 + k],
                                          bias=modT[:, bass.ds(b, 1), kind + k])
                last.then_inc(ln_mod, 1)
                act.wait_ge(ln_mod, L + 1)
                view4 = dst[:, bass.ds(2 * b, 2)].rearrange("p j a k n -> p a k j n")
                act.activation(view4[:, 0], hmod.rearrange("p k (j n) -> p k j n", j=2), ACT.Copy).then_inc(ln_hi, 1)

            def silu(n, s):
                act.wait_ge(g_done, n + 1)
                wait(act, hid_lo, n - 1)
                return act.activation(srow[:, s], gate_bank[s][:, :], ACT.Silu,
                                      scale=1.0 / WS)

            def hidden_high(n, s, dst):
                act.wait_ge(hid_mul, n + 1)
                act.activation(dst[:, 0], srow[:, s], ACT.Copy).then_inc(hid_hi, 1)

            act.wait_ge(codes_in[0], 16)
            for i in range(NF):
                square(0, 0, i, codesZ, UNIT)
                if i == 1:
                    act.wait_ge(lora_a_in, 96)
                    act.activation(A_at[0:96], rawA[0:96, 0:4 * H], ACT.Copy).then_inc(a_hi, 1)
                    act.activation(A_gu[0:96], rawA[0:96, 4 * H:6 * H], ACT.Copy).then_inc(a_hi, 1)
                    act.activation(loraM[0:96, :, 256:384],
                                   rawA[0:96, 6 * H:].rearrange("p (m n) -> p m n", m=MT), ACT.Copy)\
                        .then_inc(a_hi, 1)
                if i == 3:
                    def stack(g, n, dst):
                        act.wait_ge(lora_T, g + 1)
                        act.activation(dst, bank[g][0:96, 0:n * 64].bitcast(f16).rearrange("p (t n) -> p t n", t=n),
                                       ACT.Copy).then_inc(lora_out, 1)
                    stack(0, 8, B_at[0:96, 0:1024].rearrange("p (t n) -> p t n", t=8))
                    stack(1, 8, B_at[0:96, 1024:2048].rearrange("p (t n) -> p t n", t=8))
                    stack(2, 8, loraM[0:96, 0:8, 0:128])
                    stack(3, 6, loraM[0:96, 8:14, 0:128])
                    stack(4, 8, loraM[0:96, 0:8, 128:256])
                    stack(5, 6, loraM[0:96, 8:14, 128:256])
                    stack(6, 4, B_dn[0:96].rearrange("p (t n) -> p t n", t=4))
            natural_high(0, 0, UNIT)
            for i in range(NF):
                if i == 0:
                    act.wait_ge(codes_in[1], 16)
                square(1, 1, i, codesZ, H)
            for t in range(3):
                prep_high(t, prep_bank[t % 2], WoT[:, 0, :, t * P:(t + 1) * P],
                          lambda bk: bk[:, :].rearrange("p (o n) -> p o n", o=4))
            natural_high(1, 1, H)
            for ot in range(4):
                p = ot % 2
                act.wait_ge(codes_in[p], 16 * (ot // 2 + 2))
                for i in range(NF):
                    square(2 + ot, p, i, codesZ, UNIT)
                    if i == 3 and ot == 0:
                        prep_high(3, prep_bank[1], WoT[:, 0, :, 3 * P:4 * P],
                                  lambda bk: bk[:, :].rearrange("p (o n) -> p o n", o=4))
                    elif i == 3:
                        prep_high(3 + ot, prep_bank[1 - p], qkvS[:, 1 - p, 0])
                if ot == 0:
                    act.wait_ge(modT_ready, 1)
                ln_modulate(2 * ot, 2 * ot, 0, hT, hmod1)
                ln_modulate(2 * ot + 1, 2 * ot + 1, 0, hT, hmod1)
                natural_high(2 + ot, p, UNIT)
            prep_high(7, prep_bank[1], qkvS[:, 1, 0])
            for ht in range(KT):
                act.wait_ge(m_step, ht + 1)
                act.activation(M1T[:, ht, 0], mrow[:, ht % 2], ACT.Copy).then_inc(m_hi, 1)

            act.wait_ge(gates_out, 32)
            for tg in range(TG):
                q, p = Q0 + tg // 2, tg // 2
                if tg % 2 == 0:
                    act.wait_ge(codes_in[p], 16 * 3 + 32)
                for k in range(KT):
                    act.wait_ge(x1_done, 4 * tg + k + 1)
                    act.activation(x1T[:, 4 * tg:4 * tg + 4, 0, k], bank[k % 2][:, :].rearrange("p (t n) -> p t n", t=4),
                                   ACT.Copy, scale=1.0 / MS).then_inc(x1_hi, 1)
                    i = 4 * (tg % 2) + k
                    if i < NF:
                        square(q, p, i, codesZ, UNIT)
                    if tg == 3 and k < 3:
                        prep_high(J0 + k, prep_bank[k % 2], WT[:, 0, k, 0] if k < 2 else WdT[:, 0, 0])
                if tg % 2 == 1:
                    natural_high(q, p, UNIT)

            def mlp_tile(m, p, slot, unit, prep, codes):
                if unit:
                    act.wait_ge(codes_in[p], 48 + 32 * (m // 2 + 2) if isinstance(m, int)
                                else 48 + 16 * (m - p) + 64)
                for tg in range(TG):
                    n, s = 4 * m + tg, tg % 2
                    silu(n, s).then_inc(silu_done, 1)
                    if unit:
                        square(Q0 + m + 2, p, 2 * tg, codes, UNIT)
                    hidden_high(n, s, hid[:, slot, :, tg * GT:(tg + 1) * GT])
                    if prep and tg < 3:
                        prep_high(J0 + 3 * (m + 1) + tg, prep_bank[(p + 1 + tg) % 2],
                                  WT[:, 1 - p, tg, 0] if tg < 2 else WdT[:, m + 1, 0])
                    if unit and tg < 3:
                        square(Q0 + m + 2, p, 2 * tg + 1, codes, UNIT)
                if unit:
                    natural_high(Q0 + m + 2, p, UNIT)

            mlp_tile(0, 0, 0, True, True, codesZ)
            mlp_tile(1, 1, 1, True, True, codesZ)
            with act.Fori(1, 3) as i:
                mlp_tile(2 * i, 0, 2 * i, True, True, codesZ)
                mlp_tile(2 * i + 1, 1, 2 * i + 1, True, True, codesZ)
            mlp_tile(6, 0, 6, True, True, codesZ)
            with act.Fori(0, NB) as b:
                for j in range(2):
                    act.wait_ge(d_done, 2 * b + j + 1)
                    act.activation(z[:, 2 * b + j], d_bank[j][:, :], ACT.Copy, scale=1.0 / (WS * HS))\
                        .then_inc(z_evac, 1)
            mlp_tile(7, 1, 0, True, True, codesW)
            with act.Fori(4, 6) as i:
                mlp_tile(2 * i, 0, 2 * i - HALF, True, True, codesW)
                mlp_tile(2 * i + 1, 1, 2 * i + 1 - HALF, True, True, codesW)
            mlp_tile(12, 0, 5, False, True, codesW)
            mlp_tile(13, 1, 6, False, False, codesW)

            def ffn_out(e):
                act.wait_ge(ffn_T, e + 1)
                act.activation(F_gu[:, e].rearrange("p g n -> p (g n)"), ffn_gu_bank, ACT.Copy).then_inc(ffn_gu_out, 1)

            with act.Fori(1, NB) as b:
                ln_modulate(NB + b - 1, b - 1, 8, h2T, hmod2)
                ffn_out(2 * b - 2)
                ffn_out(2 * b - 1)
            ln_modulate(2 * NB - 1, NB - 1, 8, h2T, hmod2)

            with act.Fori(0, TG) as tg:
                with act.Fori(0, MT // 2) as i:
                    for s in range(2):
                        n = 4 * MT + tg * MT + 2 * i + s
                        act.wait_ge(g_done, n + 1)
                        act.wait_ge(hid_lo, n - 1)
                        act.activation(srow[:, s], gate_bank[s][:, :], ACT.Silu).then_inc(silu_done, 1)
                        hidden_high(n, s, hid2[:, 2 * i + s])

        @block.vector
        def _(dve):
            dve.memset(rawA[0:96], 0.0).then_inc(raw_clear, 1)
            dve.memset(Bst[:, :, :], 0.0).then_inc(raw_clear, 1)

            K = LEAD * WS
            dve.wait_ge(scales_in, 48)
            dve.tensor_scalar(sc_o.rearrange("p (t s) -> p t s", t=4), raw_sa[:, 3], K, None, ALU.mult)
            dve.tensor_scalar(sc_q.rearrange("p t m s -> p m t s"), raw_sa[:, 0:3], K, None, ALU.mult)
            dve.tensor_scalar(sc_gu[:, :, 0:16].rearrange("p m (g s) -> p g m s", g=2), raw_sg, K, None, ALU.mult)
            dve.tensor_scalar(sc_gu[:, :, 16:24].rearrange("p m (t s) -> p t m s", t=4), raw_sd, K, None,
                              ALU.mult).then_inc(scales_ready, 1)
            dve.wait_ge(bst_hi, 1)
            dve.scalar_tensor_tensor(Bst[:, :, 64:64 + R], rawB[:, :, :], WS, Bst[:, :, 0:R], ALU.mult, ALU.subtract)\
                .then_inc(bst_ready, 1)
            dve.wait_ge(cs_T, 1)
            dve.tensor_copy(csT.rearrange("p k b -> p (k b)"), bank[7][:, 0:4 * NB]).then_inc(cs_ready, 1)

            def linear(q, p, codes, scale, n):
                wait(dve, nat_lo, q - 1)
                dve.scalar_tensor_tensor(acc[:, p, 0:n].rearrange("p (s c) -> p s c", c=BLOCK),
                                         codes[:, p, 0:n].rearrange("p (s c) -> p s c", c=BLOCK), -7.0,
                                         scale.unsqueeze(2).broadcast_to([P, n // BLOCK, BLOCK]),
                                         ALU.add, ALU.mult).then_inc(lin_done, 1)
                dve.wait_ge(lin_done, q + 1)

            def product(q, p, i, n):
                dve.wait_ge(sq_ready, NF * q + i + 1)
                if i > 0:
                    dve.wait_ge(sq_used, NF * q + i)
                dve.scalar_tensor_tensor(acc[:, p, 0:n], sq[:, i % 3, 0:n], OFFSET[i], acc[:, p, 0:n],
                                         ALU.add, ALU.mult).then_inc(sq_used, 1)

            def prep_low(j, bk, dst, hi, src=None):
                dve.wait_ge(prep_hi, j + 1)
                dve.tensor_tensor(dst, bk[:, :] if src is None else src(bk), hi, ALU.subtract).then_inc(prep_evac, 1)

            def ln_statistics(L, src):
                for j in range(2):
                    last = dve.bn_stats(stats[:, j], src[:, j])
                last.then_inc(ln_stat, 1)
                dve.wait_ge(ln_stat, 2 * L + 1)
                for j in range(2):
                    last = dve.bn_aggr(moments[:, j], stats[:, j])
                last.then_inc(ln_stat, 1)
                dve.wait_ge(ln_stat, 2 * L + 2)
                dve.tensor_scalar(varpe, moments[:, :, 1], EPS, None, ALU.add).then_inc(ln_var, 1)

            def ln_normalise(L, src, dst):
                dve.wait_ge(ln_rstd, L + 1)
                for j in range(2):
                    last = dve.tensor_scalar(dst[:, j], src[:, j], moments[:, j, 0:1], rstd[:, j:j + 1],
                                             ALU.subtract, ALU.mult)
                last.then_inc(ln_xn, 1)
                dve.wait_ge(ln_xn, L + 1)

            def ln_first(b):
                dve.wait_ge(x_in[b % 4], 16 * (b // 4 + 1))
                ln_statistics(b, xin[:, b % 4])
                ln_normalise(b, xin[:, b % 4], xin[:, b % 4])

            def mod_row(n, j):
                dve.wait_ge(mod_done, n + 1)
                src = ln_bank[n % 2][0:NB, :]
                if j in (1, 4):
                    dve.tensor_scalar(rows[0:NB, j], src, 1.0, None, ALU.add).then_inc(row_done, 1)
                else:
                    dve.tensor_copy(rows[0:NB, j], src).then_inc(row_done, 1)

            def clamp_gate(c, j):
                g = rows[0:NB, j]
                dve.tensor_scalar(clamp[0:NB, 0], g, 0.0, 2.0, ALU.is_ge, ALU.mult).then_inc(clamp_step, 1)
                dve.scalar_tensor_tensor(clamp[0:NB, 1], g, -1.0, g, ALU.mult, ALU.max).then_inc(clamp_step, 1)
                dve.wait_ge(clamp_step, 4 * c + 2)
                dve.tensor_scalar(clamp[0:NB, 1], clamp[0:NB, 1], 0.25, None, ALU.max).then_inc(clamp_step, 1)
                dve.wait_ge(clamp_step, 4 * c + 3)
                dve.scalar_tensor_tensor(g, clamp[0:NB, 0], -1.0, clamp[0:NB, 1], ALU.add, ALU.mult)\
                    .then_inc(clamp_step, 1)
                dve.wait_ge(clamp_step, 4 * c + 4)

            wo_view = lambda bk: bk[:, :].rearrange("p (o n) -> p o n", o=4)
            dve.wait_ge(scales_ready, 1)
            dve.wait_ge(codes_in[0], 16)
            linear(0, 0, codesZ, sc_o[:, 0:24], UNIT)
            for i in range(NF):
                product(0, 0, i, UNIT)
                if i == 2:
                    ln_first(0)
                    ln_first(1)
            mod_row(0, 0)
            mod_row(1, 1)
            dve.wait_ge(codes_in[1], 16)
            linear(1, 1, codesZ, sc_o[:, 24:32], H)
            for i in range(NF):
                product(1, 1, i, H)
            for t in range(3):
                prep_low(t, prep_bank[t % 2], WoT[:, 1, :, t * P:(t + 1) * P], WoT[:, 0, :, t * P:(t + 1) * P], wo_view)
            mod_row(2, 3)
            mod_row(3, 4)
            dve.wait_ge(modT_T, 1)
            dve.tensor_copy(modT, bank[3][:, 0:NB * 16].rearrange("p (c b) -> p b c", b=NB)).then_inc(modT_ready, 1)
            for ot in range(4):
                p = ot % 2
                if ot > 0:
                    ln_first(2 * ot)
                    ln_first(2 * ot + 1)
                dve.wait_ge(codes_in[p], 16 * (ot // 2 + 2))
                linear(2 + ot, p, codesZ, sc_q[:, ot].rearrange("p m s -> p (m s)"), UNIT)
                for i in range(NF):
                    product(2 + ot, p, i, UNIT)
                    if i == 3 and ot == 0:
                        prep_low(3, prep_bank[1], WoT[:, 1, :, 3 * P:4 * P], WoT[:, 0, :, 3 * P:4 * P], wo_view)
                    elif i == 3:
                        prep_low(3 + ot, prep_bank[1 - p], qkvS[:, 1 - p, 1], qkvS[:, 1 - p, 0])
                if ot == 0:
                    mod_row(4, 2)
                    mod_row(5, 5)
                    dve.wait_ge(row_done, 6)
                    clamp_gate(0, 2)
                    clamp_gate(1, 5)
            prep_low(7, prep_bank[1], qkvS[:, 1, 1], qkvS[:, 1, 0])

            for ht in range(KT):
                dve.wait_ge(fold_done, 1)
                if ht >= 2:
                    dve.wait_ge(m_lo, ht - 1)
                dve.tensor_scalar(mrow[:, ht % 2], fold_bank[ht][:, :], MS / (3.0 * WS * WS), None, ALU.mult)\
                    .then_inc(chain, 1)
                dve.wait_ge(chain, ht + 1)
                blk = mrow[:, ht % 2, ht * P:(ht + 1) * P]
                dve.scalar_tensor_tensor(blk, identF, MS, blk, ALU.mult, ALU.add).then_inc(m_step, 1)
                dve.wait_ge(m_hi, ht + 1)
                dve.tensor_tensor(M1T[:, ht, 1], mrow[:, ht % 2], M1T[:, ht, 0], ALU.subtract).then_inc(m_lo, 1)

            for tg in range(TG):
                q, p = Q0 + tg // 2, tg // 2
                if tg % 2 == 0:
                    dve.wait_ge(codes_in[p], 16 * 3 + 32)
                for k in range(KT):
                    dve.wait_ge(x1_hi, 4 * tg + k + 1)
                    dve.scalar_tensor_tensor(x1T[:, 4 * tg:4 * tg + 4, 1, k],
                                             bank[k % 2][:, :].rearrange("p (t n) -> p t n", t=4), 1.0 / MS,
                                             x1T[:, 4 * tg:4 * tg + 4, 0, k], ALU.mult, ALU.subtract)\
                        .then_inc(x1_lo, 1)
                    i = 4 * (tg % 2) + k - 1
                    if i < 0:
                        linear(q, p, codesZ, sc_gu[:, tg // 2], UNIT)
                    else:
                        product(q, p, i, UNIT)
                    if tg == 3 and k < 3:
                        dst = WT[:, 0, k] if k < 2 else WdT[:, 0]
                        prep_low(J0 + k, prep_bank[k % 2], dst[:, 1], dst[:, 0])

            def hidden_mul(n, s, scale):
                dve.wait_ge(silu_done, n + 1)
                dve.wait_ge(u_done, n + 1)
                dve.scalar_tensor_tensor(srow[:, s], up_bank[s][:, :], scale, srow[:, s], ALU.mult, ALU.mult)\
                    .then_inc(hid_mul, 1)

            def mlp_tile(m, p, unit, prep, codes):
                q = Q0 + m + 2
                if unit:
                    dve.wait_ge(codes_in[p], 48 + 32 * (m // 2 + 2) if isinstance(m, int)
                                else 48 + 16 * (m - p) + 64)
                for tg in range(TG):
                    hidden_mul(4 * m + tg, tg % 2, HS / WS)
                    if prep and tg < 3:
                        dst = WT[:, 1 - p, tg] if tg < 2 else WdT[:, m + 1]
                        prep_low(J0 + 3 * (m + 1) + tg, prep_bank[(p + 1 + tg) % 2], dst[:, 1], dst[:, 0])
                    if unit:
                        if tg == 0:
                            linear(q, p, codes, sc_gu[:, m + 2], UNIT)
                        else:
                            product(q, p, 2 * tg - 1, UNIT)
                        product(q, p, 2 * tg, UNIT)

            with dve.Fori(0, 3) as i:
                mlp_tile(2 * i, 0, True, True, codesZ)
                mlp_tile(2 * i + 1, 1, True, True, codesZ)
            mlp_tile(6, 0, True, True, codesZ)
            mlp_tile(7, 1, True, True, codesW)
            with dve.Fori(4, 6) as i:
                mlp_tile(2 * i, 0, True, True, codesW)
                mlp_tile(2 * i + 1, 1, True, True, codesW)
            mlp_tile(12, 0, False, True, codesW)
            mlp_tile(13, 1, False, False, codesW)

            def residual(b):
                dve.wait_ge(xg_in, 32 * (b + 1))
                for j in range(2):
                    tt = 2 * b + j
                    dve.wait_ge(d_done, TT + tt + 1)
                    dve.scalar_tensor_tensor(z[:, tt], d_bank[j][:, :], 1.0 / (WS * HS), z[:, tt], ALU.mult, ALU.add)\
                        .then_inc(z_evac, 1)
                    dve.wait_ge(z_evac, TT + tt + 1)
                    dve.tensor_tensor(z[:, tt], z[:, tt], gateA[:, :], ALU.mult).then_inc(y_step, 1)
                    dve.wait_ge(y_step, tt + 1)
                    dve.tensor_tensor(z[:, tt], z[:, tt], xr[:, j], ALU.add).then_inc(x2_done, 1)
                dve.wait_ge(x2_done, 2 * b + 2)
                src = z[:, bass.ds(2 * b, 2)]
                ln_statistics(NB + b, src)
                dve.wait_ge(ln_T, NB + b)
                ln_normalise(NB + b, src, xn2)

            def ffn_out(e):
                dve.wait_ge(ffn_T, e + 1)
                dve.tensor_copy(F_d[:, e], ffn_d_bank).then_inc(ffn_d_out, 1)

            for b in range(NB):
                residual(b)
                if b > 0:
                    ffn_out(2 * b - 2)
                    ffn_out(2 * b - 1)

            def output(tg, j):
                w, s = 4 * tg + j, j % 2
                dve.wait_ge(o_done, w + 1)
                wait(dve, out_dma[s], 16 * (2 * tg + j // 2))
                dve.scalar_tensor_tensor(orow[:, s], out_bank[s][:, :], 1.0 / HS, gateB[:, j // 2], ALU.mult, ALU.mult)\
                    .then_inc(o_mul, 1)
                dve.wait_ge(o_mul, w + 1)
                dve.tensor_tensor(orow[:, s], orow[:, s], z[:, w], ALU.add).then_inc(out_ready, 1)

            def group(tg):
                with dve.Fori(0, MT // 2) as i:
                    for s in range(2):
                        hidden_mul(4 * MT + tg * MT + 2 * i + s, s, HS)
                dve.wait_ge(gateb_in, 32 * (tg + 1))
                for j in range(4):
                    output(tg, j)

            group(0)
            with dve.Fori(1, TG) as tg:
                group(tg)

        @block.tensor
        def _(pe):
            pe.wait_ge(ident_ready, 4)
            pe.wait_ge(silu_c, 1)
            for k in range(KT):
                last = pe.transpose(bank[7][:, k * NB:(k + 1) * NB], crow[0:NB, k * P:(k + 1) * P], identF[0:NB, 0:NB])
            last.then_inc(cs_T, 1)
            pe.wait_ge(bst_ready, 1)
            pe.wait_ge(bst_hi, 2)
            t0 = 0
            for g, n in enumerate([8, 8, 8, 6, 8, 6, 4]):
                for t in range(n):
                    last = pe.transpose(bank[g][0:96, t * 64:(t + 1) * 64].bitcast(f16), Bst[:, t0 + t], ident)
                last.then_inc(lora_T, 1)
                t0 += n
            pe.wait_ge(lora_out, 7)

            def mod_rows(n):
                pe.wait_ge(wmod_in[n % 2], 16 * (n // 2 + 1))
                if n >= 2:
                    pe.wait_ge(row_done, n - 1)
                for k in range(KT):
                    last = pe.matmul(ln_bank[n % 2][0:NB, :], csT[:, k], wm[:, n % 2, k], start=(k == 0), stop=(k == 3))
                last.then_inc(mod_done, 1)

            def three_passes(dst, lhs, rhs, first, end):
                pe.matmul(dst, lhs[0], rhs[0], start=first, stop=False)
                pe.matmul(dst, lhs[0], rhs[1], start=False, stop=False)
                return pe.matmul(dst, lhs[1], rhs[0], start=False, stop=end)

            def prep(j, bk, blocks):
                wait(pe, prep_evac, j - 1)
                for c, (cols, rowf, colf) in enumerate(blocks):
                    dst = bk[:, c * P:(c + 1) * P]
                    pe.matmul(dst, nat[:, 0, cols], ident, start=True, stop=False)
                    pe.matmul(dst, nat[:, 1, cols], ident, start=False, stop=False)
                    last = pe.matmul(dst, rowf, colf, start=False, stop=True)
                last.then_inc(prep_done, 1)

            def prep_wo(q, t, ot):
                prep(ot, prep_bank[ot % 2],
                     [(slice(t * H + o * P, t * H + (o + 1) * P), A_at[0:96, 3 * H + o * P:3 * H + (o + 1) * P],
                       B_at[0:96, 3 * H + ot * P:3 * H + (ot + 1) * P]) for o in range(4)])

            def prep_qkv(ot):
                bk = prep_bank[ot % 2]
                pe.wait_ge(nat_lo, 3 + ot)
                pe.wait_ge(prep_evac, 3 + ot)
                for m in range(3):
                    pe.matmul(bk[:, :], ident, nat[:, 0, m * H:(m + 1) * H], start=(m == 0), stop=False)
                    pe.matmul(bk[:, :], ident, nat[:, 1, m * H:(m + 1) * H], start=False, stop=False)
                    last = pe.matmul(bk[:, :], B_at[0:96, m * H + ot * P:m * H + (ot + 1) * P],
                                     A_at[0:96, m * H:(m + 1) * H], start=False, stop=(m == 2))
                last.then_inc(prep_done, 1)

            def fold(ot):
                pe.wait_ge(prep_evac, 5 + ot)
                for ht in range(KT):
                    cols = slice(ht * P, (ht + 1) * P)
                    last = three_passes(fold_bank[ht][:, :], [qkvS[:, ot % 2, 0, cols], qkvS[:, ot % 2, 1, cols]],
                                        [WoT[:, 0, ot], WoT[:, 1, ot]], ot == 0, ot == 3)
                if ot == 3:
                    last.then_inc(fold_done, 1)

            def ln_transpose(L, src):
                pe.wait_ge(ln_xn, L + 1)
                wait(pe, ln_mod, L)
                for k in range(KT):
                    for j in range(2):
                        at = (k % 2) * SEQ + j * P
                        last = pe.transpose(ln_bank[k // 2][:, at:at + P], src[:, j, k * P:(k + 1) * P], identF)
                last.then_inc(ln_T, 1)

            pe.wait_ge(cs_ready, 1)
            mod_rows(0)
            mod_rows(1)
            pe.wait_ge(a_ready, 1)
            pe.wait_ge(nat_lo, 1)
            for t in range(2):
                prep_wo(0, t, t)
            mod_rows(2)
            mod_rows(3)
            prep_wo(0, 2, 2)
            pe.wait_ge(row_done, 4)
            for c, j in enumerate([0, 1, 3, 4]):
                for k in range(KT):
                    at = (4 * c + k) * NB
                    last = pe.transpose(bank[3][:, at:at + NB], rows[0:NB, j, k * P:(k + 1) * P], identF[0:NB, 0:NB])
            last.then_inc(modT_T, 1)
            pe.wait_ge(nat_lo, 2)
            prep_wo(1, 0, 3)
            mod_rows(4)
            mod_rows(5)
            pe.wait_ge(row_done, 6)
            for ot in range(4):
                ln_transpose(2 * ot, xin[:, (2 * ot) % 4])
                ln_transpose(2 * ot + 1, xin[:, (2 * ot + 1) % 4])
                prep_qkv(ot)
                if ot == 0:
                    pe.wait_ge(modT_ready, 1)
                fold(ot)

            def prep_mlp(m, p, t):
                j = J0 + 3 * m + t
                if t == 0:
                    pe.wait_ge(nat_lo, Q0 + m + 1)
                lm = loraM[:, m]
                if t < 2:
                    blocks = [(slice(t * H + k * P, t * H + (k + 1) * P),
                               A_gu[0:96, t * H + k * P:t * H + (k + 1) * P], lm[0:96, t * P:(t + 1) * P])
                              for k in range(KT)]
                else:
                    blocks = [(slice(2 * H + o * P, 2 * H + (o + 1) * P), lm[0:96, 256:384],
                               B_dn[0:96, o * P:(o + 1) * P]) for o in range(4)]
                prep(j, prep_bank[(p + t) % 2], blocks)

            pe.wait_ge(m_lo, KT)
            for tg in range(TG):
                pe.wait_ge(ln_lo, 2 * tg + 2)
                for k in range(KT):
                    wait(pe, x1_lo, 4 * tg + k - 1)
                    for h in range(KT):
                        cols = slice(k * P, (k + 1) * P)
                        last = three_passes(bank[k % 2][:, :].rearrange("p (t n) -> p t n", t=4),
                                            [M1T[:, h, 0, cols], M1T[:, h, 1, cols]],
                                            [hT[:, 4 * tg:4 * tg + 4, 0, h], hT[:, 4 * tg:4 * tg + 4, 1, h]],
                                            h == 0, h == 3)
                    last.then_inc(x1_done, 1)
                    if tg == 3 and k < 3:
                        prep_mlp(0, 0, k)

            def mlp_tile(m, p, prep_next):
                pe.wait_ge(prep_evac, J0 + 3 * m + 2)
                for tg in range(TG):
                    n, s = 4 * m + tg, tg % 2
                    for g, bk, done in ((0, gate_bank[s], g_done), (1, up_bank[s], u_done)):
                        if g == 0:
                            wait(pe, hid_mul, n - 1)
                        for k in range(KT):
                            cols = slice(k * P, (k + 1) * P)
                            last = three_passes(bk[:, :].rearrange("p (t n) -> p t n", t=4),
                                                [WT[:, p, g, 0, cols], WT[:, p, g, 1, cols]],
                                                [x1T[:, 4 * tg:4 * tg + 4, 0, k], x1T[:, 4 * tg:4 * tg + 4, 1, k]],
                                                k == 0, k == 3)
                        last.then_inc(done, 1)
                    if prep_next and tg < 3:
                        prep_mlp(m + 1, 1 - p, tg)

            def down(b, half):
                for j in range(2):
                    tt = 2 * b + j
                    wait(pe, z_evac, half * TT + tt - 1)
                    toks = bass.ds(b * SEQ + j * P, P)
                    for s in range(HALF):
                        if s == HALF - 1:
                            pe.wait_ge(hid_lo, 4 * HALF * (half + 1))
                            pe.wait_ge(prep_evac, J0 + 3 * HALF * (half + 1))
                        last = three_passes(d_bank[j][:, :], [hid[:, s, 0, toks], hid[:, s, 1, toks]],
                                            [WdT[:, half * HALF + s, 0], WdT[:, half * HALF + s, 1]],
                                            s == 0, s == HALF - 1)
                        if half == 0 and s == 0:
                            for k in range(KT):
                                for a in range(2):
                                    pe.matmul(d_bank[j][:, k * P:(k + 1) * P], x1T[:, tt, a, k], identS,
                                              start=False, stop=False)
                    last.then_inc(d_done, 1)

            pe.wait_ge(x1_lo, TT)
            mlp_tile(0, 0, True)
            mlp_tile(1, 1, True)
            with pe.Fori(1, 3) as i:
                mlp_tile(2 * i, 0, True)
                mlp_tile(2 * i + 1, 1, True)
            mlp_tile(6, 0, True)
            pe.wait_ge(hid_mul, 4 * HALF)
            pe.wait_ge(hid_lo, 4 * (HALF - 1))
            down(0, 0)
            with pe.Fori(1, NB) as b:
                down(b, 0)
            pe.wait_ge(z_evac, TT)
            mlp_tile(7, 1, True)
            with pe.Fori(4, 6) as i:
                mlp_tile(2 * i, 0, True)
                mlp_tile(2 * i + 1, 1, True)
            mlp_tile(12, 0, True)
            mlp_tile(13, 1, False)

            def ffn_prep(e, s):
                pe.wait_ge(ffn_in[s], 24 * (e - s) + 48)
                wait(pe, ffn_gu_out, e)
                wait(pe, ffn_d_out, e)
                for c in range(8):
                    pe.transpose(ffn_gu_bank[:, c * P:(c + 1) * P], ffn_nat[:, s, c * P:(c + 1) * P], ident)
                for c in range(4):
                    last = pe.transpose(ffn_d_bank[:, c * P:(c + 1) * P],
                                        ffn_nat[:, s, 2 * H + c * P:2 * H + (c + 1) * P], ident)
                last.then_inc(ffn_T, 1)

            pe.wait_ge(hid_mul, 4 * MT)
            pe.wait_ge(hid_lo, 4 * MT - 4)
            down(0, 1)
            down(1, 1)
            ln_transpose(NB, xn2)
            ffn_prep(0, 0)
            ffn_prep(1, 1)
            with pe.Fori(2, NB) as b:
                down(b, 1)
                ln_transpose(NB + b - 1, xn2)
                ffn_prep(2 * b - 2, 0)
                ffn_prep(2 * b - 1, 1)
            ln_transpose(2 * NB - 1, xn2)
            pe.wait_ge(ffn_gu_out, MT)
            pe.wait_ge(ffn_d_out, MT)
            pe.wait_ge(z_evac, 2 * TT)

            def group(tg):
                with pe.Fori(0, MT // 2) as i:
                    for s in range(2):
                        n = 4 * MT + tg * MT + 2 * i + s
                        if s == 0:
                            pe.wait_ge(ln_lo, NB + 2 * tg + 2)
                        pe.wait_ge(hid_mul, n - 1)
                        for g, bk, done in ((0, gate_bank[s], g_done), (1, up_bank[s], u_done)):
                            for k in range(KT):
                                for a in range(2):
                                    last = pe.matmul(bk[:, :].rearrange("p (t n) -> p t n", t=4),
                                                     F_gu[:, 2 * i + s, g, k * P:(k + 1) * P],
                                                     h2T[:, bass.ds(4 * tg, 4), a, k],
                                                     start=(k == 0 and a == 0), stop=(k == 3 and a == 1))
                            last.then_inc(done, 1)
                for j in range(4):
                    w = 4 * tg + j
                    wait(pe, o_mul, w - 1)
                    for m in range(MT):
                        if j == 0 and m == 0:
                            pe.wait_ge(hid_lo, 4 * MT + MT * tg + MT - 2)
                        if j == 0 and m == MT - 2:
                            pe.wait_ge(hid_lo, 4 * MT + MT * tg + MT)
                        for a in range(2):
                            last = pe.matmul(out_bank[j % 2][:, :], hid2[:, m, a, j * P:(j + 1) * P], F_d[:, m],
                                             start=(m == 0 and a == 0), stop=(m == MT - 1 and a == 1))
                    last.then_inc(o_done, 1)

            group(0)
            with pe.Fori(1, TG) as tg:
                group(tg)


_INPUTS = ["L0_attn_x", "L0_attn_codes_attn", "L0_attn_scales_attn", "L0_attn_codes_gu", "L0_attn_scales_gu",
           "L0_attn_codes_down", "L0_attn_scales_down", "L0_attn_lora_A_h", "L0_attn_lora_A_down",
           "L0_attn_lora_B_attn", "L0_attn_lora_B_gu", "L0_attn_lora_B_down",
           "L0_ffn_W_gate", "L0_ffn_W_up", "L0_ffn_W_down", "L0_c", "L0_wmod"]


def kernel(**inputs):
    import numpy as _np
    import concourse.bacc as _bacc
    from concourse import mybir as _mybir
    from concourse.bass_utils import run_bass_kernel_spmd as _run

    nc = _bacc.Bacc("TRN2", target_bir_lowering=False, num_devices=1)
    arrays, args = {}, []
    for name in _INPUTS:
        a = _np.ascontiguousarray(inputs[name])
        arrays[f"in_{name}"] = a
        args.append(nc.dram_tensor(f"in_{name}", a.shape, _mybir.dt.from_np(a.dtype), kind="ExternalInput").ap())
    gates = nc.dram_tensor("gates", (2, NB, H), _mybir.dt.float32, kind="Internal").ap()
    res = nc.dram_tensor("out", (NB, SEQ, H), _mybir.dt.float32, kind="ExternalOutput").ap()
    adaln_kernel(nc, *args, gates, res)
    r = _run(nc, [arrays], core_ids=[0])
    return r.results[0]["out"]
```

```python
import concourse.bass as bass
from concourse import mybir
from contextlib import ExitStack

P = 128
NB, SEQ, H, I, R = 8, 256, 512, 1792, 16
T = NB * SEQ
KT = H // P
MT = I // P
TG, GT = 4, 512
TT = T // P
BLOCK = 64
UNIT = 12 * P
HALF = MT // 2
EPS = 1e-5

SHIFT = [-0.035814154893159866, -3.722414255142212, -0.4697154462337494, -3.2984719276428223,
         -1.0957497358322144, -2.6926143169403076, -1.9447404146194458]
OFFSET = [0.011445658281445503, 0.013174708932638168, 0.15736202895641327, 0.17014329135417938,
          0.338535875082016, 0.3751530349254608, 0.3761288821697235]
LEAD = 0.0039697647687094795
NF = len(SHIFT)

WS = 256.0
MS = 64.0
HS = 1.0 / 16.0


def adaln_kernel(nc, x, codes_attn, scales_attn, codes_gu, scales_gu, codes_down, scales_down,
                 lora_A_h, lora_A_down, lora_B_attn, lora_B_gu, lora_B_down,
                 W_gate, W_up, W_down, cond, wmod, gates_dram, out):
    f32, f16, i32 = mybir.dt.float32, mybir.dt.float16, mybir.dt.int32
    ALU = mybir.AluOpType
    ACT = mybir.ActivationFunctionType
    x_rows = x.rearrange("b s h -> (b s) h")
    out_rows = out.rearrange("b s h -> (b s) h")

    ctx = ExitStack()
    with ctx:
        def sb(name, nbytes):
            return ctx.enter_context(nc.sbuf_tensor(name, [P, nbytes // 4], f32))

        def view(region, at, dt, n):
            size = 2 if dt == f16 else 4
            v = region[:, at // 4:(at + n * size) // 4]
            return v if dt == f32 else v.bitcast(dt)

        def sem(name):
            return ctx.enter_context(nc.semaphore(name))

        HID = sb("hidden_region", HALF * 2 * T * 2)
        X1 = sb("x1_region", TT * 2 * KT * P * 2)
        Z = sb("z_region", TT * H * 4)
        WD = sb("down_weights_region", MT * 2 * H * 2)
        DQ = sb("dequant_region", 5 * UNIT * 4)
        NAT = sb("natural_region", 2 * UNIT * 2)
        WTR = sb("weights_region", 2 * 2 * 2 * H * 2)
        SR = sb("scratch_region", 8192)
        LSH = sb("lora_shared_region", (2 * H + H) * 2)
        CST = sb("constants_region", 512 + 256 + 256 + 512 + 1344 + 192)

        identF = view(CST, 0, f32, P)
        ident = view(CST, 512, f16, P)
        identS = view(CST, 768, f16, P)
        modT = view(CST, 1024, f32, NB * 16).rearrange("p (b c) -> p b c", b=NB)
        sc_gu = view(CST, 1536, f32, MT * 24).rearrange("p (m s) -> p m s", m=MT)
        small = view(CST, 2880, f32, 48)
        stats = small[:, 0:24].rearrange("p (t s) -> p t s", t=4)
        moments = small[:, 24:32].rearrange("p (t s) -> p t s", t=4)
        varpe, rstd, minus_half = small[:, 32:36], small[:, 36:40], small[:, 40:44]

        def acts(region):
            return view(region, 0, f16, TT * 2 * KT * P).rearrange("p (t a k n) -> p t a k n", t=TT, a=2, k=KT)
        hT, x1T, h2T = acts(HID), acts(X1), acts(X1)
        z = view(Z, 0, f32, TT * H).rearrange("p (t n) -> p t n", t=TT)
        hid = view(HID, 0, f16, HALF * 2 * T).rearrange("p (m a n) -> p m a n", m=HALF, a=2)
        hid2 = view(HID, 0, f16, MT * 2 * GT).rearrange("p (m a n) -> p m a n", m=MT, a=2)
        WdT = view(WD, 0, f16, MT * 2 * H).rearrange("p (m a n) -> p m a n", m=MT, a=2)
        loraM = view(WD, 0, f16, MT * 1024).rearrange("p (m n) -> p m n", m=MT)
        WT = view(WTR, 0, f16, 2 * 2 * 2 * H).rearrange("p (s g a n) -> p s g a n", s=2, g=2, a=2)
        sq = view(DQ, 0, f32, 3 * UNIT).rearrange("p (s n) -> p s n", s=3)
        acc = view(DQ, 3 * UNIT * 4, f32, 2 * UNIT).rearrange("p (s n) -> p s n", s=2)
        nat = view(NAT, 0, f16, 2 * UNIT).rearrange("p (a n) -> p a n", a=2)
        srow = view(SR, 0, f32, 2 * GT).rearrange("p (s n) -> p s n", s=2)
        A_gu = view(LSH, 0, f16, 2 * H)
        B_dn = view(LSH, 2 * H * 2, f16, H)
        codesZ = view(Z, 0, i32, 2 * UNIT).rearrange("p (s n) -> p s n", s=2)
        codesW = view(WD, 0, i32, 2 * UNIT).rearrange("p (s n) -> p s n", s=2)

        xin = view(Z, 2 * UNIT * 4, f32, 4 * 2 * H).rearrange("p (s j n) -> p s j n", s=4, j=2)
        hmod1 = view(Z, 2 * UNIT * 4 + 4 * 4096, f32, 2 * H).rearrange("p (k n) -> p k n", k=KT)
        WoT = view(HID, 32768, f16, 2 * 4 * H).rearrange("p (a o n) -> p a o n", a=2, o=4)
        M1T = view(HID, 40960, f16, 4 * 2 * H).rearrange("p (k a n) -> p k a n", k=4, a=2)
        qkvS = view(HID, 49152, f16, 2 * 2 * H).rearrange("p (s a n) -> p s a n", s=2, a=2)
        raw_sa = view(HID, 53248, f32, 128).rearrange("p (m t s) -> p m t s", m=4, t=4)
        raw_sg = view(HID, 53760, f32, 224).rearrange("p (g m s) -> p g m s", g=2, m=MT)
        raw_sd = view(HID, 54656, f32, 112).rearrange("p (t m s) -> p t m s", t=4, m=MT)
        sc_o = view(HID, 55104, f32, 32)
        sc_q = view(HID, 55232, f32, 96).rearrange("p (t m s) -> p t m s", t=4, m=3)
        rawA = view(HID, 0, f32, 6 * H + I)
        rawB = view(HID, 19456, f32, 48 * R).rearrange("p (t r) -> p t r", t=48)
        Bst = view(HID, 22528, f16, 48 * 96).rearrange("p (t c) -> p t c", t=48)
        A_at = view(WTR, 0, f16, 4 * H)
        B_at = view(WTR, 4096, f16, 4 * H)
        wm = view(X1, 0, f32, 2 * 4 * H).rearrange("p (s k n) -> p s k n", s=2, k=4)
        rows = view(X1, 16384, f32, 6 * H).rearrange("p (j n) -> p j n", j=6)
        clamp = view(X1, 28672, f32, 2 * H).rearrange("p (s n) -> p s n", s=2)
        crow = view(SR, 4096, f32, H)
        csT = view(SR, 6144, f32, 4 * NB).rearrange("p (k b) -> p k b", k=4)
        mrow = srow

        xr = view(WTR, 0, f32, 2 * H).rearrange("p (j n) -> p j n", j=2)
        gateA = view(WTR, 4096, f32, H)
        xn2 = view(SR, 0, f32, 2 * H).rearrange("p (j n) -> p j n", j=2)
        hmod2 = view(SR, 4096, f32, 2 * H).rearrange("p (k n) -> p k n", k=KT)
        ffn_nat = view(NAT, 0, f16, 2 * UNIT).rearrange("p (s n) -> p s n", s=2)
        F_gu = view(DQ, 0, f16, MT * 2 * H).rearrange("p (m g n) -> p m g n", m=MT, g=2)
        F_d = view(WD, 0, f16, MT * H).rearrange("p (m n) -> p m n", m=MT)
        orow = view(WTR, 0, f32, 2 * H).rearrange("p (s n) -> p s n", s=2)
        gateB = view(WTR, 4096, f32, 2 * H).rearrange("p (s n) -> p s n", s=2)

        bank = [ctx.enter_context(nc.psum_tensor(f"bank{i}", [P, 512], f32)) for i in range(8)]
        gate_bank, up_bank, prep_bank, out_bank = bank[0:2], bank[2:4], bank[4:6], bank[4:6]
        d_bank, ln_bank, fold_bank = bank[0:2], bank[6:8], bank[0:4]
        ffn_gu_bank = bank[2][:, :].bitcast(f16)
        ffn_d_bank = bank[3][:, 0:256].bitcast(f16)

        stack_clear, ident_ready, lora_b_in, lora_a_in, scales_in, cond_in = map(
            sem, ["stack_clear", "ident_ready", "lora_b_in", "lora_a_in", "scales_in", "cond_in"])
        bst_hi, bst_ready, lora_T, lora_out, a_hi, a_ready, scales_ready, scales_mlp_in = map(
            sem, ["bst_hi", "bst_ready", "lora_T", "lora_out", "a_hi", "a_ready", "scales_ready", "scales_mlp_in"])
        silu_c, cs_T, cs_ready, mod_done, row_done, modT_T, modT_ready, clamp_step, gates_out = map(
            sem, ["silu_c", "cs_T", "cs_ready", "mod_done", "row_done", "modT_T", "modT_ready",
                  "clamp_step", "gates_out"])
        wmod_in = [sem("wmod_in0"), sem("wmod_in1")]
        codes_in = [sem("codes_in0"), sem("codes_in1")]
        x_in = [sem(f"x_in{s}") for s in range(4)]
        sq_ready, lin_done, sq_used, chain, nat_hi, nat_lo = map(
            sem, ["sq_ready", "lin_done", "sq_used", "chain", "nat_hi", "nat_lo"])
        prep_done, prep_hi, prep_evac = map(sem, ["prep_done", "prep_hi", "prep_evac"])
        fold_done, m_step, m_hi, m_lo = map(sem, ["fold_done", "m_step", "m_hi", "m_lo"])
        ln_stat, ln_var, ln_rstd, ln_xn, ln_T, ln_mod, ln_hi, ln_lo = map(
            sem, ["ln_stat", "ln_var", "ln_rstd", "ln_xn", "ln_T", "ln_mod", "ln_hi", "ln_lo"])
        x1_done, x1_hi, x1_lo = map(sem, ["x1_done", "x1_hi", "x1_lo"])
        g_done, u_done, silu_done, hid_mul, hid_hi, hid_lo = map(
            sem, ["g_done", "u_done", "silu_done", "hid_mul", "hid_hi", "hid_lo"])
        d_done, z_evac, y_step, x2_done, xg_in = map(
            sem, ["d_done", "z_evac", "y_step", "x2_done", "xg_in"])
        ffn_in = [sem("ffn_in0"), sem("ffn_in1")]
        ffn_T, ffn_gu_out, ffn_d_out = map(sem, ["ffn_T", "ffn_gu_out", "ffn_d_out"])
        gateb_in, o_done, o_mul, out_ready = map(sem, ["gateb_in", "o_done", "o_mul", "out_ready"])
        out_dma = [sem("out_dma0"), sem("out_dma1")]

        def wait(eng, s, value):
            if isinstance(value, int) and value <= 0:
                return
            eng.wait_ge(s, value)

        Q0, J0 = 6, 8

        block = ctx.enter_context(nc.Block())

        @block.sync
        def _(sp):
            def load_x(b):
                if b >= 4:
                    sp.wait_ge(ln_T, b - 3)
                sp.dma_start(xin[:, b % 4], x_rows[b * SEQ:(b + 1) * SEQ].rearrange("(j p) n -> p j n", p=P))\
                    .then_inc(x_in[b % 4], 16)

            def slot_free(q):
                wait(sp, sq_ready, 7 * (q - 1))
                wait(sp, lin_done, q - 1)

            def load_attn(q):
                slot_free(q)
                if q == 0:
                    src = codes_attn[3, 0:3 * P].rearrange("(t p) n -> p t n", p=P)
                elif q == 1:
                    src = codes_attn[3, 3 * P:4 * P].rearrange("(t p) n -> p t n", p=P)
                else:
                    src = codes_attn[0:3, (q - 2) * P:(q - 1) * P].rearrange("m p n -> p m n")
                n = 1 if q == 1 else 3
                sp.dma_start(codesZ[:, q % 2, 0:n * H].rearrange("p (t n) -> p t n", t=n), src)\
                    .then_inc(codes_in[q % 2], 16)

            def load_mlp(m, p, codes, first):
                if first:
                    sp.wait_ge(d_done, TT)
                else:
                    slot_free(Q0 + m)
                sp.dma_start(codes[:, p, 0:2 * H].rearrange("p (g n) -> p g n", g=2),
                             codes_gu[:, bass.ds(m * P, P)].rearrange("g p n -> p g n"))\
                    .then_inc(codes_in[p], 16)
                sp.dma_start(codes[:, p, 2 * H:3 * H].rearrange("p (t n) -> p t n", t=4),
                             codes_down[:, bass.ds(m * P, P)].rearrange("(t p) n -> p t n", p=P))\
                    .then_inc(codes_in[p], 16)

            def load_wmod(n, j):
                if n >= 2:
                    sp.wait_ge(mod_done, n - 1)
                sp.dma_start(wm[:, n % 2], wmod[:, j * H:(j + 1) * H].rearrange("(k p) n -> p k n", p=P))\
                    .then_inc(wmod_in[n % 2], 16)

            sp.dma_start(raw_sa, scales_attn.rearrange("m (t p) s -> p m t s", p=P)).then_inc(scales_in, 16)
            load_attn(0)
            load_wmod(0, 0)
            load_x(0)
            load_x(1)
            load_attn(1)
            load_wmod(1, 1)
            load_wmod(2, 3)
            load_attn(2)
            load_wmod(3, 4)
            load_wmod(4, 2)
            load_attn(3)
            load_wmod(5, 5)
            sp.dma_start(raw_sg, scales_gu.rearrange("g (m p) s -> p g m s", p=P)).then_inc(scales_mlp_in, 16)
            sp.dma_start(raw_sd.rearrange("p t m s -> p t (m s)"),
                         scales_down.rearrange("(t p) s -> p t s", p=P)).then_inc(scales_mlp_in, 16)
            load_x(2)
            load_x(3)
            load_attn(4)
            sp.wait_ge(clamp_step, 8)
            sp.dma_start(gates_dram[0], rows[0:NB, 2]).then_inc(gates_out, 16)
            sp.dma_start(gates_dram[1], rows[0:NB, 5]).then_inc(gates_out, 16)
            load_attn(5)
            load_x(4)
            load_x(5)
            load_mlp(0, 0, codesZ, False)
            load_mlp(1, 1, codesZ, False)
            load_x(6)
            load_x(7)
            with sp.Fori(1, 4) as i:
                load_mlp(2 * i, 0, codesZ, False)
                load_mlp(2 * i + 1, 1, codesZ, False)
            load_mlp(8, 0, codesZ, False)
            load_mlp(9, 1, codesW, True)
            load_mlp(10, 0, codesW, True)
            load_mlp(11, 1, codesW, False)
            load_mlp(12, 0, codesW, False)
            load_mlp(13, 1, codesW, False)

            def load_residual(b):
                wait(sp, x2_done, 2 * b)
                sp.dma_start(xr[:, :, :], x_rows[bass.ds(b * SEQ, SEQ)].rearrange("(j p) n -> p j n", p=P))\
                    .then_inc(xg_in, 16)
                sp.dma_start(gateA[:, :], gates_dram[0, bass.ds(b, 1)].partition_broadcast(P)
                             .rearrange("p a n -> p (a n)")).then_inc(xg_in, 16)

            sp.wait_ge(gates_out, 32)
            sp.wait_ge(u_done, 4 * MT)
            load_residual(0)
            with sp.Fori(1, NB) as b:
                load_residual(b)

            def load_gate(tg):
                for s in range(2):
                    sp.dma_start(gateB[:, s], gates_dram[1, bass.ds(2 * tg + s, 1)].partition_broadcast(P)
                                 .rearrange("p a n -> p (a n)")).then_inc(gateb_in, 16)

            def store(tg):
                for j in range(4):
                    sp.wait_ge(out_ready, 4 * tg + j + 1)
                    sp.dma_start(out_rows[bass.ds(tg * GT + j * P, P)], orow[:, j % 2]).then_inc(out_dma[j % 2], 16)

            sp.wait_ge(x2_done, TT)
            load_gate(0)
            with sp.Fori(0, 3) as tg:
                store(tg)
                load_gate(tg + 1)
            store(3)
            sp.wait_ge(out_dma[0], 16 * TT // 2)
            sp.wait_ge(out_dma[1], 16 * TT // 2)

        @block.gpsimd
        def _(pool):
            pool.memset(minus_half, -0.5)
            pool.memset(identF, 0.0).then_inc(ident_ready, 1)
            pool.wait_ge(ident_ready, 1)
            pool.affine_select(out=identF, in_=identF, compare_op=ALU.not_equal, fill=1.0, base=0,
                               pattern=[[-1, P]], channel_multiplier=1).then_inc(ident_ready, 1)

            def low_a(dst, src):
                pool.tensor_tensor(dst, src, dst, ALU.subtract).then_inc(a_ready, 1)

            def ln_power(c, n):
                pool.wait_ge(ln_var, c + 1)
                pool.tensor_tensor(rstd[:, 0:n], varpe[:, 0:n], minus_half[:, 0:n], ALU.pow).then_inc(ln_rstd, 1)

            def ln_low(L, b, dst, hmod):
                pool.wait_ge(ln_hi, L + 1)
                view4 = dst[:, bass.ds(2 * b, 2)].rearrange("p j a k n -> p a k j n")
                pool.tensor_tensor(view4[:, 1], hmod.rearrange("p k (j n) -> p k j n", j=2), view4[:, 0],
                                   ALU.subtract).then_inc(ln_lo, 1)

            def natural_low(q, p, n):
                pool.wait_ge(nat_hi, q + 1)
                t = n // 3 if n == UNIT else 0
                for c in range(3):
                    part = slice(c * t, (c + 1) * t) if t else slice(c * P, n if c == 2 else (c + 1) * P)
                    pool.tensor_tensor(nat[:, 1, part], acc[:, p, part], nat[:, 0, part], ALU.subtract)\
                        .then_inc(nat_lo, 1)

            def hidden_low(n, s, dst):
                pool.wait_ge(hid_hi, n + 1)
                pool.tensor_tensor(dst[:, 1], srow[:, s], dst[:, 0], ALU.subtract).then_inc(hid_lo, 1)

            def mlp_tile(m, p, slot, finish):
                for tg in range(TG):
                    hidden_low(4 * m + tg, tg % 2, hid[:, slot, :, tg * GT:(tg + 1) * GT])
                    if finish and tg == 0:
                        natural_low(Q0 + m + 1, 1 - p, UNIT)

            grp = slice(32, 48)
            ln_power(0, 4)
            pool.wait_ge(ln_rstd, 1)
            pool.wait_ge(a_hi, 3)
            low_a(A_at[grp], rawA[grp, 0:4 * H])
            pool.wait_ge(a_ready, 1)
            natural_low(0, 0, UNIT)
            pool.wait_ge(nat_lo, 3)
            low_a(A_gu[grp], rawA[grp, 4 * H:6 * H])
            low_a(loraM[grp, :, 256:384], rawA[grp, 6 * H:].rearrange("p (m n) -> p m n", m=MT))
            pool.wait_ge(a_ready, 3)
            natural_low(1, 1, H)
            ln_low(0, 0, hT, hmod1)
            natural_low(2, 0, UNIT)
            ln_low(1, 1, hT, hmod1)
            for ot in range(1, 4):
                natural_low(2 + ot, ot % 2, UNIT)
                if ot == 3:
                    ln_power(1, 4)
            ln_low(2, 2, hT, hmod1)
            ln_low(3, 3, hT, hmod1)
            ln_power(2, 4)
            ln_low(4, 4, hT, hmod1)
            ln_power(3, 4)
            ln_low(5, 5, hT, hmod1)
            ln_low(6, 6, hT, hmod1)
            ln_low(7, 7, hT, hmod1)
            natural_low(Q0, 0, UNIT)
            with pool.Fori(0, 3) as i:
                mlp_tile(2 * i, 0, 2 * i, True)
                mlp_tile(2 * i + 1, 1, 2 * i + 1, True)
            mlp_tile(6, 0, 6, True)
            mlp_tile(7, 1, 0, True)
            with pool.Fori(4, 6) as i:
                mlp_tile(2 * i, 0, 2 * i - HALF, True)
                mlp_tile(2 * i + 1, 1, 2 * i + 1 - HALF, True)
            mlp_tile(12, 0, 5, True)
            mlp_tile(13, 1, 6, False)

            ln_power(4, 2)
            with pool.Fori(1, NB) as b:
                ln_power(4 + b, 2)
                ln_low(NB + b - 1, b - 1, h2T, hmod2)
            ln_low(2 * NB - 1, NB - 1, h2T, hmod2)
            with pool.Fori(0, TG) as tg:
                with pool.Fori(0, MT // 2) as i:
                    for s in range(2):
                        hidden_low(4 * MT + tg * MT + 2 * i + s, s, hid2[:, 2 * i + s])

        @block.scalar
        def _(act):
            act.dma_start(crow[0:NB], cond).then_inc(cond_in, 16)
            act.dma_start(rawB[:, 0:16].rearrange("p (m t) r -> p m t r", m=4),
                          lora_B_attn.rearrange("m (t p) r -> p m t r", p=P)).then_inc(lora_b_in, 16)
            for m in range(6):
                act.dma_start(rawA[0:96, m * H:(m + 1) * H], lora_A_h[m].unsqueeze(0).broadcast_to([6, R, H]))\
                    .then_inc(lora_a_in, 16)
            act.dma_start(rawB[:, 16:44].rearrange("p (g t) r -> p g t r", g=2),
                          lora_B_gu.rearrange("g (t p) r -> p g t r", p=P)).then_inc(lora_b_in, 16)
            act.dma_start(rawB[:, 44:48], lora_B_down.rearrange("(t p) r -> p t r", p=P)).then_inc(lora_b_in, 16)
            act.dma_start(rawA[0:96, 6 * H:6 * H + I], lora_A_down.unsqueeze(0).broadcast_to([6, R, I]))\
                .then_inc(lora_a_in, 16)

            act.wait_ge(ident_ready, 2)
            act.activation(ident, identF, ACT.Copy).then_inc(ident_ready, 1)
            act.activation(identS, identF, ACT.Copy, scale=WS * HS).then_inc(ident_ready, 1)
            act.wait_ge(cond_in, 16)
            act.activation(crow[0:NB], crow[0:NB], ACT.Silu).then_inc(silu_c, 1)
            def square(q, p, i, codes, n):
                if i == 0:
                    wait(act, sq_used, NF * q)
                elif i >= 3:
                    act.wait_ge(sq_used, NF * q + i - 2)
                act.activation(sq[:, i % 3, 0:n], codes[:, p, 0:n], ACT.Square, bias=SHIFT[i], scale=0.25)\
                    .then_inc(sq_ready, 1)

            def natural_high(q, p, n):
                act.wait_ge(sq_used, NF * (q + 1))
                wait(act, prep_done, (J0 + 3 * (q - Q0)) if not isinstance(q, int) or q >= Q0
                     else [0, 3, 4, 5, 6, 7][q])
                act.activation(nat[:, 0, 0:n], acc[:, p, 0:n], ACT.Copy).then_inc(nat_hi, 1)

            def stack(g, bk, n, dst):
                act.wait_ge(lora_T, g + 1)
                act.activation(dst, bk[0:96, 0:n * 64].bitcast(f16).rearrange("p (t n) -> p t n", t=n),
                               ACT.Copy).then_inc(lora_out, 1)

            def prep_high(j, bk, dst, src=None):
                act.wait_ge(prep_done, j + 1)
                act.activation(dst, bk[:, :] if src is None else src(bk), ACT.Copy).then_inc(prep_hi, 1)

            def ln_modulate(L, b, kind, dst, hmod):
                act.wait_ge(ln_T, L + 1)
                wait(act, ln_lo, L)
                for k in range(KT):
                    last = act.activation(hmod[:, k], ln_bank[k // 2][:, (k % 2) * SEQ:(k % 2 + 1) * SEQ],
                                          ACT.Identity,
                                          scale=modT[:, bass.ds(b, 1), kind + 4 + k],
                                          bias=modT[:, bass.ds(b, 1), kind + k])
                last.then_inc(ln_mod, 1)
                act.wait_ge(ln_mod, L + 1)
                view4 = dst[:, bass.ds(2 * b, 2)].rearrange("p j a k n -> p a k j n")
                act.activation(view4[:, 0], hmod.rearrange("p k (j n) -> p k j n", j=2), ACT.Copy).then_inc(ln_hi, 1)

            def silu(n, s):
                act.wait_ge(g_done, n + 1)
                wait(act, hid_lo, n - 1)
                return act.activation(srow[:, s], gate_bank[s][:, :], ACT.Silu,
                                      scale=1.0 / WS)

            def hidden_high(n, s, dst):
                act.wait_ge(hid_mul, n + 1)
                act.activation(dst[:, 0], srow[:, s], ACT.Copy).then_inc(hid_hi, 1)

            act.wait_ge(codes_in[0], 16)
            for i in range(NF):
                square(0, 0, i, codesZ, UNIT)
                if i == 1:
                    act.wait_ge(lora_b_in, 48)
                    act.wait_ge(stack_clear, 1)
                    act.activation(Bst[:, :, 0:R], rawB[:, :, :], ACT.Copy, scale=WS).then_inc(bst_hi, 1)
                if i == 2:
                    act.activation(Bst[:, :, 32:32 + R], rawB[:, :, :], ACT.Copy, scale=WS).then_inc(bst_hi, 1)
            stack(0, bank[0], 8, B_at[0:96, 0:1024].rearrange("p (t n) -> p t n", t=8))
            stack(1, bank[1], 8, B_at[0:96, 1024:2048].rearrange("p (t n) -> p t n", t=8))
            act.wait_ge(codes_in[1], 16)
            square(1, 1, 0, codesZ, H)
            natural_high(0, 0, UNIT)
            for i in range(1, NF):
                square(1, 1, i, codesZ, H)
            act.wait_ge(codes_in[0], 16 * 2)
            square(2, 0, 0, codesZ, UNIT)
            for t in range(3):
                prep_high(t, prep_bank[t % 2], WoT[:, 0, :, t * P:(t + 1) * P],
                          lambda bk: bk[:, :].rearrange("p (o n) -> p o n", o=4))
            natural_high(1, 1, H)
            for ot in range(4):
                p = ot % 2
                if ot > 0:
                    act.wait_ge(codes_in[p], 16 * (ot // 2 + 2))
                for i in range(1 if ot == 0 else 0, NF):
                    square(2 + ot, p, i, codesZ, UNIT)
                    if ot > 0 and i == 0:
                        natural_high(1 + ot, 1 - p, UNIT)
                    if ot == 1 and i == 1:
                        ln_modulate(1, 1, 0, hT, hmod1)
                    if i == 3 and ot == 0:
                        prep_high(3, prep_bank[1], WoT[:, 0, :, 3 * P:4 * P],
                                  lambda bk: bk[:, :].rearrange("p (o n) -> p o n", o=4))
                    elif i == 3:
                        prep_high(3 + ot, prep_bank[1 - p], qkvS[:, 1 - p, 0])
                if ot == 0:
                    act.wait_ge(modT_ready, 1)
                    ln_modulate(0, 0, 0, hT, hmod1)
                if ot == 1:
                    stack(2, bank[6], 8, loraM[0:96, 0:8, 0:128])
                    stack(3, bank[7], 6, loraM[0:96, 8:14, 0:128])
                if ot == 2:
                    stack(4, bank[6], 8, loraM[0:96, 0:8, 128:256])
                    stack(5, bank[7], 6, loraM[0:96, 8:14, 128:256])
                if ot == 3:
                    stack(6, bank[6], 4, B_dn[0:96].rearrange("p (t n) -> p t n", t=4))
            natural_high(5, 1, UNIT)
            prep_high(7, prep_bank[1], qkvS[:, 1, 0])
            for ht in range(KT):
                act.wait_ge(m_step, ht + 1)
                act.activation(M1T[:, ht, 0], mrow[:, ht % 2], ACT.Copy).then_inc(m_hi, 1)
            ln_modulate(2, 2, 0, hT, hmod1)
            ln_modulate(3, 3, 0, hT, hmod1)

            act.wait_ge(gates_out, 32)

            def x1_high(tg, k):
                act.wait_ge(x1_done, 4 * tg + k + 1)
                act.activation(x1T[:, 4 * tg:4 * tg + 4, 0, k], bank[k % 2][:, :].rearrange("p (t n) -> p t n", t=4),
                               ACT.Copy, scale=1.0 / MS).then_inc(x1_hi, 1)

            Q1 = Q0 + 1
            x1_high(0, 0)
            act.wait_ge(codes_in[0], 48 + 32)
            square(Q0, 0, 0, codesZ, UNIT)
            x1_high(0, 1)
            square(Q0, 0, 1, codesZ, UNIT)
            x1_high(0, 2)
            square(Q0, 0, 2, codesZ, UNIT)
            x1_high(0, 3)
            ln_modulate(4, 4, 0, hT, hmod1)
            x1_high(1, 0)
            square(Q0, 0, 3, codesZ, UNIT)
            x1_high(1, 1)
            ln_modulate(5, 5, 0, hT, hmod1)
            x1_high(1, 2)
            square(Q0, 0, 4, codesZ, UNIT)
            x1_high(1, 3)
            ln_modulate(6, 6, 0, hT, hmod1)
            x1_high(2, 0)
            square(Q0, 0, 5, codesZ, UNIT)
            x1_high(2, 1)
            ln_modulate(7, 7, 0, hT, hmod1)
            x1_high(2, 2)
            square(Q0, 0, 6, codesZ, UNIT)
            x1_high(2, 3)
            natural_high(Q0, 0, UNIT)
            x1_high(3, 0)
            act.wait_ge(codes_in[1], 48 + 32)
            square(Q1, 1, 0, codesZ, UNIT)
            x1_high(3, 1)
            square(Q1, 1, 1, codesZ, UNIT)
            x1_high(3, 2)
            prep_high(J0, prep_bank[0], WT[:, 0, 0, 0])
            square(Q1, 1, 2, codesZ, UNIT)
            x1_high(3, 3)
            prep_high(J0 + 1, prep_bank[1], WT[:, 0, 1, 0])
            square(Q1, 1, 3, codesZ, UNIT)
            prep_high(J0 + 2, prep_bank[0], WdT[:, 0, 0])
            for i in range(4, NF):
                square(Q1, 1, i, codesZ, UNIT)

            def mlp_tile(m, p, slot, finish, start, codes):
                q, j = Q0 + m + 2, J0 + 3 * (m + 1)
                for tg in range(TG):
                    n, s = 4 * m + tg, tg % 2
                    silu(n, s).then_inc(silu_done, 1)
                    if start and tg > 0:
                        square(q, p, [None, 1, 2, 4][tg], codes, UNIT)
                    hidden_high(n, s, hid[:, slot, :, tg * GT:(tg + 1) * GT])
                    if tg == 0:
                        if finish:
                            natural_high(q - 1, 1 - p, UNIT)
                        if start:
                            act.wait_ge(codes_in[p], 48 + 32 * (m // 2 + 2) if isinstance(m, int)
                                        else 48 + 16 * (m - p) + 64)
                            square(q, p, 0, codes, UNIT)
                    if tg == 1 and finish:
                        prep_high(j, prep_bank[1 - p], WT[:, 1 - p, 0, 0])
                    if tg == 2:
                        if finish:
                            prep_high(j + 1, prep_bank[p], WT[:, 1 - p, 1, 0])
                        if start:
                            square(q, p, 3, codes, UNIT)
                        if finish:
                            prep_high(j + 2, prep_bank[1 - p], WdT[:, m + 1, 0])
                    if tg == 3 and start:
                        square(q, p, 5, codes, UNIT)
                        square(q, p, 6, codes, UNIT)

            mlp_tile(0, 0, 0, True, True, codesZ)
            mlp_tile(1, 1, 1, True, True, codesZ)
            with act.Fori(1, 3) as i:
                mlp_tile(2 * i, 0, 2 * i, True, True, codesZ)
                mlp_tile(2 * i + 1, 1, 2 * i + 1, True, True, codesZ)
            mlp_tile(6, 0, 6, True, True, codesZ)
            act.wait_ge(sq_ready, NF * (Q0 + 9))
            act.wait_ge(lin_done, Q0 + 9)
            with act.Fori(0, NB) as b:
                for j in range(2):
                    act.wait_ge(d_done, 2 * b + j + 1)
                    act.activation(z[:, 2 * b + j], d_bank[j][:, :], ACT.Copy, scale=1.0 / (WS * HS))\
                        .then_inc(z_evac, 1)
            mlp_tile(7, 1, 0, True, True, codesW)
            with act.Fori(4, 6) as i:
                mlp_tile(2 * i, 0, 2 * i - HALF, True, True, codesW)
                mlp_tile(2 * i + 1, 1, 2 * i + 1 - HALF, True, True, codesW)
            mlp_tile(12, 0, 5, True, False, codesW)
            mlp_tile(13, 1, 6, False, False, codesW)

            def load_ffn(e, s):
                row = bass.ds(e * P, P)
                act.dma_start(ffn_nat[:, s, 0:H], W_gate[row]).then_inc(ffn_in[s], 16)
                act.dma_start(ffn_nat[:, s, H:2 * H], W_up[row]).then_inc(ffn_in[s], 16)
                act.dma_start(ffn_nat[:, s, 2 * H:3 * H].rearrange("p (t n) -> p t n", t=4),
                              W_down[:, row].rearrange("(t p) n -> p t n", p=P)).then_inc(ffn_in[s], 16)

            def ffn_out(e, s, more):
                act.wait_ge(ffn_T, e + 1)
                if more:
                    load_ffn(e + 2, s)
                act.activation(F_gu[:, e].rearrange("p g n -> p (g n)"), ffn_gu_bank, ACT.Copy).then_inc(ffn_gu_out, 1)

            act.wait_ge(prep_done, J0 + 3 * MT)
            load_ffn(0, 0)
            load_ffn(1, 1)
            with act.Fori(1, NB - 1) as b:
                ffn_out(2 * b - 2, 0, True)
                ffn_out(2 * b - 1, 1, True)
                ln_modulate(NB + b - 1, b - 1, 8, h2T, hmod2)
            ffn_out(MT - 2, 0, False)
            ffn_out(MT - 1, 1, False)
            for b in (NB - 2, NB - 1):
                ln_modulate(NB + b, b, 8, h2T, hmod2)

            with act.Fori(0, TG) as tg:
                with act.Fori(0, MT // 2) as i:
                    for s in range(2):
                        n = 4 * MT + tg * MT + 2 * i + s
                        act.wait_ge(g_done, n + 1)
                        act.wait_ge(hid_lo, n - 1)
                        act.activation(srow[:, s], gate_bank[s][:, :], ACT.Silu).then_inc(silu_done, 1)
                        hidden_high(n, s, hid2[:, 2 * i + s])

        @block.vector
        def _(dve):
            dve.memset(Bst[:, :, :], 0.0).then_inc(stack_clear, 1)
            K = LEAD * WS
            dve.wait_ge(scales_in, 16)
            dve.tensor_scalar(sc_o.rearrange("p (t s) -> p t s", t=4), raw_sa[:, 3], K, None, ALU.mult)
            dve.tensor_scalar(sc_q.rearrange("p t m s -> p m t s"), raw_sa[:, 0:3], K, None, ALU.mult)\
                .then_inc(scales_ready, 1)
            def linear(q, p, codes, scale, n):
                wait(dve, nat_lo, 3 * (q - 1))
                dve.scalar_tensor_tensor(acc[:, p, 0:n].rearrange("p (s c) -> p s c", c=BLOCK),
                                         codes[:, p, 0:n].rearrange("p (s c) -> p s c", c=BLOCK), -7.0,
                                         scale.unsqueeze(2).broadcast_to([P, n // BLOCK, BLOCK]),
                                         ALU.add, ALU.mult).then_inc(lin_done, 1)
                dve.wait_ge(lin_done, q + 1)

            def product(q, p, i, n):
                dve.wait_ge(sq_ready, NF * q + i + 1)
                if i > 0:
                    dve.wait_ge(sq_used, NF * q + i)
                dve.scalar_tensor_tensor(acc[:, p, 0:n], sq[:, i % 3, 0:n], OFFSET[i], acc[:, p, 0:n],
                                         ALU.add, ALU.mult).then_inc(sq_used, 1)

            def prep_low(j, bk, dst, hi, src=None):
                dve.wait_ge(prep_hi, j + 1)
                dve.tensor_tensor(dst, bk[:, :] if src is None else src(bk), hi, ALU.subtract).then_inc(prep_evac, 1)

            def ln_statistics(c, tiles):
                n = len(tiles)
                for t in range(n):
                    last = dve.bn_stats(stats[:, t], tiles[t])
                last.then_inc(ln_stat, 1)
                dve.wait_ge(ln_stat, 2 * c + 1)
                for t in range(n):
                    last = dve.bn_aggr(moments[:, t], stats[:, t])
                last.then_inc(ln_stat, 1)
                dve.wait_ge(ln_stat, 2 * c + 2)
                dve.tensor_scalar(varpe[:, 0:n], moments[:, 0:n, 1], EPS, None, ALU.add).then_inc(ln_var, 1)

            def ln_normalise(c, L, tiles, dst):
                dve.wait_ge(ln_rstd, c + 1)
                for t in range(len(tiles)):
                    last = dve.tensor_scalar(dst[t], tiles[t], moments[:, t, 0:1], rstd[:, t:t + 1],
                                             ALU.subtract, ALU.mult)
                    if t % 2:
                        last.then_inc(ln_xn, 1)
                dve.wait_ge(ln_xn, L + len(tiles) // 2)

            def x_tiles(c):
                return [xin[:, (2 * c + t // 2) % 4, t % 2] for t in range(4)]

            def ln_first(c):
                for b in (2 * c, 2 * c + 1):
                    dve.wait_ge(x_in[b % 4], 16 * (b // 4 + 1))
                ln_statistics(c, x_tiles(c))

            def mod_row(n, j):
                dve.wait_ge(mod_done, n + 1)
                src = ln_bank[n % 2][0:NB, :]
                if j in (1, 4):
                    dve.tensor_scalar(rows[0:NB, j], src, 1.0, None, ALU.add).then_inc(row_done, 1)
                else:
                    dve.tensor_copy(rows[0:NB, j], src).then_inc(row_done, 1)

            def clamp_gate(c, j):
                g = rows[0:NB, j]
                dve.tensor_scalar(clamp[0:NB, 0], g, 0.0, 2.0, ALU.is_ge, ALU.mult).then_inc(clamp_step, 1)
                dve.scalar_tensor_tensor(clamp[0:NB, 1], g, -1.0, g, ALU.mult, ALU.max).then_inc(clamp_step, 1)
                dve.wait_ge(clamp_step, 4 * c + 2)
                dve.tensor_scalar(clamp[0:NB, 1], clamp[0:NB, 1], 0.25, None, ALU.max).then_inc(clamp_step, 1)
                dve.wait_ge(clamp_step, 4 * c + 3)
                dve.scalar_tensor_tensor(g, clamp[0:NB, 0], -1.0, clamp[0:NB, 1], ALU.add, ALU.mult)\
                    .then_inc(clamp_step, 1)
                dve.wait_ge(clamp_step, 4 * c + 4)

            wo_view = lambda bk: bk[:, :].rearrange("p (o n) -> p o n", o=4)
            dve.wait_ge(scales_ready, 1)
            dve.wait_ge(codes_in[0], 16)
            linear(0, 0, codesZ, sc_o[:, 0:24], UNIT)
            product(0, 0, 0, UNIT)
            dve.wait_ge(cs_T, 1)
            dve.tensor_copy(csT.rearrange("p k b -> p (k b)"), bank[7][:, 0:4 * NB]).then_inc(cs_ready, 1)
            product(0, 0, 1, UNIT)
            dve.wait_ge(lora_a_in, 16 * 7)
            dve.tensor_copy(A_at[0:96], rawA[0:96, 0:4 * H]).then_inc(a_hi, 1)
            dve.tensor_copy(A_gu[0:96], rawA[0:96, 4 * H:6 * H]).then_inc(a_hi, 1)
            dve.tensor_copy(loraM[0:96, :, 256:384], rawA[0:96, 6 * H:].rearrange("p (m n) -> p m n", m=MT))\
                .then_inc(a_hi, 1)
            dve.wait_ge(bst_hi, 1)
            dve.scalar_tensor_tensor(Bst[:, :, 64:64 + R], rawB[:, :, :], WS, Bst[:, :, 0:R], ALU.mult, ALU.subtract)\
                .then_inc(bst_ready, 1)
            product(0, 0, 2, UNIT)
            ln_first(0)
            product(0, 0, 3, UNIT)
            ln_normalise(0, 0, x_tiles(0), x_tiles(0))
            mod_row(0, 0)
            product(0, 0, 4, UNIT)
            product(0, 0, 5, UNIT)
            mod_row(1, 1)
            product(0, 0, 6, UNIT)
            dve.wait_ge(codes_in[1], 16)
            linear(1, 1, codesZ, sc_o[:, 24:32], H)
            for i in range(NF):
                product(1, 1, i, H)
            mod_row(2, 3)
            dve.wait_ge(codes_in[0], 16 * 2)
            linear(2, 0, codesZ, sc_q[:, 0].rearrange("p m s -> p (m s)"), UNIT)
            for t in range(3):
                prep_low(t, prep_bank[t % 2], WoT[:, 1, :, t * P:(t + 1) * P], WoT[:, 0, :, t * P:(t + 1) * P], wo_view)
            for ot in range(4):
                p = ot % 2
                if ot > 0:
                    dve.wait_ge(codes_in[p], 16 * (ot // 2 + 2))
                    linear(2 + ot, p, codesZ, sc_q[:, ot].rearrange("p m s -> p (m s)"), UNIT)
                for i in range(NF):
                    product(2 + ot, p, i, UNIT)
                    if i == 1 and ot == 0:
                        mod_row(3, 4)
                    if i == 4 and ot == 0:
                        mod_row(4, 2)
                    if i == 5 and ot == 0:
                        mod_row(5, 5)
                    if i == 5 and ot == 0:
                        dve.wait_ge(modT_T, 1)
                        dve.tensor_copy(modT, bank[3][:, 0:NB * 16].rearrange("p (c b) -> p b c", b=NB))\
                            .then_inc(modT_ready, 1)
                    if i == 3 and ot == 0:
                        prep_low(3, prep_bank[1], WoT[:, 1, :, 3 * P:4 * P], WoT[:, 0, :, 3 * P:4 * P], wo_view)
                    elif i == 3:
                        prep_low(3 + ot, prep_bank[1 - p], qkvS[:, 1 - p, 1], qkvS[:, 1 - p, 0])
                if ot == 1:
                    dve.wait_ge(row_done, 6)
                    clamp_gate(0, 2)
                    clamp_gate(1, 5)
            ln_first(1)
            dve.wait_ge(scales_mlp_in, 32)
            dve.tensor_scalar(sc_gu[:, :, 0:16].rearrange("p m (g s) -> p g m s", g=2), raw_sg, K, None, ALU.mult)
            dve.tensor_scalar(sc_gu[:, :, 16:24].rearrange("p m (t s) -> p t m s", t=4), raw_sd, K, None,
                              ALU.mult).then_inc(scales_ready, 1)
            ln_normalise(1, 2, x_tiles(1), x_tiles(1))
            prep_low(7, prep_bank[1], qkvS[:, 1, 1], qkvS[:, 1, 0])

            for ht in range(KT):
                dve.wait_ge(fold_done, 1)
                if ht >= 2:
                    dve.wait_ge(m_lo, ht - 1)
                dve.tensor_scalar(mrow[:, ht % 2], fold_bank[ht][:, :], MS / (3.0 * WS * WS), None, ALU.mult)\
                    .then_inc(chain, 1)
                dve.wait_ge(chain, ht + 1)
                blk = mrow[:, ht % 2, ht * P:(ht + 1) * P]
                dve.scalar_tensor_tensor(blk, identF, MS, blk, ALU.mult, ALU.add).then_inc(m_step, 1)
                dve.wait_ge(m_hi, ht + 1)
                dve.tensor_tensor(M1T[:, ht, 1], mrow[:, ht % 2], M1T[:, ht, 0], ALU.subtract).then_inc(m_lo, 1)

            def x1_low(tg, k):
                dve.wait_ge(x1_hi, 4 * tg + k + 1)
                dve.scalar_tensor_tensor(x1T[:, 4 * tg:4 * tg + 4, 1, k],
                                         bank[k % 2][:, :].rearrange("p (t n) -> p t n", t=4), 1.0 / MS,
                                         x1T[:, 4 * tg:4 * tg + 4, 0, k], ALU.mult, ALU.subtract).then_inc(x1_lo, 1)

            Q1 = Q0 + 1
            dve.wait_ge(scales_ready, 2)
            for tg in range(2):
                x1_low(tg, 0)
                ln_first(2 + tg)
                x1_low(tg, 1)
                ln_normalise(2 + tg, 4 + 2 * tg, x_tiles(2 + tg), x_tiles(2 + tg))
                x1_low(tg, 2)
                if tg == 0:
                    dve.wait_ge(codes_in[0], 48 + 32)
                    linear(Q0, 0, codesZ, sc_gu[:, 0], UNIT)
                else:
                    product(Q0, 0, 1, UNIT)
                x1_low(tg, 3)
                product(Q0, 0, 2 * tg, UNIT)
            for k in range(KT):
                x1_low(2, k)
                product(Q0, 0, 3 + k, UNIT)
            x1_low(3, 0)
            dve.wait_ge(codes_in[1], 48 + 32)
            linear(Q1, 1, codesZ, sc_gu[:, 1], UNIT)
            x1_low(3, 1)
            product(Q1, 1, 0, UNIT)
            x1_low(3, 2)
            prep_low(J0, prep_bank[0], WT[:, 0, 0, 1], WT[:, 0, 0, 0])
            product(Q1, 1, 1, UNIT)
            x1_low(3, 3)
            prep_low(J0 + 1, prep_bank[1], WT[:, 0, 1, 1], WT[:, 0, 1, 0])
            product(Q1, 1, 2, UNIT)
            prep_low(J0 + 2, prep_bank[0], WdT[:, 0, 1], WdT[:, 0, 0])
            for i in range(3, 6):
                product(Q1, 1, i, UNIT)

            def hidden_mul(n, s, scale):
                dve.wait_ge(silu_done, n + 1)
                dve.wait_ge(u_done, n + 1)
                dve.scalar_tensor_tensor(srow[:, s], up_bank[s][:, :], scale, srow[:, s], ALU.mult, ALU.mult)\
                    .then_inc(hid_mul, 1)

            def mlp_tile(m, p, finish, start, codes):
                q, j = Q0 + m + 2, J0 + 3 * (m + 1)
                for tg in range(TG):
                    hidden_mul(4 * m + tg, tg % 2, HS / WS)
                    if tg == 0 and finish:
                        product(q - 1, 1 - p, 6, UNIT)
                    if tg == 1:
                        if start:
                            dve.wait_ge(codes_in[p], 48 + 32 * (m // 2 + 2) if isinstance(m, int)
                                        else 48 + 16 * (m - p) + 64)
                            linear(q, p, codes, sc_gu[:, m + 2], UNIT)
                            product(q, p, 0, UNIT)
                        if finish:
                            prep_low(j, prep_bank[1 - p], WT[:, 1 - p, 0, 1], WT[:, 1 - p, 0, 0])
                    if tg == 2:
                        if start:
                            product(q, p, 1, UNIT)
                        if finish:
                            prep_low(j + 1, prep_bank[p], WT[:, 1 - p, 1, 1], WT[:, 1 - p, 1, 0])
                        if start:
                            product(q, p, 2, UNIT)
                        if finish:
                            prep_low(j + 2, prep_bank[1 - p], WdT[:, m + 1, 1], WdT[:, m + 1, 0])
                    if tg == 3 and start:
                        for i in range(3, 6):
                            product(q, p, i, UNIT)

            with dve.Fori(0, 3) as i:
                mlp_tile(2 * i, 0, True, True, codesZ)
                mlp_tile(2 * i + 1, 1, True, True, codesZ)
            mlp_tile(6, 0, True, True, codesZ)
            mlp_tile(7, 1, True, True, codesW)
            with dve.Fori(4, 6) as i:
                mlp_tile(2 * i, 0, True, True, codesW)
                mlp_tile(2 * i + 1, 1, True, True, codesW)
            mlp_tile(12, 0, True, False, codesW)
            mlp_tile(13, 1, False, False, codesW)

            def ffn_out(e):
                dve.wait_ge(ffn_T, e + 1)
                dve.tensor_copy(F_d[:, e], ffn_d_bank).then_inc(ffn_d_out, 1)

            def residual(b):
                if b > 0:
                    ffn_out(2 * b - 2)
                for j in range(2):
                    tt = 2 * b + j
                    dve.wait_ge(d_done, TT + tt + 1)
                    dve.scalar_tensor_tensor(z[:, tt], d_bank[j][:, :], 1.0 / (WS * HS), z[:, tt], ALU.mult, ALU.add)\
                        .then_inc(z_evac, 1)
                    if j == 0:
                        dve.wait_ge(xg_in, 32 * (b + 1))
                    dve.wait_ge(z_evac, TT + tt + 1)
                    dve.tensor_tensor(z[:, tt], z[:, tt], gateA[:, :], ALU.mult).then_inc(y_step, 1)
                    dve.wait_ge(y_step, tt + 1)
                    dve.tensor_tensor(z[:, tt], z[:, tt], xr[:, j], ALU.add).then_inc(x2_done, 1)
                    if j == 0 and b > 0:
                        ffn_out(2 * b - 1)
                dve.wait_ge(x2_done, 2 * b + 2)
                tiles = [z[:, 2 * b], z[:, 2 * b + 1]]
                ln_statistics(4 + b, tiles)
                dve.wait_ge(ln_T, NB + b)
                ln_normalise(4 + b, NB + b, tiles, [xn2[:, 0], xn2[:, 1]])

            for b in range(NB):
                residual(b)

            def output(tg, j):
                w, s = 4 * tg + j, j % 2
                dve.wait_ge(o_done, w + 1)
                wait(dve, out_dma[s], 16 * (2 * tg + j // 2))
                dve.scalar_tensor_tensor(orow[:, s], out_bank[s][:, :], 1.0 / HS, gateB[:, j // 2], ALU.mult, ALU.mult)\
                    .then_inc(o_mul, 1)
                dve.wait_ge(o_mul, w + 1)
                dve.tensor_tensor(orow[:, s], orow[:, s], z[:, w], ALU.add).then_inc(out_ready, 1)

            def group(tg):
                with dve.Fori(0, MT // 2) as i:
                    for s in range(2):
                        hidden_mul(4 * MT + tg * MT + 2 * i + s, s, HS)
                dve.wait_ge(gateb_in, 32 * (tg + 1))
                for j in range(4):
                    output(tg, j)

            group(0)
            with dve.Fori(1, TG) as tg:
                group(tg)

        @block.tensor
        def _(pe):
            pe.wait_ge(ident_ready, 4)
            pe.wait_ge(silu_c, 1)
            for k in range(KT):
                last = pe.transpose(bank[7][:, k * NB:(k + 1) * NB], crow[0:NB, k * P:(k + 1) * P], identF[0:NB, 0:NB])
            last.then_inc(cs_T, 1)

            def lora_transpose(g, bk, t0, n):
                for t in range(n):
                    last = pe.transpose(bk[0:96, t * 64:(t + 1) * 64].bitcast(f16), Bst[:, t0 + t], ident)
                last.then_inc(lora_T, 1)

            def mod_rows(n):
                pe.wait_ge(wmod_in[n % 2], 16 * (n // 2 + 1))
                if n >= 2:
                    pe.wait_ge(row_done, n - 1)
                for k in range(KT):
                    last = pe.matmul(ln_bank[n % 2][0:NB, :], csT[:, k], wm[:, n % 2, k], start=(k == 0), stop=(k == 3))
                last.then_inc(mod_done, 1)

            def three_passes(dst, lhs, rhs, first, end):
                pe.matmul(dst, lhs[0], rhs[0], start=first, stop=False)
                pe.matmul(dst, lhs[0], rhs[1], start=False, stop=False)
                return pe.matmul(dst, lhs[1], rhs[0], start=False, stop=end)

            def prep(j, bk, blocks):
                wait(pe, prep_evac, j - 1)
                for c, (cols, rowf, colf) in enumerate(blocks):
                    dst = bk[:, c * P:(c + 1) * P]
                    pe.matmul(dst, nat[:, 0, cols], ident, start=True, stop=False)
                    pe.matmul(dst, nat[:, 1, cols], ident, start=False, stop=False)
                    last = pe.matmul(dst, rowf, colf, start=False, stop=True)
                last.then_inc(prep_done, 1)

            def prep_wo(q, t, ot):
                prep(ot, prep_bank[ot % 2],
                     [(slice(t * H + o * P, t * H + (o + 1) * P), A_at[0:96, 3 * H + o * P:3 * H + (o + 1) * P],
                       B_at[0:96, 3 * H + ot * P:3 * H + (ot + 1) * P]) for o in range(4)])

            def prep_qkv(ot):
                bk = prep_bank[ot % 2]
                pe.wait_ge(nat_lo, 3 * (3 + ot))
                pe.wait_ge(prep_evac, 3 + ot)
                for m in range(3):
                    pe.matmul(bk[:, :], ident, nat[:, 0, m * H:(m + 1) * H], start=(m == 0), stop=False)
                    pe.matmul(bk[:, :], ident, nat[:, 1, m * H:(m + 1) * H], start=False, stop=False)
                    last = pe.matmul(bk[:, :], B_at[0:96, m * H + ot * P:m * H + (ot + 1) * P],
                                     A_at[0:96, m * H:(m + 1) * H], start=False, stop=(m == 2))
                last.then_inc(prep_done, 1)

            def fold(ot):
                pe.wait_ge(prep_evac, 5 + ot)
                for ht in range(KT):
                    cols = slice(ht * P, (ht + 1) * P)
                    last = three_passes(fold_bank[ht][:, :], [qkvS[:, ot % 2, 0, cols], qkvS[:, ot % 2, 1, cols]],
                                        [WoT[:, 0, ot], WoT[:, 1, ot]], ot == 0, ot == 3)
                if ot == 3:
                    last.then_inc(fold_done, 1)

            def ln_transpose(L, src):
                pe.wait_ge(ln_xn, L + 1)
                wait(pe, ln_mod, L)
                for k in range(KT):
                    for j in range(2):
                        at = (k % 2) * SEQ + j * P
                        last = pe.transpose(ln_bank[k // 2][:, at:at + P], src[:, j, k * P:(k + 1) * P], identF)
                last.then_inc(ln_T, 1)

            pe.wait_ge(bst_ready, 1)
            pe.wait_ge(bst_hi, 2)
            lora_transpose(0, bank[0], 0, 8)
            lora_transpose(1, bank[1], 8, 8)
            pe.wait_ge(cs_ready, 1)
            mod_rows(0)
            mod_rows(1)
            pe.wait_ge(lora_out, 2)
            pe.wait_ge(a_ready, 1)
            pe.wait_ge(nat_lo, 3)
            for t in range(2):
                prep_wo(0, t, t)
            mod_rows(2)
            prep_wo(0, 2, 2)
            pe.wait_ge(nat_lo, 6)
            prep_wo(1, 0, 3)
            mod_rows(3)
            pe.wait_ge(row_done, 4)
            for c, j in enumerate([0, 1, 3, 4]):
                for k in range(KT):
                    at = (4 * c + k) * NB
                    last = pe.transpose(bank[3][:, at:at + NB], rows[0:NB, j, k * P:(k + 1) * P], identF[0:NB, 0:NB])
            last.then_inc(modT_T, 1)
            mod_rows(4)
            mod_rows(5)
            for ot in range(4):
                if ot == 0:
                    pe.wait_ge(row_done, 6)
                    ln_transpose(0, xin[:, 0])
                elif ot == 1:
                    pe.wait_ge(ln_mod, 2)
                    lora_transpose(2, bank[6], 16, 8)
                    lora_transpose(3, bank[7], 24, 6)
                elif ot == 2:
                    pe.wait_ge(lora_out, 4)
                    lora_transpose(4, bank[6], 30, 8)
                    lora_transpose(5, bank[7], 38, 6)
                else:
                    pe.wait_ge(lora_out, 6)
                    lora_transpose(6, bank[6], 44, 4)
                prep_qkv(ot)
                if ot == 0:
                    ln_transpose(1, xin[:, 1])
                    pe.wait_ge(modT_ready, 1)
                fold(ot)
            pe.wait_ge(lora_out, 7)
            ln_transpose(2, xin[:, 2])
            ln_transpose(3, xin[:, 3])

            def prep_mlp(m, p, t):
                j = J0 + 3 * m + t
                pe.wait_ge(nat_lo, 3 * (Q0 + m) + t + 1)
                lm = loraM[:, m]
                if t < 2:
                    blocks = [(slice(t * H + k * P, t * H + (k + 1) * P),
                               A_gu[0:96, t * H + k * P:t * H + (k + 1) * P], lm[0:96, t * P:(t + 1) * P])
                              for k in range(KT)]
                else:
                    blocks = [(slice(2 * H + o * P, 2 * H + (o + 1) * P), lm[0:96, 256:384],
                               B_dn[0:96, o * P:(o + 1) * P]) for o in range(4)]
                prep(j, prep_bank[(p + t) % 2], blocks)

            pe.wait_ge(m_lo, KT)
            for tg in range(TG):
                pe.wait_ge(ln_lo, 2 * tg + 2)
                for k in range(KT):
                    wait(pe, x1_lo, 4 * tg + k - 1)
                    for h in range(KT):
                        cols = slice(k * P, (k + 1) * P)
                        last = three_passes(bank[k % 2][:, :].rearrange("p (t n) -> p t n", t=4),
                                            [M1T[:, h, 0, cols], M1T[:, h, 1, cols]],
                                            [hT[:, 4 * tg:4 * tg + 4, 0, h], hT[:, 4 * tg:4 * tg + 4, 1, h]],
                                            h == 0, h == 3)
                    last.then_inc(x1_done, 1)
                    if tg == 3 and k > 0:
                        prep_mlp(0, 0, k - 1)
                    b = {(0, 2): 4, (1, 0): 5, (1, 2): 6, (2, 0): 7}.get((tg, k))
                    if b:
                        ln_transpose(b, xin[:, b % 4])

            def mlp_tile(m, p, prep_next):
                pe.wait_ge(prep_evac, J0 + 3 * m + 2)
                for tg in range(TG):
                    n, s = 4 * m + tg, tg % 2
                    for g, bk, done in ((0, gate_bank[s], g_done), (1, up_bank[s], u_done)):
                        if g == 0:
                            wait(pe, hid_mul, n - 1)
                        for k in range(KT):
                            cols = slice(k * P, (k + 1) * P)
                            last = three_passes(bk[:, :].rearrange("p (t n) -> p t n", t=4),
                                                [WT[:, p, g, 0, cols], WT[:, p, g, 1, cols]],
                                                [x1T[:, 4 * tg:4 * tg + 4, 0, k], x1T[:, 4 * tg:4 * tg + 4, 1, k]],
                                                k == 0, k == 3)
                        last.then_inc(done, 1)
                        if prep_next and (tg, g) in ((2, 0), (2, 1), (3, 0)):
                            prep_mlp(m + 1, 1 - p, tg - 2 + g if tg == 2 else 2)

            def down(b, j, half):
                tt = 2 * b + j
                wait(pe, z_evac, half * TT + tt - 1)
                toks = bass.ds(b * SEQ + j * P, P)
                for s in range(HALF):
                    if s == HALF - 1:
                        pe.wait_ge(hid_lo, 4 * HALF * (half + 1))
                        pe.wait_ge(prep_evac, J0 + 3 * HALF * (half + 1))
                    last = three_passes(d_bank[j][:, :], [hid[:, s, 0, toks], hid[:, s, 1, toks]],
                                        [WdT[:, half * HALF + s, 0], WdT[:, half * HALF + s, 1]],
                                        s == 0, s == HALF - 1)
                    if half == 0 and s == 0:
                        for k in range(KT):
                            for a in range(2):
                                pe.matmul(d_bank[j][:, k * P:(k + 1) * P], x1T[:, tt, a, k], identS,
                                          start=False, stop=False)
                last.then_inc(d_done, 1)

            pe.wait_ge(x1_lo, TT)
            mlp_tile(0, 0, True)
            mlp_tile(1, 1, True)
            with pe.Fori(1, 3) as i:
                mlp_tile(2 * i, 0, True)
                mlp_tile(2 * i + 1, 1, True)
            mlp_tile(6, 0, True)
            pe.wait_ge(hid_mul, 4 * HALF)
            pe.wait_ge(hid_lo, 4 * (HALF - 1))
            down(0, 0, 0)
            down(0, 1, 0)
            with pe.Fori(1, NB) as b:
                down(b, 0, 0)
                down(b, 1, 0)
            pe.wait_ge(z_evac, TT)
            mlp_tile(7, 1, True)
            with pe.Fori(4, 6) as i:
                mlp_tile(2 * i, 0, True)
                mlp_tile(2 * i + 1, 1, True)
            mlp_tile(12, 0, True)
            mlp_tile(13, 1, False)

            def ffn_prep(e, s):
                pe.wait_ge(ffn_in[s], 24 * (e - s) + 48)
                wait(pe, ffn_gu_out, e)
                wait(pe, ffn_d_out, e)
                for c in range(8):
                    pe.transpose(ffn_gu_bank[:, c * P:(c + 1) * P], ffn_nat[:, s, c * P:(c + 1) * P], ident)
                for c in range(4):
                    last = pe.transpose(ffn_d_bank[:, c * P:(c + 1) * P],
                                        ffn_nat[:, s, 2 * H + c * P:2 * H + (c + 1) * P], ident)
                last.then_inc(ffn_T, 1)

            pe.wait_ge(hid_mul, 4 * MT)
            pe.wait_ge(hid_lo, 4 * MT - 4)
            down(0, 0, 1)
            down(0, 1, 1)

            def down_and_more(b):
                ffn_prep(2 * b - 2, 0)
                down(b, 0, 1)
                ffn_prep(2 * b - 1, 1)
                down(b, 1, 1)
                ln_transpose(NB + b - 1, xn2)

            down_and_more(1)
            with pe.Fori(2, NB) as b:
                down_and_more(b)
            ln_transpose(2 * NB - 1, xn2)
            pe.wait_ge(ffn_gu_out, MT)
            pe.wait_ge(ffn_d_out, MT)
            pe.wait_ge(z_evac, 2 * TT)

            def group(tg):
                with pe.Fori(0, MT // 2) as i:
                    for s in range(2):
                        n = 4 * MT + tg * MT + 2 * i + s
                        if s == 0:
                            pe.wait_ge(ln_lo, NB + 2 * tg + 2)
                        pe.wait_ge(hid_mul, n - 1)
                        for g, bk, done in ((0, gate_bank[s], g_done), (1, up_bank[s], u_done)):
                            for k in range(KT):
                                for a in range(2):
                                    last = pe.matmul(bk[:, :].rearrange("p (t n) -> p t n", t=4),
                                                     F_gu[:, 2 * i + s, g, k * P:(k + 1) * P],
                                                     h2T[:, bass.ds(4 * tg, 4), a, k],
                                                     start=(k == 0 and a == 0), stop=(k == 3 and a == 1))
                            last.then_inc(done, 1)
                for j in range(4):
                    w = 4 * tg + j
                    wait(pe, o_mul, w - 1)
                    for m in range(MT):
                        if j == 0 and m == 0:
                            pe.wait_ge(hid_lo, 4 * MT + MT * tg + MT - 2)
                        if j == 0 and m == MT - 2:
                            pe.wait_ge(hid_lo, 4 * MT + MT * tg + MT)
                        for a in range(2):
                            last = pe.matmul(out_bank[j % 2][:, :], hid2[:, m, a, j * P:(j + 1) * P], F_d[:, m],
                                             start=(m == 0 and a == 0), stop=(m == MT - 1 and a == 1))
                    last.then_inc(o_done, 1)

            group(0)
            with pe.Fori(1, TG) as tg:
                group(tg)


_INPUTS = ["L0_attn_x", "L0_attn_codes_attn", "L0_attn_scales_attn", "L0_attn_codes_gu", "L0_attn_scales_gu",
           "L0_attn_codes_down", "L0_attn_scales_down", "L0_attn_lora_A_h", "L0_attn_lora_A_down",
           "L0_attn_lora_B_attn", "L0_attn_lora_B_gu", "L0_attn_lora_B_down",
           "L0_ffn_W_gate", "L0_ffn_W_up", "L0_ffn_W_down", "L0_c", "L0_wmod"]


def kernel(**inputs):
    import numpy as _np
    import concourse.bacc as _bacc
    from concourse import mybir as _mybir
    from concourse.bass_utils import run_bass_kernel_spmd as _run

    nc = _bacc.Bacc("TRN2", target_bir_lowering=False, num_devices=1)
    arrays, args = {}, []
    for name in _INPUTS:
        a = _np.ascontiguousarray(inputs[name])
        arrays[f"in_{name}"] = a
        args.append(nc.dram_tensor(f"in_{name}", a.shape, _mybir.dt.from_np(a.dtype), kind="ExternalInput").ap())
    gates = nc.dram_tensor("gates", (2, NB, H), _mybir.dt.float32, kind="Internal").ap()
    res = nc.dram_tensor("out", (NB, SEQ, H), _mybir.dt.float32, kind="ExternalOutput").ap()
    adaln_kernel(nc, *args, gates, res)
    r = _run(nc, [arrays], core_ids=[0])
    return r.results[0]["out"]
```

```python
import concourse.bass as bass
from concourse import mybir
from contextlib import ExitStack

P = 128
NB, SEQ, H, I, R = 8, 256, 512, 1792, 16
T = NB * SEQ
KT = H // P
MT = I // P
TG, GT = 4, 512
TT = T // P
BLOCK = 64
UNIT = 12 * P
HALF = MT // 2
EPS = 1e-5

SHIFT = [-0.035814154893159866, -3.722414255142212, -0.4697154462337494, -3.2984719276428223,
         -1.0957497358322144, -2.6926143169403076, -1.9447404146194458]
OFFSET = [0.011445658281445503, 0.013174708932638168, 0.15736202895641327, 0.17014329135417938,
          0.338535875082016, 0.3751530349254608, 0.3761288821697235]
LEAD = 0.0039697647687094795
NF = len(SHIFT)

WS = 256.0
MS = 64.0
HS = 1.0 / 16.0


def adaln_kernel(nc, x, codes_attn, scales_attn, codes_gu, scales_gu, codes_down, scales_down,
                 lora_A_h, lora_A_down, lora_B_attn, lora_B_gu, lora_B_down,
                 W_gate, W_up, W_down, cond, wmod, gates_dram, out):
    f32, f16, i32 = mybir.dt.float32, mybir.dt.float16, mybir.dt.int32
    ALU = mybir.AluOpType
    ACT = mybir.ActivationFunctionType
    x_rows = x.rearrange("b s h -> (b s) h")
    out_rows = out.rearrange("b s h -> (b s) h")

    ctx = ExitStack()
    with ctx:
        def sb(name, nbytes):
            return ctx.enter_context(nc.sbuf_tensor(name, [P, nbytes // 4], f32))

        def view(region, at, dt, n):
            size = 2 if dt == f16 else 4
            v = region[:, at // 4:(at + n * size) // 4]
            return v if dt == f32 else v.bitcast(dt)

        def sem(name):
            return ctx.enter_context(nc.semaphore(name))

        HID = sb("hidden_region", HALF * 2 * T * 2)
        X1 = sb("x1_region", TT * 2 * KT * P * 2)
        Z = sb("z_region", TT * H * 4)
        WD = sb("down_weights_region", MT * 2 * H * 2)
        DQ = sb("dequant_region", 5 * UNIT * 4)
        NAT = sb("natural_region", 2 * UNIT * 2)
        WTR = sb("weights_region", 2 * 2 * 2 * H * 2)
        SR = sb("scratch_region", 8192)
        LSH = sb("lora_shared_region", (2 * H + H) * 2)
        CST = sb("constants_region", 512 + 3 * 256 + 512 + 1344 + 224)

        identF = view(CST, 0, f32, P)
        ident = view(CST, 512, f16, P)
        identS = view(CST, 768, f16, P)
        identK = view(CST, 1024, f16, P)
        modT = view(CST, 1280, f32, NB * 16).rearrange("p (b c) -> p b c", b=NB)
        sc_gu = view(CST, 1792, f32, MT * 24).rearrange("p (m s) -> p m s", m=MT)
        small = view(CST, 3136, f32, 56)
        stats = small[:, 0:24].rearrange("p (t s) -> p t s", t=4)
        moments = small[:, 24:32].rearrange("p (t s) -> p t s", t=4)
        varpe, rstd, minus_half, offset0 = small[:, 32:36], small[:, 36:40], small[:, 40:44], small[:, 44:45]

        def acts(region):
            return view(region, 0, f16, TT * 2 * KT * P).rearrange("p (t a k n) -> p t a k n", t=TT, a=2, k=KT)
        hT, x1T, h2T = acts(HID), acts(X1), acts(X1)
        z = view(Z, 0, f32, TT * H).rearrange("p (t n) -> p t n", t=TT)
        hid = view(HID, 0, f16, HALF * 2 * T).rearrange("p (m a n) -> p m a n", m=HALF, a=2)
        hid2 = view(HID, 0, f16, MT * 2 * GT).rearrange("p (m a n) -> p m a n", m=MT, a=2)
        WdT = view(WD, 0, f16, MT * 2 * H).rearrange("p (m a n) -> p m a n", m=MT, a=2)
        loraM = view(WD, 0, f16, MT * 1024).rearrange("p (m n) -> p m n", m=MT)
        WT = view(WTR, 0, f16, 2 * 2 * 2 * H).rearrange("p (s g a n) -> p s g a n", s=2, g=2, a=2)
        sq = view(DQ, 0, f32, 3 * UNIT).rearrange("p (s n) -> p s n", s=3)
        acc = view(DQ, 3 * UNIT * 4, f32, 2 * UNIT).rearrange("p (s n) -> p s n", s=2)
        nat = view(NAT, 0, f16, 2 * UNIT).rearrange("p (a n) -> p a n", a=2)
        hidden_row = view(SR, 0, f32, 2 * GT).rearrange("p (s n) -> p s n", s=2)
        A_gu = view(LSH, 0, f16, 2 * H)
        B_dn = view(LSH, 2 * H * 2, f16, H)
        codesZ = view(Z, 0, i32, 2 * UNIT).rearrange("p (s n) -> p s n", s=2)
        codesW = view(WD, 0, i32, 2 * UNIT).rearrange("p (s n) -> p s n", s=2)

        xin = view(Z, 2 * UNIT * 4, f32, 4 * 2 * H).rearrange("p (s j n) -> p s j n", s=4, j=2)
        hmod1 = view(Z, 2 * UNIT * 4 + 4 * 4096, f32, 2 * H).rearrange("p (k n) -> p k n", k=KT)
        WoT = view(HID, 32768, f16, 2 * 4 * H).rearrange("p (a o n) -> p a o n", a=2, o=4)
        M1T = view(HID, 40960, f16, 4 * 2 * H).rearrange("p (k a n) -> p k a n", k=4, a=2)
        qkvS = view(HID, 49152, f16, 2 * 2 * H).rearrange("p (s a n) -> p s a n", s=2, a=2)
        raw_sa = view(HID, 53248, f32, 128).rearrange("p (m t s) -> p m t s", m=4, t=4)
        raw_sg = view(HID, 53760, f32, 224).rearrange("p (g m s) -> p g m s", g=2, m=MT)
        raw_sd = view(HID, 54656, f32, 112).rearrange("p (t m s) -> p t m s", t=4, m=MT)
        sc_o = view(HID, 55104, f32, 32)
        sc_q = view(HID, 55232, f32, 96).rearrange("p (t m s) -> p t m s", t=4, m=3)
        rawA = view(HID, 0, f32, 6 * H + I)
        rawB = view(HID, 19456, f32, 48 * R).rearrange("p (t r) -> p t r", t=48)
        Bst = view(HID, 22528, f16, 48 * 96).rearrange("p (t c) -> p t c", t=48)
        A_at = view(WTR, 0, f16, 4 * H)
        B_at = view(WTR, 4096, f16, 4 * H)
        wm = view(X1, 0, f32, 2 * 4 * H).rearrange("p (s k n) -> p s k n", s=2, k=4)
        rows = view(SR, 0, f32, 2 * H).rearrange("p (j n) -> p j n", j=2)
        clamp = view(SR, 4096, f32, 2 * H).rearrange("p (s n) -> p s n", s=2)
        crow = view(SR, 4096, f32, H)
        csT = view(SR, 6144, f32, 4 * NB).rearrange("p (k b) -> p k b", k=4)

        xr = view(WTR, 0, f32, 2 * H).rearrange("p (j n) -> p j n", j=2)
        gateA = view(WTR, 4096, f32, H)
        xn2 = view(SR, 0, f32, 2 * H).rearrange("p (j n) -> p j n", j=2)
        hmod2 = view(SR, 4096, f32, 2 * H).rearrange("p (k n) -> p k n", k=KT)
        ffn_nat = view(NAT, 0, f16, 2 * UNIT).rearrange("p (s n) -> p s n", s=2)
        F_gu = view(DQ, 0, f16, MT * 2 * H).rearrange("p (m g n) -> p m g n", m=MT, g=2)
        F_d = view(WD, 0, f16, MT * H).rearrange("p (m n) -> p m n", m=MT)
        orow = view(WTR, 0, f32, 2 * H).rearrange("p (s n) -> p s n", s=2)
        gateB = view(WTR, 4096, f32, 2 * H).rearrange("p (s n) -> p s n", s=2)

        bank = [ctx.enter_context(nc.psum_tensor(f"bank{i}", [P, 512], f32)) for i in range(8)]
        wo_bank = [bank[4], bank[5], bank[2], bank[1]]
        gate_bank, up_bank, prep_bank, out_bank = bank[0:2], bank[2:4], bank[4:6], bank[4:6]
        d_bank, ln_bank, fold_bank, row_bank = bank[0:2], bank[6:8], bank[0:4], bank[0:2]
        ffn_gu_bank = bank[2][:, :].bitcast(f16)
        ffn_d_bank = bank[3][:, 0:256].bitcast(f16)

        stack_clear, ident_ready, lora_b_in, lora_a_in, lora_a_mlp_in, scales_in, cond_in = map(
            sem, ["stack_clear", "ident_ready", "lora_b_in", "lora_a_in", "lora_a_mlp_in", "scales_in", "cond_in"])
        bst_hi, bst_ready, lora_T, lora_out, a_hi, a_ready, scales_ready, scales_mlp_in = map(
            sem, ["bst_hi", "bst_ready", "lora_T", "lora_out", "a_hi", "a_ready", "scales_ready", "scales_mlp_in"])
        silu_c, cs_T, cs_ready, mod_done, row_done, modT_ready, clamp_step, gates_out = map(
            sem, ["silu_c", "cs_T", "cs_ready", "mod_done", "row_done", "modT_ready",
                  "clamp_step", "gates_out"])
        wmod_in = [sem("wmod_in0"), sem("wmod_in1")]
        codes_in = [sem("codes_in0"), sem("codes_in1")]
        x_in = [sem(f"x_in{s}") for s in range(4)]
        sq_ready, lead_sq, lead_sum, lead_done, lin_done, sq_used, nat_hi, nat_lo = map(
            sem, ["sq_ready", "lead_sq", "lead_sum", "lead_done", "lin_done", "sq_used", "nat_hi", "nat_lo"])
        prep_done, prep_hi, prep_evac = map(sem, ["prep_done", "prep_hi", "prep_evac"])
        fold_done, m_hi, m_lo = map(sem, ["fold_done", "m_hi", "m_lo"])
        ln_centred = sem("ln_centred")
        ln_stat, ln_var, ln_rstd, ln_xn, ln_T, ln_mod, ln_hi, ln_lo = map(
            sem, ["ln_stat", "ln_var", "ln_rstd", "ln_xn", "ln_T", "ln_mod", "ln_hi", "ln_lo"])
        x1_done, x1_hi, x1_lo = map(sem, ["x1_done", "x1_hi", "x1_lo"])
        g_done, u_done, silu_done, hid_mul, hid_hi, hid_lo = map(
            sem, ["g_done", "u_done", "silu_done", "hid_mul", "hid_hi", "hid_lo"])
        d_done, z_evac, y_step, x2_done, xg_in = map(
            sem, ["d_done", "z_evac", "y_step", "x2_done", "xg_in"])
        ffn_in = [sem("ffn_in0"), sem("ffn_in1")]
        ffn_T, ffn_gu_out, ffn_d_out = map(sem, ["ffn_T", "ffn_gu_out", "ffn_d_out"])
        gateb_in, o_done, o_mul, out_ready = map(sem, ["gateb_in", "o_done", "o_mul", "out_ready"])
        out_dma = [sem("out_dma0"), sem("out_dma1")]

        def wait(eng, s, value):
            if isinstance(value, int) and value <= 0:
                return
            eng.wait_ge(s, value)

        Q0, J0 = 6, 8
        LED = (1, 3, 4, 5, 6, 7)

        def is_led(q):
            return isinstance(q, int) and q in LED

        def led_before(q):
            return sum(u < q for u in LED) if isinstance(q, int) else len(LED)

        def squares(q):
            return NF * q - led_before(q)

        def accumulator_free(eng, q):
            if isinstance(q, int) and q < 2:
                return
            if isinstance(q, int) and q < Q0 + 2:
                eng.wait_ge(prep_done, q + 1)
            else:
                eng.wait_ge(nat_lo, 3 * (q - Q0 - 1))

        CODES_IN = [16, 16, 32, 32, 48, 48, 80, 80]

        block = ctx.enter_context(nc.Block())

        @block.sync
        def _(sp):
            def load_x(b):
                if b >= 4:
                    sp.wait_ge(ln_T, b - 3)
                sp.dma_start(xin[:, b % 4], x_rows[b * SEQ:(b + 1) * SEQ].rearrange("(j p) n -> p j n", p=P))\
                    .then_inc(x_in[b % 4], 16)

            def slot_free(q):
                if not isinstance(q, int):
                    sp.wait_ge(sq_used, NF * (q - 1))
                elif q >= 2:
                    sp.wait_ge(sq_ready, squares(q - 1))
                    sp.wait_ge(sq_used, NF * (q - 2) + 1)

            def load_attn(q):
                slot_free(q)
                if q == 0:
                    src = codes_attn[3, 0:3 * P].rearrange("(t p) n -> p t n", p=P)
                elif q == 1:
                    src = codes_attn[3, 3 * P:4 * P].rearrange("(t p) n -> p t n", p=P)
                else:
                    src = codes_attn[0:3, (q - 2) * P:(q - 1) * P].rearrange("m p n -> p m n")
                n = 1 if q == 1 else 3
                sp.dma_start(codesZ[:, q % 2, 0:n * H].rearrange("p (t n) -> p t n", t=n), src)\
                    .then_inc(codes_in[q % 2], 16)

            def load_mlp(m, p, codes, first):
                if first:
                    sp.wait_ge(d_done, TT)
                else:
                    slot_free(Q0 + m)
                sp.dma_start(codes[:, p, 0:2 * H].rearrange("p (g n) -> p g n", g=2),
                             codes_gu[:, bass.ds(m * P, P)].rearrange("g p n -> p g n"))\
                    .then_inc(codes_in[p], 16)
                sp.dma_start(codes[:, p, 2 * H:3 * H].rearrange("p (t n) -> p t n", t=4),
                             codes_down[:, bass.ds(m * P, P)].rearrange("(t p) n -> p t n", p=P))\
                    .then_inc(codes_in[p], 16)

            def load_wmod(n, j):
                if n >= 2:
                    sp.wait_ge(mod_done, n - 1)
                sp.dma_start(wm[:, n % 2], wmod[:, j * H:(j + 1) * H].rearrange("(k p) n -> p k n", p=P))\
                    .then_inc(wmod_in[n % 2], 16)

            sp.dma_start(raw_sa, scales_attn.rearrange("m (t p) s -> p m t s", p=P)).then_inc(scales_in, 16)
            load_attn(0)
            sp.dma_start(crow[0:NB], cond).then_inc(cond_in, 16)
            sp.dma_start(rawB[:, 0:16].rearrange("p (m t) r -> p m t r", m=4),
                         lora_B_attn.rearrange("m (t p) r -> p m t r", p=P)).then_inc(lora_b_in, 16)
            for m in range(4):
                sp.dma_start(rawA[0:96, m * H:(m + 1) * H], lora_A_h[m].unsqueeze(0).broadcast_to([6, R, H]))\
                    .then_inc(lora_a_in, 16)
            load_wmod(0, 0)
            load_attn(1)
            sp.dma_start(rawB[:, 16:44].rearrange("p (g t) r -> p g t r", g=2),
                         lora_B_gu.rearrange("g (t p) r -> p g t r", p=P)).then_inc(lora_b_in, 16)
            sp.dma_start(rawB[:, 44:48], lora_B_down.rearrange("(t p) r -> p t r", p=P)).then_inc(lora_b_in, 16)
            for m in range(4, 6):
                sp.dma_start(rawA[0:96, m * H:(m + 1) * H], lora_A_h[m].unsqueeze(0).broadcast_to([6, R, H]))\
                    .then_inc(lora_a_mlp_in, 16)
            sp.dma_start(rawA[0:96, 6 * H:6 * H + I], lora_A_down.unsqueeze(0).broadcast_to([6, R, I]))\
                .then_inc(lora_a_mlp_in, 16)
            load_wmod(1, 1)
            load_wmod(2, 3)
            load_x(0)
            load_x(1)
            load_attn(2)
            load_attn(3)
            load_wmod(3, 4)
            sp.dma_start(raw_sg, scales_gu.rearrange("g (m p) s -> p g m s", p=P)).then_inc(scales_mlp_in, 16)
            sp.dma_start(raw_sd.rearrange("p t m s -> p t (m s)"),
                         scales_down.rearrange("(t p) s -> p t s", p=P)).then_inc(scales_mlp_in, 16)
            load_x(2)
            load_x(3)
            load_wmod(4, 2)
            load_wmod(5, 5)
            load_attn(4)
            load_attn(5)
            load_x(4)
            load_x(5)
            load_mlp(0, 0, codesZ, False)
            load_mlp(1, 1, codesZ, False)
            load_x(6)
            load_x(7)
            sp.wait_ge(clamp_step, 8)
            sp.dma_start(gates_dram[0], rows[0:NB, 0]).then_inc(gates_out, 16)
            sp.dma_start(gates_dram[1], rows[0:NB, 1]).then_inc(gates_out, 16)
            with sp.Fori(1, 4) as i:
                load_mlp(2 * i, 0, codesZ, False)
                load_mlp(2 * i + 1, 1, codesZ, False)
            load_mlp(8, 0, codesZ, False)
            load_mlp(9, 1, codesW, True)
            load_mlp(10, 0, codesW, True)
            load_mlp(11, 1, codesW, False)
            load_mlp(12, 0, codesW, False)
            load_mlp(13, 1, codesW, False)

            def load_residual(b):
                wait(sp, x2_done, 2 * b)
                sp.dma_start(xr[:, :, :], x_rows[bass.ds(b * SEQ, SEQ)].rearrange("(j p) n -> p j n", p=P))\
                    .then_inc(xg_in, 16)
                sp.dma_start(gateA[:, :], gates_dram[0, bass.ds(b, 1)].partition_broadcast(P)
                             .rearrange("p a n -> p (a n)")).then_inc(xg_in, 16)

            sp.wait_ge(gates_out, 32)
            sp.wait_ge(u_done, 4 * MT)
            load_residual(0)
            with sp.Fori(1, NB) as b:
                load_residual(b)

            def load_gate(tg):
                for s in range(2):
                    sp.dma_start(gateB[:, s], gates_dram[1, bass.ds(2 * tg + s, 1)].partition_broadcast(P)
                                 .rearrange("p a n -> p (a n)")).then_inc(gateb_in, 16)

            def store(tg):
                for j in range(4):
                    sp.wait_ge(out_ready, 4 * tg + j + 1)
                    sp.dma_start(out_rows[bass.ds(tg * GT + j * P, P)], orow[:, j % 2]).then_inc(out_dma[j % 2], 16)

            sp.wait_ge(x2_done, TT)
            load_gate(0)
            with sp.Fori(0, 3) as tg:
                store(tg)
                load_gate(tg + 1)
            store(3)
            sp.wait_ge(out_dma[0], 16 * TT // 2)
            sp.wait_ge(out_dma[1], 16 * TT // 2)

        @block.gpsimd
        def _(pool):
            pool.memset(minus_half, -0.5)
            pool.memset(offset0, OFFSET[0])
            pool.memset(identF, 0.0).then_inc(ident_ready, 1)
            pool.wait_ge(ident_ready, 1)
            pool.affine_select(out=identF, in_=identF, compare_op=ALU.not_equal, fill=1.0, base=0,
                               pattern=[[-1, P]], channel_multiplier=1).then_inc(ident_ready, 1)

            def low_a(dst, src):
                pool.tensor_tensor(dst, src, dst, ALU.subtract).then_inc(a_ready, 1)

            def ln_power(c, n):
                pool.wait_ge(ln_var, c + 1)
                pool.tensor_tensor(rstd[:, 0:n], varpe[:, 0:n], minus_half[:, 0:n], ALU.pow).then_inc(ln_rstd, 1)

            def ln_normalise():
                pool.wait_ge(ln_rstd, 1)
                xs = xin[:, 0:2].rearrange("p b j n -> p (b j) n")
                pool.tensor_tensor(xs, xs, moments[:, :, 0:1].broadcast_to([P, 4, H]), ALU.subtract)\
                    .then_inc(ln_centred, 1)
                pool.wait_ge(ln_centred, 1)
                pool.tensor_tensor(xs, xs, rstd.unsqueeze(2).broadcast_to([P, 4, H]), ALU.mult).then_inc(ln_xn, 2)

            def ln_low(L, b, dst, hmod):
                pool.wait_ge(ln_hi, L + 1)
                view4 = dst[:, bass.ds(2 * b, 2)].rearrange("p j a k n -> p a k j n")
                pool.tensor_tensor(view4[:, 1], hmod.rearrange("p k (j n) -> p k j n", j=2), view4[:, 0],
                                   ALU.subtract).then_inc(ln_lo, 1)

            def natural_low(q, p):
                pool.wait_ge(nat_hi, q - Q0 + 1)
                for c in range(3):
                    part = slice(c * H, (c + 1) * H)
                    pool.tensor_tensor(nat[:, 1, part], acc[:, p, part], nat[:, 0, part], ALU.subtract)\
                        .then_inc(nat_lo, 1)

            def lead(q, p, scale, n):
                pool.wait_ge(lead_sq, led_before(q) + 1)
                pool.tensor_tensor(acc[:, p, 0:n], acc[:, p, 0:n], offset0.broadcast_to([P, n]), ALU.add)\
                    .then_inc(lead_sum, 1)
                pool.wait_ge(lead_sum, led_before(q) + 1)
                blocks = acc[:, p, 0:n].rearrange("p (s c) -> p s c", c=BLOCK)
                pool.tensor_tensor(blocks, blocks, scale.unsqueeze(2).broadcast_to([P, n // BLOCK, BLOCK]),
                                   ALU.mult).then_inc(lead_done, 1)

            def hidden_low(n, s, dst):
                pool.wait_ge(hid_hi, n + 1)
                pool.tensor_tensor(dst[:, 1], hidden_row[:, s], dst[:, 0], ALU.subtract).then_inc(hid_lo, 1)

            def mlp_tile(m, p, slot, finish):
                for tg in range(TG):
                    hidden_low(4 * m + tg, tg % 2, hid[:, slot, :, tg * GT:(tg + 1) * GT])
                    if finish and tg == 0:
                        natural_low(Q0 + m + 1, 1 - p)

            low_rows = slice(32, 48)
            pool.wait_ge(a_hi, 1)
            low_a(A_at[low_rows], rawA[low_rows, 0:4 * H])
            pool.wait_ge(a_ready, 1)
            pool.wait_ge(scales_ready, 1)
            lead(1, 1, sc_o[:, 24:32], H)
            pool.wait_ge(a_hi, 3)
            pool.wait_ge(lead_done, 1)
            low_a(A_gu[low_rows], rawA[low_rows, 4 * H:6 * H])
            low_a(loraM[low_rows, :, 256:384], rawA[low_rows, 6 * H:].rearrange("p (m n) -> p m n", m=MT))
            pool.wait_ge(a_ready, 3)
            ln_power(0, 4)
            ln_normalise()
            lead(3, 1, sc_q[:, 1].rearrange("p m s -> p (m s)"), UNIT)
            lead(4, 0, sc_q[:, 2].rearrange("p m s -> p (m s)"), UNIT)
            ln_low(0, 0, hT, hmod1)
            lead(5, 1, sc_q[:, 3].rearrange("p m s -> p (m s)"), UNIT)
            ln_low(1, 1, hT, hmod1)
            pool.wait_ge(scales_ready, 2)
            lead(6, 0, sc_gu[:, 0], UNIT)
            ln_power(1, 4)
            lead(7, 1, sc_gu[:, 1], UNIT)
            ln_low(2, 2, hT, hmod1)
            ln_power(2, 4)
            ln_low(3, 3, hT, hmod1)
            ln_power(3, 4)
            ln_low(4, 4, hT, hmod1)
            ln_low(5, 5, hT, hmod1)
            ln_low(6, 6, hT, hmod1)
            ln_low(7, 7, hT, hmod1)
            natural_low(Q0, 0)
            with pool.Fori(0, 3) as i:
                mlp_tile(2 * i, 0, 2 * i, True)
                mlp_tile(2 * i + 1, 1, 2 * i + 1, True)
            mlp_tile(6, 0, 6, True)
            mlp_tile(7, 1, 0, True)
            with pool.Fori(4, 6) as i:
                mlp_tile(2 * i, 0, 2 * i - HALF, True)
                mlp_tile(2 * i + 1, 1, 2 * i + 1 - HALF, True)
            mlp_tile(12, 0, 5, True)
            mlp_tile(13, 1, 6, False)

            ln_power(4, 2)
            with pool.Fori(1, NB) as b:
                ln_power(4 + b, 2)
                ln_low(NB + b - 1, b - 1, h2T, hmod2)

            def group(tg):
                with pool.Fori(0, MT // 2) as i:
                    for s in range(2):
                        hidden_low(4 * MT + tg * MT + 2 * i + s, s, hid2[:, 2 * i + s])

            group(0)
            ln_low(2 * NB - 1, NB - 1, h2T, hmod2)
            with pool.Fori(1, TG) as tg:
                group(tg)

        @block.scalar
        def _(act):
            act.wait_ge(ident_ready, 2)
            act.activation(ident, identF, ACT.Copy).then_inc(ident_ready, 1)
            act.activation(identS, identF, ACT.Copy, scale=WS * HS).then_inc(ident_ready, 1)
            act.activation(identK, identF, ACT.Copy, scale=3.0 * WS / HS).then_inc(ident_ready, 1)
            act.wait_ge(cond_in, 16)
            act.activation(crow[0:NB], crow[0:NB], ACT.Silu).then_inc(silu_c, 1)

            def square(q, p, i, codes, n):
                if is_led(q) and i <= 3:
                    act.wait_ge(sq_used, NF * q + i - 3)
                elif i == 0:
                    wait(act, sq_used, NF * q)
                elif i >= 3:
                    act.wait_ge(sq_used, NF * q + i - 2)
                act.activation(sq[:, i % 3, 0:n], codes[:, p, 0:n], ACT.Square, bias=SHIFT[i], scale=0.25)\
                    .then_inc(sq_ready, 1)

            def lead_square(q, p, n):
                act.wait_ge(codes_in[p], CODES_IN[q])
                accumulator_free(act, q)
                act.activation(acc[:, p, 0:n], codesZ[:, p, 0:n], ACT.Square, bias=SHIFT[0], scale=0.25)\
                    .then_inc(lead_sq, 1)

            def natural_high(q, p):
                act.wait_ge(sq_used, NF * (q + 1))
                act.wait_ge(prep_done, J0 + 3 * (q - Q0))
                act.activation(nat[:, 0], acc[:, p], ACT.Copy).then_inc(nat_hi, 1)

            def stack(g, bk, n, dst):
                act.wait_ge(lora_T, g + 1)
                act.activation(dst, bk[0:96, 0:n * 64].bitcast(f16).rearrange("p (t n) -> p t n", t=n),
                               ACT.Copy).then_inc(lora_out, 1)

            def prep_high(j, bk, dst, src=None):
                act.wait_ge(prep_done, j + 1)
                act.activation(dst, bk[:, :] if src is None else src(bk), ACT.Copy).then_inc(prep_hi, 1)

            def ln_modulate(L, b, kind, dst, hmod):
                act.wait_ge(ln_T, L + 1)
                wait(act, ln_lo, L)
                for k in range(KT):
                    last = act.activation(hmod[:, k], ln_bank[k // 2][:, (k % 2) * SEQ:(k % 2 + 1) * SEQ],
                                          ACT.Identity,
                                          scale=modT[:, bass.ds(b, 1), kind + 4 + k],
                                          bias=modT[:, bass.ds(b, 1), kind + k])
                last.then_inc(ln_mod, 1)
                act.wait_ge(ln_mod, L + 1)
                view4 = dst[:, bass.ds(2 * b, 2)].rearrange("p j a k n -> p a k j n")
                act.activation(view4[:, 0], hmod.rearrange("p k (j n) -> p k j n", j=2), ACT.Copy).then_inc(ln_hi, 1)

            def silu(n, s):
                act.wait_ge(g_done, n + 1)
                wait(act, hid_lo, n - 1)
                return act.activation(hidden_row[:, s], gate_bank[s][:, :], ACT.Silu,
                                      scale=1.0 / WS)

            def hidden_high(n, s, dst):
                act.wait_ge(hid_mul, n + 1)
                act.activation(dst[:, 0], hidden_row[:, s], ACT.Copy).then_inc(hid_hi, 1)

            act.wait_ge(codes_in[0], 16)
            for i in range(NF):
                square(0, 0, i, codesZ, UNIT)
                if i == 3:
                    act.wait_ge(lora_b_in, 48)
                    act.wait_ge(stack_clear, 1)
                    act.activation(Bst[:, :, 0:R], rawB[:, :, :], ACT.Copy, scale=WS).then_inc(bst_hi, 1)
                if i == 2:
                    lead_square(1, 1, H)
                if i == 5:
                    act.activation(Bst[:, :, 32:32 + R], rawB[:, :, :], ACT.Copy, scale=WS).then_inc(bst_hi, 1)
            for i in range(1, NF):
                square(1, 1, i, codesZ, H)
                if i == 2:
                    stack(0, bank[0], 8, B_at[0:96, 0:1024].rearrange("p (t n) -> p t n", t=8))
                    stack(1, bank[1], 8, B_at[0:96, 1024:2048].rearrange("p (t n) -> p t n", t=8))
            act.wait_ge(codes_in[0], CODES_IN[2])
            square(2, 0, 0, codesZ, UNIT)
            for ot in range(4):
                p = ot % 2
                for i in range(1, NF):
                    square(2 + ot, p, i, codesZ, UNIT)
                    if ot == 0 and i < 4:
                        prep_high(i - 1, wo_bank[i - 1], WoT[:, 0, :, (i - 1) * P:i * P],
                                  lambda bk: bk[:, :].rearrange("p (o n) -> p o n", o=4))
                    if i == 4:
                        lead_square(3 + ot, 1 - p, UNIT)
                    if i == 5 and ot > 0:
                        prep_high(3 + ot, prep_bank[1 - p], qkvS[:, 1 - p, 0])
                    elif i == 6 and ot == 0:
                        prep_high(3, wo_bank[3], WoT[:, 0, :, 3 * P:4 * P],
                                  lambda bk: bk[:, :].rearrange("p (o n) -> p o n", o=4))
                if ot == 0:
                    stack(2, bank[6], 8, loraM[0:96, 0:8, 0:128])
                    stack(3, bank[7], 6, loraM[0:96, 8:14, 0:128])
                elif ot == 1:
                    act.wait_ge(modT_ready, 4)
                    ln_modulate(0, 0, 0, hT, hmod1)
                elif ot == 2:
                    ln_modulate(1, 1, 0, hT, hmod1)
                else:
                    stack(4, bank[6], 8, loraM[0:96, 0:8, 128:256])
                    stack(5, bank[7], 6, loraM[0:96, 8:14, 128:256])
            square(Q0, 0, 1, codesZ, UNIT)
            square(Q0, 0, 2, codesZ, UNIT)
            stack(6, bank[6], 4, B_dn[0:96].rearrange("p (t n) -> p t n", t=4))
            prep_high(7, prep_bank[1], qkvS[:, 1, 0])
            lead_square(Q0 + 1, 1, UNIT)
            for ht in range(KT):
                act.wait_ge(fold_done, ht + 1)
                act.activation(M1T[:, ht, 0], fold_bank[ht][:, :], ACT.Copy, scale=MS / (3.0 * WS * WS))\
                    .then_inc(m_hi, 1)

            def x1_high(tg, k):
                act.wait_ge(x1_done, 4 * tg + k + 1)
                act.activation(x1T[:, 4 * tg:4 * tg + 4, 0, k], bank[k % 2][:, :].rearrange("p (t n) -> p t n", t=4),
                               ACT.Copy, scale=1.0 / MS).then_inc(x1_hi, 1)

            Q1 = Q0 + 1
            ln_modulate(2, 2, 0, hT, hmod1)
            x1_high(0, 0)
            ln_modulate(3, 3, 0, hT, hmod1)
            x1_high(0, 1)
            square(Q0, 0, 3, codesZ, UNIT)
            x1_high(0, 2)
            x1_high(0, 3)
            ln_modulate(4, 4, 0, hT, hmod1)
            x1_high(1, 0)
            square(Q0, 0, 4, codesZ, UNIT)
            square(Q0, 0, 5, codesZ, UNIT)
            x1_high(1, 1)
            ln_modulate(5, 5, 0, hT, hmod1)
            x1_high(1, 2)
            square(Q0, 0, 6, codesZ, UNIT)
            x1_high(1, 3)
            ln_modulate(6, 6, 0, hT, hmod1)
            x1_high(2, 0)
            natural_high(Q0, 0)
            x1_high(2, 1)
            ln_modulate(7, 7, 0, hT, hmod1)
            x1_high(2, 2)
            square(Q1, 1, 1, codesZ, UNIT)
            x1_high(2, 3)
            square(Q1, 1, 2, codesZ, UNIT)
            x1_high(3, 0)
            square(Q1, 1, 3, codesZ, UNIT)
            x1_high(3, 1)
            prep_high(J0, prep_bank[0], WT[:, 0, 0, 0])
            x1_high(3, 2)
            prep_high(J0 + 1, prep_bank[1], WT[:, 0, 1, 0])
            square(Q1, 1, 4, codesZ, UNIT)
            x1_high(3, 3)
            prep_high(J0 + 2, prep_bank[0], WdT[:, 0, 0])
            square(Q1, 1, 5, codesZ, UNIT)
            square(Q1, 1, 6, codesZ, UNIT)

            def mlp_tile(m, p, slot, finish, start, codes):
                q, j = Q0 + m + 2, J0 + 3 * (m + 1)
                for tg in range(TG):
                    n, s = 4 * m + tg, tg % 2
                    silu(n, s).then_inc(silu_done, 1)
                    if start and tg > 0:
                        square(q, p, [None, 1, 2, 4][tg], codes, UNIT)
                    hidden_high(n, s, hid[:, slot, :, tg * GT:(tg + 1) * GT])
                    if tg == 0:
                        if finish:
                            natural_high(q - 1, 1 - p)
                        if start:
                            act.wait_ge(codes_in[p], 48 + 32 * (m // 2 + 2) if isinstance(m, int)
                                        else 48 + 16 * (m - p) + 64)
                            square(q, p, 0, codes, UNIT)
                    if tg == 1 and finish:
                        prep_high(j, prep_bank[1 - p], WT[:, 1 - p, 0, 0])
                    if tg == 2:
                        if finish:
                            prep_high(j + 1, prep_bank[p], WT[:, 1 - p, 1, 0])
                        if start:
                            square(q, p, 3, codes, UNIT)
                        if finish:
                            prep_high(j + 2, prep_bank[1 - p], WdT[:, m + 1, 0])
                    if tg == 3 and start:
                        square(q, p, 5, codes, UNIT)
                        square(q, p, 6, codes, UNIT)

            act.wait_ge(gates_out, 32)
            mlp_tile(0, 0, 0, True, True, codesZ)
            mlp_tile(1, 1, 1, True, True, codesZ)
            with act.Fori(1, 3) as i:
                mlp_tile(2 * i, 0, 2 * i, True, True, codesZ)
                mlp_tile(2 * i + 1, 1, 2 * i + 1, True, True, codesZ)
            mlp_tile(6, 0, 6, True, True, codesZ)
            act.wait_ge(sq_ready, squares(Q0 + 9))
            act.wait_ge(lin_done, Q0 + 9 - len(LED))
            with act.Fori(0, NB) as b:
                for j in range(2):
                    act.wait_ge(d_done, 2 * b + j + 1)
                    act.activation(z[:, 2 * b + j], d_bank[j][:, :], ACT.Copy, scale=1.0 / (WS * HS))\
                        .then_inc(z_evac, 1)
            mlp_tile(7, 1, 0, True, True, codesW)
            with act.Fori(4, 6) as i:
                mlp_tile(2 * i, 0, 2 * i - HALF, True, True, codesW)
                mlp_tile(2 * i + 1, 1, 2 * i + 1 - HALF, True, True, codesW)
            mlp_tile(12, 0, 5, True, False, codesW)
            mlp_tile(13, 1, 6, False, False, codesW)

            def load_ffn(e, s):
                row = bass.ds(e * P, P)
                act.dma_start(ffn_nat[:, s, 0:H], W_gate[row]).then_inc(ffn_in[s], 16)
                act.dma_start(ffn_nat[:, s, H:2 * H], W_up[row]).then_inc(ffn_in[s], 16)
                act.dma_start(ffn_nat[:, s, 2 * H:3 * H].rearrange("p (t n) -> p t n", t=4),
                              W_down[:, row].rearrange("(t p) n -> p t n", p=P)).then_inc(ffn_in[s], 16)

            def ffn_out(e, s, more):
                act.wait_ge(ffn_T, e + 1)
                act.activation(F_gu[:, e].rearrange("p g n -> p (g n)"), ffn_gu_bank, ACT.Copy).then_inc(ffn_gu_out, 1)
                if more:
                    load_ffn(e + 2, s)

            act.wait_ge(prep_done, J0 + 3 * MT)
            load_ffn(0, 0)
            load_ffn(1, 1)
            with act.Fori(1, NB - 1) as b:
                ffn_out(2 * b - 2, 0, True)
                ffn_out(2 * b - 1, 1, True)
                ln_modulate(NB + b - 1, b - 1, 8, h2T, hmod2)
            ffn_out(MT - 2, 0, False)
            ffn_out(MT - 1, 1, False)
            ln_modulate(2 * NB - 2, NB - 2, 8, h2T, hmod2)

            def group(tg):
                with act.Fori(0, MT // 2) as i:
                    for s in range(2):
                        n = 4 * MT + tg * MT + 2 * i + s
                        act.wait_ge(g_done, n + 1)
                        act.wait_ge(hid_lo, n - 1)
                        act.activation(hidden_row[:, s], gate_bank[s][:, :], ACT.Silu).then_inc(silu_done, 1)
                        hidden_high(n, s, hid2[:, 2 * i + s])

            group(0)
            ln_modulate(2 * NB - 1, NB - 1, 8, h2T, hmod2)
            with act.Fori(1, TG) as tg:
                group(tg)

        @block.vector
        def _(dve):
            dve.memset(Bst[:, :, :], 0.0).then_inc(stack_clear, 1)
            K = LEAD * WS
            dve.wait_ge(scales_in, 16)
            dve.tensor_scalar(sc_o.rearrange("p (t s) -> p t s", t=4), raw_sa[:, 3], K, None, ALU.mult)
            dve.tensor_scalar(sc_q.rearrange("p t m s -> p m t s"), raw_sa[:, 0:3], K, None, ALU.mult)\
                .then_inc(scales_ready, 1)

            def linear(q, p, codes, scale, n):
                accumulator_free(dve, q)
                dve.scalar_tensor_tensor(acc[:, p, 0:n].rearrange("p (s c) -> p s c", c=BLOCK),
                                         codes[:, p, 0:n].rearrange("p (s c) -> p s c", c=BLOCK), -7.0,
                                         scale.unsqueeze(2).broadcast_to([P, n // BLOCK, BLOCK]),
                                         ALU.add, ALU.mult).then_inc(lin_done, 1)
                dve.wait_ge(lin_done, q + 1 - led_before(q))

            def product(q, p, i, n):
                if i == 0 and is_led(q):
                    dve.wait_ge(lead_done, led_before(q) + 1)
                    dve.scalar_tensor_tensor(acc[:, p, 0:n], codesZ[:, p, 0:n], -7.0, acc[:, p, 0:n],
                                             ALU.add, ALU.mult).then_inc(sq_used, 1)
                    return
                dve.wait_ge(sq_ready, squares(q) + i + (0 if is_led(q) else 1))
                if i > 0:
                    dve.wait_ge(sq_used, NF * q + i)
                dve.scalar_tensor_tensor(acc[:, p, 0:n], sq[:, i % 3, 0:n], OFFSET[i], acc[:, p, 0:n],
                                         ALU.add, ALU.mult).then_inc(sq_used, 1)

            def prep_low(j, bk, dst, hi, src=None):
                dve.wait_ge(prep_hi, j + 1)
                dve.tensor_tensor(dst, bk[:, :] if src is None else src(bk), hi, ALU.subtract).then_inc(prep_evac, 1)

            def ln_statistics(c, tiles):
                n = len(tiles)
                for t in range(n):
                    last = dve.bn_stats(stats[:, t], tiles[t])
                last.then_inc(ln_stat, 1)
                dve.wait_ge(ln_stat, 2 * c + 1)
                for t in range(n):
                    last = dve.bn_aggr(moments[:, t], stats[:, t])
                last.then_inc(ln_stat, 1)
                dve.wait_ge(ln_stat, 2 * c + 2)
                dve.tensor_scalar(varpe[:, 0:n], moments[:, 0:n, 1], EPS, None, ALU.add).then_inc(ln_var, 1)

            def ln_normalise(c, L, tiles, dst):
                dve.wait_ge(ln_rstd, c + 1)
                for t in range(len(tiles)):
                    last = dve.tensor_scalar(dst[t], tiles[t], moments[:, t, 0:1], rstd[:, t:t + 1],
                                             ALU.subtract, ALU.mult)
                    if t % 2:
                        last.then_inc(ln_xn, 1)

            def x_tiles(c):
                return [xin[:, (2 * c + t // 2) % 4, t % 2] for t in range(4)]

            def ln_first(c):
                for b in (2 * c, 2 * c + 1):
                    dve.wait_ge(x_in[b % 4], 16 * (b // 4 + 1))
                ln_statistics(c, x_tiles(c))

            def mod_row(n):
                dve.wait_ge(mod_done, n + 1)
                dve.tensor_copy(rows[0:NB, n % 2], row_bank[n % 2][0:NB, :]).then_inc(row_done, 1)

            def clamp_gate(c):
                g = rows[0:NB, c]
                dve.tensor_scalar(clamp[0:NB, 0], g, 0.0, 2.0, ALU.is_ge, ALU.mult).then_inc(clamp_step, 1)
                dve.scalar_tensor_tensor(clamp[0:NB, 1], g, -1.0, g, ALU.mult, ALU.max).then_inc(clamp_step, 1)
                dve.wait_ge(clamp_step, 4 * c + 2)
                dve.tensor_scalar(clamp[0:NB, 1], clamp[0:NB, 1], 0.25, None, ALU.max).then_inc(clamp_step, 1)
                dve.wait_ge(clamp_step, 4 * c + 3)
                dve.scalar_tensor_tensor(g, clamp[0:NB, 0], -1.0, clamp[0:NB, 1], ALU.add, ALU.mult)\
                    .then_inc(clamp_step, 1)
                dve.wait_ge(clamp_step, 4 * c + 4)

            wo_view = lambda bk: bk[:, :].rearrange("p (o n) -> p o n", o=4)
            dve.wait_ge(scales_ready, 1)
            dve.wait_ge(codes_in[0], CODES_IN[0])
            linear(0, 0, codesZ, sc_o[:, 0:24], UNIT)
            product(0, 0, 0, UNIT)
            dve.wait_ge(cs_T, 1)
            dve.tensor_copy(csT.rearrange("p k b -> p (k b)"), bank[7][:, 0:4 * NB]).then_inc(cs_ready, 1)
            product(0, 0, 1, UNIT)
            dve.wait_ge(lora_a_in, 16 * 4)
            dve.tensor_copy(A_at[0:96], rawA[0:96, 0:4 * H]).then_inc(a_hi, 1)
            product(0, 0, 2, UNIT)
            product(0, 0, 3, UNIT)
            dve.wait_ge(lora_a_mlp_in, 16 * 3)
            dve.tensor_copy(A_gu[0:96], rawA[0:96, 4 * H:6 * H]).then_inc(a_hi, 1)
            dve.tensor_copy(loraM[0:96, :, 256:384], rawA[0:96, 6 * H:].rearrange("p (m n) -> p m n", m=MT))\
                .then_inc(a_hi, 1)
            product(0, 0, 4, UNIT)
            dve.wait_ge(bst_hi, 1)
            dve.scalar_tensor_tensor(Bst[:, :, 64:64 + R], rawB[:, :, :], WS, Bst[:, :, 0:R], ALU.mult, ALU.subtract)\
                .then_inc(bst_ready, 1)
            product(0, 0, 5, UNIT)
            product(0, 0, 6, UNIT)
            for i in range(NF):
                product(1, 1, i, H)
            ln_first(0)
            for ot in range(4):
                p = ot % 2
                if ot == 0:
                    dve.wait_ge(codes_in[0], CODES_IN[2])
                    linear(2, 0, codesZ, sc_q[:, 0].rearrange("p m s -> p (m s)"), UNIT)
                for i in range(NF):
                    product(2 + ot, p, i, UNIT)
                    if ot == 0 and i in (0, 1, 2):
                        prep_low(i, wo_bank[i], WoT[:, 1, :, i * P:(i + 1) * P],
                                 WoT[:, 0, :, i * P:(i + 1) * P], wo_view)
                    if ot == 1 and i == 2:
                        dve.wait_ge(mod_done, 4)
                        src = bank[3][:, 0:NB * 16].rearrange("p (g h c b) -> p h g c b", g=2, h=2, b=NB)
                        dst = modT.rearrange("p b (g h c) -> p h g c b", g=2, h=2)
                        for g in range(2):
                            dve.tensor_copy(dst[:, 0, g], src[:, 0, g]).then_inc(modT_ready, 1)
                            dve.tensor_scalar(dst[:, 1, g], src[:, 1, g], 1.0, None, ALU.add).then_inc(modT_ready, 1)
                    if ot == 1 and i in (4, 5):
                        mod_row(i)
                    if i == 6 and ot == 0:
                        prep_low(3, wo_bank[3], WoT[:, 1, :, 3 * P:4 * P], WoT[:, 0, :, 3 * P:4 * P], wo_view)
                    elif i == 5 and ot > 0:
                        prep_low(3 + ot, prep_bank[1 - p], qkvS[:, 1 - p, 1], qkvS[:, 1 - p, 0])
                if ot == 1:
                    dve.wait_ge(scales_mlp_in, 32)
                    dve.tensor_scalar(sc_gu[:, :, 0:16].rearrange("p m (g s) -> p g m s", g=2), raw_sg, K, None,
                                      ALU.mult)
                    dve.tensor_scalar(sc_gu[:, :, 16:24].rearrange("p m (t s) -> p t m s", t=4), raw_sd, K, None,
                                      ALU.mult).then_inc(scales_ready, 1)
            ln_first(1)
            product(Q0, 0, 0, UNIT)
            product(Q0, 0, 1, UNIT)
            prep_low(7, prep_bank[1], qkvS[:, 1, 1], qkvS[:, 1, 0])
            ln_normalise(1, 2, x_tiles(1), x_tiles(1))

            for ht in range(KT):
                dve.wait_ge(m_hi, ht + 1)
                dve.scalar_tensor_tensor(M1T[:, ht, 1], fold_bank[ht][:, :], MS / (3.0 * WS * WS), M1T[:, ht, 0],
                                         ALU.mult, ALU.subtract).then_inc(m_lo, 1)

            def x1_low(tg, k):
                dve.wait_ge(x1_hi, 4 * tg + k + 1)
                dve.scalar_tensor_tensor(x1T[:, 4 * tg:4 * tg + 4, 1, k],
                                         bank[k % 2][:, :].rearrange("p (t n) -> p t n", t=4), 1.0 / MS,
                                         x1T[:, 4 * tg:4 * tg + 4, 0, k], ALU.mult, ALU.subtract).then_inc(x1_lo, 1)

            Q1 = Q0 + 1
            product(Q0, 0, 2, UNIT)
            ln_first(2)
            x1_low(0, 0)
            ln_normalise(2, 4, x_tiles(2), x_tiles(2))
            x1_low(0, 1)
            product(Q0, 0, 3, UNIT)
            x1_low(0, 2)
            ln_first(3)
            x1_low(0, 3)
            x1_low(1, 0)
            ln_normalise(3, 6, x_tiles(3), x_tiles(3))
            product(Q0, 0, 4, UNIT)
            x1_low(1, 1)
            product(Q0, 0, 5, UNIT)
            x1_low(1, 2)
            product(Q0, 0, 6, UNIT)
            x1_low(1, 3)
            product(Q1, 1, 0, UNIT)
            x1_low(2, 0)
            dve.wait_ge(row_done, 2)
            clamp_gate(0)
            x1_low(2, 1)
            clamp_gate(1)
            x1_low(2, 2)
            product(Q1, 1, 1, UNIT)
            x1_low(2, 3)
            product(Q1, 1, 2, UNIT)
            x1_low(3, 0)
            product(Q1, 1, 3, UNIT)
            x1_low(3, 1)
            prep_low(J0, prep_bank[0], WT[:, 0, 0, 1], WT[:, 0, 0, 0])
            x1_low(3, 2)
            prep_low(J0 + 1, prep_bank[1], WT[:, 0, 1, 1], WT[:, 0, 1, 0])
            product(Q1, 1, 4, UNIT)
            x1_low(3, 3)
            prep_low(J0 + 2, prep_bank[0], WdT[:, 0, 1], WdT[:, 0, 0])
            product(Q1, 1, 5, UNIT)

            def hidden_mul(n, s, scale):
                dve.wait_ge(silu_done, n + 1)
                dve.wait_ge(u_done, n + 1)
                dve.scalar_tensor_tensor(hidden_row[:, s], up_bank[s][:, :], scale, hidden_row[:, s], ALU.mult, ALU.mult)\
                    .then_inc(hid_mul, 1)

            def mlp_tile(m, p, finish, start, codes):
                q, j = Q0 + m + 2, J0 + 3 * (m + 1)
                for tg in range(TG):
                    hidden_mul(4 * m + tg, tg % 2, HS / WS)
                    if tg == 0 and finish:
                        product(q - 1, 1 - p, 6, UNIT)
                    if tg == 1:
                        if start:
                            dve.wait_ge(codes_in[p], 48 + 32 * (m // 2 + 2) if isinstance(m, int)
                                        else 48 + 16 * (m - p) + 64)
                            linear(q, p, codes, sc_gu[:, m + 2], UNIT)
                            product(q, p, 0, UNIT)
                        if finish:
                            prep_low(j, prep_bank[1 - p], WT[:, 1 - p, 0, 1], WT[:, 1 - p, 0, 0])
                    if tg == 2:
                        if start:
                            product(q, p, 1, UNIT)
                        if finish:
                            prep_low(j + 1, prep_bank[p], WT[:, 1 - p, 1, 1], WT[:, 1 - p, 1, 0])
                        if start:
                            product(q, p, 2, UNIT)
                        if finish:
                            prep_low(j + 2, prep_bank[1 - p], WdT[:, m + 1, 1], WdT[:, m + 1, 0])
                    if tg == 3 and start:
                        for i in range(3, 6):
                            product(q, p, i, UNIT)

            with dve.Fori(0, 3) as i:
                mlp_tile(2 * i, 0, True, True, codesZ)
                mlp_tile(2 * i + 1, 1, True, True, codesZ)
            mlp_tile(6, 0, True, True, codesZ)
            mlp_tile(7, 1, True, True, codesW)
            with dve.Fori(4, 6) as i:
                mlp_tile(2 * i, 0, True, True, codesW)
                mlp_tile(2 * i + 1, 1, True, True, codesW)
            mlp_tile(12, 0, True, False, codesW)
            mlp_tile(13, 1, False, False, codesW)

            def ffn_out(e):
                dve.wait_ge(ffn_T, e + 1)
                dve.tensor_copy(F_d[:, e], ffn_d_bank).then_inc(ffn_d_out, 1)

            def residual(b):
                for j in range(2):
                    tt = 2 * b + j
                    dve.wait_ge(d_done, TT + tt + 1)
                    dve.scalar_tensor_tensor(z[:, tt], d_bank[j][:, :], 1.0 / (WS * HS), z[:, tt], ALU.mult, ALU.add)\
                        .then_inc(z_evac, 1)
                    if j == 0:
                        dve.wait_ge(xg_in, 32 * (b + 1))
                    dve.wait_ge(z_evac, TT + tt + 1)
                    dve.tensor_tensor(z[:, tt], z[:, tt], gateA[:, :], ALU.mult).then_inc(y_step, 1)
                    dve.wait_ge(y_step, tt + 1)
                    dve.tensor_tensor(z[:, tt], z[:, tt], xr[:, j], ALU.add).then_inc(x2_done, 1)
                    if j == 0 and b > 0:
                        ffn_out(2 * b - 1)
                dve.wait_ge(x2_done, 2 * b + 2)
                tiles = [z[:, 2 * b], z[:, 2 * b + 1]]
                ln_statistics(4 + b, tiles)
                if b < NB - 1:
                    ffn_out(2 * b)
                    dve.wait_ge(ln_T, NB + b)
                dst = xn2 if b < NB - 1 else xr
                ln_normalise(4 + b, NB + b, tiles, [dst[:, 0], dst[:, 1]])

            for b in range(NB):
                residual(b)

            def output(tg, j):
                w, s = 4 * tg + j, j % 2
                dve.wait_ge(o_done, w + 1)
                wait(dve, out_dma[s], 16 * (2 * tg + j // 2))
                dve.scalar_tensor_tensor(orow[:, s], out_bank[s][:, :], 1.0 / HS, gateB[:, j // 2], ALU.mult, ALU.mult)\
                    .then_inc(o_mul, 1)
                dve.wait_ge(o_mul, w + 1)
                dve.tensor_tensor(orow[:, s], orow[:, s], z[:, w], ALU.add).then_inc(out_ready, 1)

            def group(tg):
                with dve.Fori(0, MT // 2) as i:
                    for s in range(2):
                        hidden_mul(4 * MT + tg * MT + 2 * i + s, s, HS)
                if isinstance(tg, int):
                    dve.wait_ge(ln_T, 2 * NB)
                dve.wait_ge(gateb_in, 32 * (tg + 1))
                for j in range(4):
                    output(tg, j)

            group(0)
            with dve.Fori(1, TG) as tg:
                group(tg)

        @block.tensor
        def _(pe):
            pe.wait_ge(ident_ready, 5)
            pe.wait_ge(silu_c, 1)
            for k in range(KT):
                last = pe.transpose(bank[7][:, k * NB:(k + 1) * NB], crow[0:NB, k * P:(k + 1) * P], identF[0:NB, 0:NB])
            last.then_inc(cs_T, 1)

            def lora_transpose(g, bk, t0, n):
                for t in range(n):
                    last = pe.transpose(bk[0:96, t * 64:(t + 1) * 64].bitcast(f16), Bst[:, t0 + t], ident)
                last.then_inc(lora_T, 1)

            def mod_columns(n):
                pe.wait_ge(wmod_in[n % 2], 16 * (n // 2 + 1))
                for c in range(KT):
                    for k in range(KT):
                        at = (4 * n + c) * NB
                        last = pe.matmul(bank[3][:, at:at + NB], wm[:, n % 2, k, c * P:(c + 1) * P], csT[:, k],
                                         start=(k == 0), stop=(k == 3))
                last.then_inc(mod_done, 1)

            def mod_rows(n):
                pe.wait_ge(wmod_in[n % 2], 16 * (n // 2 + 1))
                for k in range(KT):
                    last = pe.matmul(row_bank[n % 2][0:NB, :], csT[:, k], wm[:, n % 2, k], start=(k == 0), stop=(k == 3))
                last.then_inc(mod_done, 1)

            def three_passes(dst, lhs, rhs, first, end):
                pe.matmul(dst, lhs[0], rhs[0], start=first, stop=False)
                pe.matmul(dst, lhs[0], rhs[1], start=False, stop=False)
                return pe.matmul(dst, lhs[1], rhs[0], start=False, stop=end)

            def prep(j, bk, blocks):
                wait(pe, prep_evac, j - 1)
                for c, (cols, rowf, colf) in enumerate(blocks):
                    dst = bk[:, c * P:(c + 1) * P]
                    pe.matmul(dst, nat[:, 0, cols], ident, start=True, stop=False)
                    pe.matmul(dst, nat[:, 1, cols], ident, start=False, stop=False)
                    last = pe.matmul(dst, rowf, colf, start=False, stop=True)
                last.then_inc(prep_done, 1)

            def prep_wo(q, t, ot):
                bk = wo_bank[ot]
                for o in range(4):
                    pe.matmul(bk[:, o * P:(o + 1) * P], A_at[0:96, 3 * H + o * P:3 * H + (o + 1) * P],
                              B_at[0:96, 3 * H + ot * P:3 * H + (ot + 1) * P], start=True, stop=False)
                    if o == 0:
                        pe.wait_ge(sq_used, NF * (q + 1))
                    last = pe.matmul(bk[:, o * P:(o + 1) * P], acc[:, q, t * H + o * P:t * H + (o + 1) * P], identF,
                                     start=False, stop=True)
                last.then_inc(prep_done, 1)

            def prep_qkv(ot):
                bk = prep_bank[ot % 2]
                pe.wait_ge(prep_evac, 3 + ot)
                for m in range(3):
                    pe.matmul(bk[:, :], B_at[0:96, m * H + ot * P:m * H + (ot + 1) * P],
                              A_at[0:96, m * H:(m + 1) * H], start=(m == 0), stop=False)
                pe.wait_ge(sq_used, NF * (3 + ot))
                for m in range(3):
                    last = pe.matmul(bk[:, :], identF, acc[:, ot % 2, m * H:(m + 1) * H], start=False, stop=(m == 2))
                last.then_inc(prep_done, 1)

            def fold(ot):
                pe.wait_ge(prep_evac, 5 + ot)
                for ht in range(KT):
                    cols = slice(ht * P, (ht + 1) * P)
                    if ot == 3:
                        pe.matmul(fold_bank[ht][:, cols], identS, identK, start=False, stop=False)
                    last = three_passes(fold_bank[ht][:, :], [qkvS[:, ot % 2, 0, cols], qkvS[:, ot % 2, 1, cols]],
                                        [WoT[:, 0, ot], WoT[:, 1, ot]], ot == 0, ot == 3)
                    if ot == 3:
                        last.then_inc(fold_done, 1)

            def ln_transpose(L, src):
                pe.wait_ge(ln_xn, L + 1)
                wait(pe, ln_mod, L)
                for k in range(KT):
                    for j in range(2):
                        at = (k % 2) * SEQ + j * P
                        last = pe.transpose(ln_bank[k // 2][:, at:at + P], src[:, j, k * P:(k + 1) * P], identF)
                last.then_inc(ln_T, 1)

            pe.wait_ge(cs_ready, 1)
            mod_columns(0)
            pe.wait_ge(bst_ready, 1)
            pe.wait_ge(bst_hi, 2)
            lora_transpose(0, bank[0], 0, 8)
            lora_transpose(1, bank[1], 8, 8)
            lora_transpose(2, bank[6], 16, 8)
            lora_transpose(3, bank[7], 24, 6)
            pe.wait_ge(lora_out, 2)
            pe.wait_ge(a_ready, 1)
            for t in range(3):
                prep_wo(0, t, t)
            mod_columns(1)
            prep_wo(1, 0, 3)
            mod_columns(2)
            mod_columns(3)
            for ot in range(4):
                if ot == 3:
                    pe.wait_ge(lora_out, 5)
                    lora_transpose(6, bank[6], 44, 4)
                prep_qkv(ot)
                if ot == 0:
                    pe.wait_ge(prep_evac, 4)
                    mod_rows(4)
                    mod_rows(5)
                    pe.wait_ge(lora_out, 4)
                    ln_transpose(0, xin[:, 0])
                    pe.wait_ge(modT_ready, 4)
                    pe.wait_ge(row_done, 2)
                elif ot == 1:
                    ln_transpose(1, xin[:, 1])
                elif ot == 2:
                    pe.wait_ge(ln_mod, 2)
                    lora_transpose(4, bank[6], 30, 8)
                    lora_transpose(5, bank[7], 38, 6)
                fold(ot)
            pe.wait_ge(lora_out, 7)
            ln_transpose(2, xin[:, 2])

            def prep_mlp(m, p, t):
                j = J0 + 3 * m + t
                pe.wait_ge(nat_lo, 3 * m + t + 1)
                lm = loraM[:, m]
                if t < 2:
                    blocks = [(slice(t * H + k * P, t * H + (k + 1) * P),
                               A_gu[0:96, t * H + k * P:t * H + (k + 1) * P], lm[0:96, t * P:(t + 1) * P])
                              for k in range(KT)]
                else:
                    blocks = [(slice(2 * H + o * P, 2 * H + (o + 1) * P), lm[0:96, 256:384],
                               B_dn[0:96, o * P:(o + 1) * P]) for o in range(4)]
                prep(j, prep_bank[(p + t) % 2], blocks)

            pe.wait_ge(m_lo, KT)
            for tg in range(TG):
                pe.wait_ge(ln_lo, 2 * tg + 2)
                for k in range(KT):
                    wait(pe, x1_lo, 4 * tg + k - 1)
                    for h in range(KT):
                        cols = slice(k * P, (k + 1) * P)
                        last = three_passes(bank[k % 2][:, :].rearrange("p (t n) -> p t n", t=4),
                                            [M1T[:, h, 0, cols], M1T[:, h, 1, cols]],
                                            [hT[:, 4 * tg:4 * tg + 4, 0, h], hT[:, 4 * tg:4 * tg + 4, 1, h]],
                                            h == 0, h == 3)
                    last.then_inc(x1_done, 1)
                    if tg == 3 and k < 3:
                        prep_mlp(0, 0, k)
                    b = {(0, 0): 3, (0, 2): 4, (1, 0): 5, (1, 2): 6, (2, 0): 7}.get((tg, k))
                    if b:
                        ln_transpose(b, xin[:, b % 4])

            def mlp_tile(m, p, prep_next, read=None, count=0):
                pe.wait_ge(prep_evac, J0 + 3 * m + 2)
                for tg in range(TG):
                    if read is not None and tg < 2:
                        pe.wait_ge(read, count - 1 + tg)
                    n, s = 4 * m + tg, tg % 2
                    for g, bk, done in ((0, gate_bank[s], g_done), (1, up_bank[s], u_done)):
                        if g == 0:
                            wait(pe, hid_mul, n - 1)
                        for k in range(KT):
                            cols = slice(k * P, (k + 1) * P)
                            last = three_passes(bk[:, :].rearrange("p (t n) -> p t n", t=4),
                                                [WT[:, p, g, 0, cols], WT[:, p, g, 1, cols]],
                                                [x1T[:, 4 * tg:4 * tg + 4, 0, k], x1T[:, 4 * tg:4 * tg + 4, 1, k]],
                                                k == 0, k == 3)
                        last.then_inc(done, 1)
                        if prep_next and (tg, g) in ((2, 0), (2, 1), (3, 0)):
                            prep_mlp(m + 1, 1 - p, tg - 2 + g if tg == 2 else 2)

            def down(b, j, half):
                tt = 2 * b + j
                wait(pe, z_evac, half * TT + tt - 1)
                toks = bass.ds(b * SEQ + j * P, P)
                for s in range(HALF):
                    if s == HALF - 1:
                        pe.wait_ge(hid_lo, 4 * HALF * (half + 1))
                        pe.wait_ge(prep_evac, J0 + 3 * HALF * (half + 1))
                    last = three_passes(d_bank[j][:, :], [hid[:, s, 0, toks], hid[:, s, 1, toks]],
                                        [WdT[:, half * HALF + s, 0], WdT[:, half * HALF + s, 1]],
                                        s == 0, s == HALF - 1)
                    if half == 0 and s == 0:
                        for k in range(KT):
                            for a in range(2):
                                pe.matmul(d_bank[j][:, k * P:(k + 1) * P], x1T[:, tt, a, k], identS,
                                          start=False, stop=False)
                last.then_inc(d_done, 1)

            mlp_tile(0, 0, True, x1_lo, TT)
            mlp_tile(1, 1, True)
            with pe.Fori(1, 3) as i:
                mlp_tile(2 * i, 0, True)
                mlp_tile(2 * i + 1, 1, True)
            mlp_tile(6, 0, True)
            pe.wait_ge(hid_lo, 4 * (HALF - 1))
            pe.wait_ge(hid_mul, 4 * HALF - 1)
            down(0, 0, 0)
            pe.wait_ge(hid_mul, 4 * HALF)
            down(0, 1, 0)
            with pe.Fori(1, NB) as b:
                down(b, 0, 0)
                down(b, 1, 0)
            mlp_tile(7, 1, True, z_evac, TT)
            with pe.Fori(4, 6) as i:
                mlp_tile(2 * i, 0, True)
                mlp_tile(2 * i + 1, 1, True)
            mlp_tile(12, 0, True)
            mlp_tile(13, 1, False)

            def ffn_prep(e, s):
                pe.wait_ge(ffn_in[s], 24 * (e - s) + 48)
                wait(pe, ffn_gu_out, e)
                wait(pe, ffn_d_out, e)
                for c in range(8):
                    pe.transpose(ffn_gu_bank[:, c * P:(c + 1) * P], ffn_nat[:, s, c * P:(c + 1) * P], ident)
                for c in range(4):
                    last = pe.transpose(ffn_d_bank[:, c * P:(c + 1) * P],
                                        ffn_nat[:, s, 2 * H + c * P:2 * H + (c + 1) * P], ident)
                last.then_inc(ffn_T, 1)

            pe.wait_ge(hid_lo, 4 * MT - 4)
            pe.wait_ge(hid_mul, 4 * MT - 1)
            down(0, 0, 1)
            pe.wait_ge(hid_mul, 4 * MT)
            down(0, 1, 1)

            def down_and_more(b):
                ffn_prep(2 * b - 2, 0)
                down(b, 0, 1)
                ffn_prep(2 * b - 1, 1)
                down(b, 1, 1)
                ln_transpose(NB + b - 1, xn2)

            down_and_more(1)
            with pe.Fori(2, NB) as b:
                down_and_more(b)
            pe.wait_ge(ffn_gu_out, MT)
            pe.wait_ge(ffn_d_out, MT)

            def group(tg):
                with pe.Fori(0, MT // 2) as i:
                    for s in range(2):
                        n = 4 * MT + tg * MT + 2 * i + s
                        if s == 0:
                            pe.wait_ge(ln_lo, NB + 2 * tg + 2)
                        if isinstance(tg, int):
                            pe.wait_ge(z_evac, 2 * TT - 1 + s)
                        pe.wait_ge(hid_mul, n - 1)
                        for g, bk, done in ((0, gate_bank[s], g_done), (1, up_bank[s], u_done)):
                            for k in range(KT):
                                for a in range(2):
                                    last = pe.matmul(bk[:, :].rearrange("p (t n) -> p t n", t=4),
                                                     F_gu[:, 2 * i + s, g, k * P:(k + 1) * P],
                                                     h2T[:, bass.ds(4 * tg, 4), a, k],
                                                     start=(k == 0 and a == 0), stop=(k == 3 and a == 1))
                            last.then_inc(done, 1)
                if isinstance(tg, int):
                    ln_transpose(2 * NB - 1, xr)
                for j in range(4):
                    w = 4 * tg + j
                    wait(pe, o_mul, w - 1)
                    for m in range(MT):
                        if j == 0 and m == 0:
                            pe.wait_ge(hid_lo, 4 * MT + MT * tg + MT - 2)
                        if j == 0 and m == MT - 2:
                            pe.wait_ge(hid_lo, 4 * MT + MT * tg + MT)
                        for a in range(2):
                            last = pe.matmul(out_bank[j % 2][:, :], hid2[:, m, a, j * P:(j + 1) * P], F_d[:, m],
                                             start=(m == 0 and a == 0), stop=(m == MT - 1 and a == 1))
                    last.then_inc(o_done, 1)

            group(0)
            with pe.Fori(1, TG) as tg:
                group(tg)


_INPUTS = ["L0_attn_x", "L0_attn_codes_attn", "L0_attn_scales_attn", "L0_attn_codes_gu", "L0_attn_scales_gu",
           "L0_attn_codes_down", "L0_attn_scales_down", "L0_attn_lora_A_h", "L0_attn_lora_A_down",
           "L0_attn_lora_B_attn", "L0_attn_lora_B_gu", "L0_attn_lora_B_down",
           "L0_ffn_W_gate", "L0_ffn_W_up", "L0_ffn_W_down", "L0_c", "L0_wmod"]


def kernel(**inputs):
    import numpy as _np
    import concourse.bacc as _bacc
    from concourse import mybir as _mybir
    from concourse.bass_utils import run_bass_kernel_spmd as _run

    nc = _bacc.Bacc("TRN2", target_bir_lowering=False, num_devices=1)
    arrays, args = {}, []
    for name in _INPUTS:
        a = _np.ascontiguousarray(inputs[name])
        arrays[f"in_{name}"] = a
        args.append(nc.dram_tensor(f"in_{name}", a.shape, _mybir.dt.from_np(a.dtype), kind="ExternalInput").ap())
    gates = nc.dram_tensor("gates", (2, NB, H), _mybir.dt.float32, kind="Internal").ap()
    res = nc.dram_tensor("out", (NB, SEQ, H), _mybir.dt.float32, kind="ExternalOutput").ap()
    adaln_kernel(nc, *args, gates, res)
    r = _run(nc, [arrays], core_ids=[0])
    return r.results[0]["out"]
```
